# Optimizing a Trainium2 kernel written in Bass

```python
import numpy as np
import jax
import jax.numpy as jnp

def _softmax(x, axis=-1):
    return jax.nn.softmax(x, axis=axis)
def _gelu(x):
    return jax.nn.gelu(x, approximate=True)
def _silu(x):
    return jax.nn.silu(x)
def _sigmoid(x):
    return jax.nn.sigmoid(x)
def _layernorm(x, axis=-1, eps=1e-5):
    m = jnp.mean(x, axis=axis, keepdims=True)
    v = jnp.var(x, axis=axis, keepdims=True)
    return (x - m) / jnp.sqrt(v + eps)
def _scatter_add(tgt, idx, src, axis=0):
    return tgt.at[idx].add(src)
def _segment_sum(src, seg, n):
    return jax.ops.segment_sum(src, seg, n)

kernel_name = 'mk_adj_ffn_d2_adj_256_c34b57'

def setup_inputs(seed: int = 0):
    np.random.seed(seed)
    _w = jnp.asarray
    def _rec_inputs():
        import jax
        import jax.numpy as jnp
        _gk = jax.random.key(seed)
        x = -0.0005207 + 1.001 * jax.random.normal(jax.random.fold_in(_gk, 1), (3327, 256), jnp.float32)
        _a = jax.random.bernoulli(jax.random.fold_in(_gk, 2), 0.00240457, (3327, 3327))
        _a = jnp.logical_or(_a, jnp.eye(3327, dtype=bool))
        _af = _a.astype(jnp.float32)
        _af = _af * jax.random.uniform(jax.random.fold_in(_gk, 3), (3327, 3327), jnp.float32, 0.05, 1)
        adj = _af
        return x, adj
    x, adj = _rec_inputs()
    def _L0_gnn_setup():
        import jax, jax.numpy as jnp
        import numpy as np
        N = 8192
        D_IN = 256
        D_OUT = 256
        key = jax.random.key(seed)
        k1, k2, k3 = jax.random.split(key, 3)
        x = jax.random.normal(k1, (N, D_IN), dtype=jnp.float32)
        adj = jax.random.uniform(k2, (N, N), dtype=jnp.float32)
        W = jax.random.normal(k3, (D_OUT, D_IN), dtype=jnp.float32) * (1.0 / np.sqrt(D_IN))
        return {'x': x, 'adj': adj, 'W': W}
    _L0_gnn_all = _L0_gnn_setup()
    _L0_gnn_in = {k: v for k, v in _L0_gnn_all.items() if k in ('W', )}
    del _L0_gnn_all

    def _L0_ffn_setup():
        import jax, jax.numpy as jnp
        import numpy as np
        B, S, D, H, E, K = (8, 8192, 256, 1024, 8, 2)
        key = jax.random.key(seed)
        ks = jax.random.split(key, 7)
        s_in = 1.0 / np.sqrt(D)
        s_hid = 1.0 / np.sqrt(H)
        return {'x': jax.random.normal(ks[0], (B, S, D), dtype=jnp.float32), 'Wg': jax.random.uniform(ks[1], (E, D), jnp.float32, -s_in, s_in), 'bg': jax.random.uniform(ks[2], (E,), jnp.float32, -s_in, s_in), 'W1': jax.random.uniform(ks[3], (E, H, D), jnp.float32, -s_in, s_in), 'b1': jax.random.uniform(ks[4], (E, H), jnp.float32, -s_in, s_in), 'W2': jax.random.uniform(ks[5], (E, D, H), jnp.float32, -s_hid, s_hid), 'b2': jax.random.uniform(ks[6], (E, D), jnp.float32, -s_hid, s_hid)}
    _L0_ffn_all = _L0_ffn_setup()
    _L0_ffn_in = {k: v for k, v in _L0_ffn_all.items() if k in ('Wg', 'bg', 'W1', 'b1', 'W2', 'b2', )}
    del _L0_ffn_all

    def _L1_gnn_setup():
        import jax, jax.numpy as jnp
        import numpy as np
        N = 8192
        IN = 256
        OUT = 256
        EDGE_P = 0.004
        key = jax.random.key(seed)
        k1, k2, k3, k4 = jax.random.split(key, 4)
        node_feats = jax.random.normal(k1, (N, IN), dtype=jnp.float32)
        a = (jax.random.uniform(k2, (N, N)) < EDGE_P).astype(jnp.float32)
        adj_matrix = jnp.maximum(a, a.T)
        W = jax.random.normal(k3, (OUT, IN), dtype=jnp.float32) / np.float32(np.sqrt(IN))
        b = jax.random.normal(k4, (OUT,), dtype=jnp.float32) * 0.01
        return {'node_feats': node_feats, 'adj_matrix': adj_matrix, 'W': W, 'b': b}
    _L1_gnn_all = _L1_gnn_setup()
    _L1_gnn_in = {k: v for k, v in _L1_gnn_all.items() if k in ('W', 'b', )}
    del _L1_gnn_all

    def _L1_ffn_setup():
        import jax, jax.numpy as jnp
        import numpy as np
        C = 256
        EPS = 1e-05
        N_ITERS = 30

        def _layernorm(x, w, bias):
            mu = jnp.mean(x, axis=-1, keepdims=True)
            var = jnp.mean(jnp.square(x - mu), axis=-1, keepdims=True)
            return (x - mu) * jax.lax.rsqrt(var + EPS) * w + bias
        key = jax.random.key(seed)
        kx, kw, kb, klw, klb = jax.random.split(key, 5)
        x = jax.random.normal(kx, (8, 2048, C), dtype=jnp.float32)
        bound = 1.0 / np.sqrt(C)
        W = jax.random.uniform(kw, (C, C), minval=-bound, maxval=bound, dtype=jnp.float32)
        b = jax.random.uniform(kb, (C,), minval=-bound, maxval=bound, dtype=jnp.float32)
        ln_w = jnp.ones((C,), dtype=jnp.float32)
        ln_b = jnp.zeros((C,), dtype=jnp.float32)
        return {'x': x, 'ln_w': ln_w, 'ln_b': ln_b, 'W': W, 'b': b}
    _L1_ffn_all = _L1_ffn_setup()
    _L1_ffn_in = {k: v for k, v in _L1_ffn_all.items() if k in ('ln_w', 'ln_b', 'W', 'b', )}
    del _L1_ffn_all

    return {
        "x": x,
        "adj": adj,
        "L0_gnn_W": _L0_gnn_in["W"],
        "L0_ffn_Wg": _L0_ffn_in["Wg"],
        "L0_ffn_bg": _L0_ffn_in["bg"],
        "L0_ffn_W1": _L0_ffn_in["W1"],
        "L0_ffn_b1": _L0_ffn_in["b1"],
        "L0_ffn_W2": _L0_ffn_in["W2"],
        "L0_ffn_b2": _L0_ffn_in["b2"],
        "L1_gnn_W": _L1_gnn_in["W"],
        "L1_gnn_b": _L1_gnn_in["b"],
        "L1_ffn_ln_w": _L1_ffn_in["ln_w"],
        "L1_ffn_ln_b": _L1_ffn_in["ln_b"],
        "L1_ffn_W": _L1_ffn_in["W"],
        "L1_ffn_b": _L1_ffn_in["b"],
    }

def reference(x, adj, L0_gnn_W, L0_ffn_Wg, L0_ffn_bg, L0_ffn_W1, L0_ffn_b1, L0_ffn_W2, L0_ffn_b2, L1_gnn_W, L1_gnn_b, L1_ffn_ln_w, L1_ffn_ln_b, L1_ffn_W, L1_ffn_b):
    import jax
    import jax.numpy as jnp
    def _L0_gnn_ref(x, adj, W):
        import jax, jax.numpy as jnp
        import numpy as np
        N = 8192
        D_IN = 256
        D_OUT = 256
        A_hat = adj + jnp.eye(adj.shape[0], dtype=adj.dtype)
        d_inv_sqrt = jnp.sum(A_hat, axis=1) ** (-0.5)
        A_norm = d_inv_sqrt[:, None] * A_hat * d_inv_sqrt[None, :]
        support = x @ W.T
        out = A_norm @ support
        return jax.nn.relu(out)

    def _L0_ffn_ref(x, Wg, bg, W1, b1, W2, b2):
        import jax, jax.numpy as jnp
        import numpy as np
        B, S, D, H, E, K = (8, 8192, 256, 1024, 8, 2)
        gate_scores = jnp.einsum('bsd,ed->bse', x, Wg) + bg
        topk_scores, topk_idx = jax.lax.top_k(gate_scores, K)
        topk_probs = jax.nn.softmax(topk_scores, axis=-1)
        combine = jnp.sum(topk_probs[..., None] * jax.nn.one_hot(topk_idx, E, dtype=x.dtype), axis=-2)
        out = jnp.zeros_like(x)
        for e in range(E):
            h = jax.nn.relu(jnp.einsum('bsd,hd->bsh', x, W1[e]) + b1[e])
            y = jnp.einsum('bsh,dh->bsd', h, W2[e]) + b2[e]
            out = out + combine[..., e:e + 1] * y
        return out

    def _L1_gnn_ref(node_feats, adj_matrix, W, b):
        import jax, jax.numpy as jnp
        import numpy as np
        N = 8192
        IN = 256
        OUT = 256
        EDGE_P = 0.004
        n = adj_matrix.shape[0]
        adj = adj_matrix + jnp.eye(n, dtype=adj_matrix.dtype)
        deg = jnp.sum(adj, axis=1)
        dinv = jnp.where(deg > 0, deg ** (-0.5), 0.0)
        adj_norm = dinv[:, None] * adj * dinv[None, :]
        x = node_feats @ W.T + b
        mean = jnp.mean(x, axis=0, keepdims=True)
        std = jnp.std(x, axis=0, ddof=1, keepdims=True)
        x = (x - mean) / (std + 1e-06)
        return adj_norm @ x

    def _L1_ffn_ref(x, ln_w, ln_b, W, b):
        import jax, jax.numpy as jnp
        import numpy as np
        C = 256
        EPS = 1e-05
        N_ITERS = 30

        def _layernorm(x, w, bias):
            mu = jnp.mean(x, axis=-1, keepdims=True)
            var = jnp.mean(jnp.square(x - mu), axis=-1, keepdims=True)
            return (x - mu) * jax.lax.rsqrt(var + EPS) * w + bias
        def step(h, _):
            h = h + 0.01 * jnp.tanh(h)
            h = h * jax.nn.sigmoid(h)
            h = _layernorm(h, ln_w, ln_b)
            h = jnp.einsum('bsc,dc->bsd', h, W) + b
            return (h, None)
        x, _ = jax.lax.scan(step, x, None, length=N_ITERS)
        return x

    x = x + _L0_gnn_ref(_layernorm(x, axis=-1), adj, L0_gnn_W)
    x = x + _L0_ffn_ref((_layernorm(x, axis=-1))[None], L0_ffn_Wg, L0_ffn_bg, L0_ffn_W1, L0_ffn_b1, L0_ffn_W2, L0_ffn_b2)[0]
    x = x + _L1_gnn_ref(_layernorm(x, axis=-1), adj, L1_gnn_W, L1_gnn_b)
    x = x + _L1_ffn_ref((_layernorm(x, axis=-1))[None], L1_ffn_ln_w, L1_ffn_ln_b, L1_ffn_W, L1_ffn_b)[0]
    return x


_drawn_inputs = setup_inputs


def setup_inputs(seed=0):
    import zlib

    import numpy as np

    out = dict(_drawn_inputs(seed))
    spreads = {'L1_ffn_ln_w': (1.0, 0.2), 'L1_ffn_ln_b': (0.0, 0.1)}
    factors = {'L0_ffn_b1': 3.174, 'L1_gnn_b': 8.0}
    for name, (base, spread) in spreads.items():
        noise = np.random.default_rng([zlib.crc32(name.encode()), seed]).standard_normal(out[name].shape)
        drawn = base * np.exp(spread * noise) if base else spread * noise
        out[name] = jnp.asarray(drawn.astype(out[name].dtype))
    for name, factor in factors.items():
        out[name] = (out[name] * factor).astype(out[name].dtype)
    return out
```

```python
from contextlib import ExitStack

import concourse.bass as bass
from concourse import mybir

F32 = mybir.dt.float32
F32R = mybir.dt.float32r
U32 = mybir.dt.uint32
I32 = mybir.dt.int32
ALU = mybir.AluOpType
ACT = mybir.ActivationFunctionType
AX = mybir.AxisListType

P = 128
N = 3327
NT = (N + P - 1) // P
NPAD = NT * P
LAST = N - (NT - 1) * P
D = 256
KD = D // P
E = 8
H = 1024
HB = H // P
LN_EPS = 1e-5
STEPS = 30

PANEL = 416
PANELS = NPAD // PANEL
CT = 2
CHUNKS = NT // CT
CW = CT * PANEL

TW = 256
REG = ((N + TW - 1) // TW + 1) * TW
TILES = (2 * N + E * (TW - 1)) // TW
SLOTS = E * REG + (TILES + 1) * TW
ROWS = NPAD + TW
KMAX = (N + TW - 1) // TW


class Shared:

    def __init__(self, sb):
        self.ident = sb("ident", [P, P])
        self.ones = sb("ones", [P, P])
        self.negones = sb("negones", [P, P])
        self.before = sb("before", [P, P])
        self.valid = sb("valid", [P, P])
        self.mhalf = sb("mhalf", [P, NT])
        self.dinv0 = sb("dinv0", [P, NT])
        self.dinv1 = sb("dinv1", [P, NT])
        self.x = sb("x", [P, NT, D])


class Chain:

    def __init__(self, eng, sem):
        self.eng, self.sem, self.n = eng, sem, 0

    def __call__(self, ins):
        self.n += 1
        ins.then_inc(self.sem, 1)
        self.eng.wait_ge(self.sem, self.n)


def wait_apart(eng, sem, value, passed):
    eng.wait_ge(sem, value)
    eng.sem_inc(passed, 1)


def tensors(nc, stack):
    def sb(name, shape, dt=F32):
        return stack.enter_context(nc.sbuf_tensor(name, shape, dt))

    def ps(name, shape, dt=F32):
        return stack.enter_context(nc.psum_tensor(name, shape, dt))

    return sb, ps


def semaphores(nc, stack, tag):
    held = []

    def clear():
        nc.clear_and_free_semaphores(held)
        nc.all_engine_barrier()

    stack.callback(clear)

    def sem(name):
        held.append(nc.alloc_semaphore(f"{tag}_{name}"))
        return held[-1]

    return sem


def constants_block(nc, g):
    with ExitStack() as ctx:
        sem = semaphores(nc, ctx, "const")
        filled = sem("filled")
        block = ctx.enter_context(nc.Block())

        @block.gpsimd
        def _(pool):
            pool.memset(g.ident[:], 0.0)
            pool.memset(g.ones[:], 1.0)
            pool.memset(g.negones[:], -1.0)
            pool.memset(g.mhalf[:], -0.5).then_inc(filled, 1)
            pool.wait_ge(filled, 1)
            pool.affine_select(out=g.ident[:], in_=g.ident[:], compare_op=ALU.not_equal, fill=1.0, base=0,
                               pattern=[[-1, P]], channel_multiplier=1)
            pool.affine_select(out=g.before[:], in_=g.ones[:], compare_op=ALU.is_gt, fill=0.0, base=0,
                               pattern=[[1, P]], channel_multiplier=-1)
            pool.affine_select(out=g.valid[:], in_=g.ones[:], compare_op=ALU.is_ge, fill=0.0, base=LAST - 1,
                               pattern=[[0, P]], channel_multiplier=-1).then_inc(filled, 1)
            pool.wait_ge(filled, 2)


def support_block(nc, g, x_in, w0, adjt, sp_, sh, sl):
    with ExitStack() as ctx:
        sb, ps = tensors(nc, ctx)
        sem = semaphores(nc, ctx, "sup")
        ring = sb("deg_ring", [P, CHUNKS, CW])
        part = sb("deg_part", [P, 3, PANEL])
        colsum = sb("deg_colsum", [P, NPAD])
        w = sb("sup_w", [P, KD, D])
        stats = sb("sup_stats", [P, NT, 6])
        mv = sb("sup_mv", [P, NT, 2])
        veps = sb("sup_veps", [P, NT])
        rstd = sb("sup_rstd", [P, NT])
        shift = sb("sup_shift", [P, NT])
        negshift = sb("sup_negshift", [P, NT])
        xn = sb("sup_xn", [P, 2, D])
        xnT = sb("sup_xnT", [P, 2, KD, P])
        deg = sb("sup_deg", [P, NT])
        degc = sb("sup_degc", [P, NT])
        has = sb("sup_has", [P, NT])
        root = sb("sup_root", [P, NT])
        psT = [ps(f"sup_psT{k}", [P, KD, P]) for k in range(2)]
        psS = [ps(f"sup_psS{k}", [P, D]) for k in range(2)]
        psD = ps("sup_psD", [P, NT])

        x_loaded, w_loaded = sem("x_loaded"), sem("w_loaded")
        chunk_loaded = [sem(f"chunk{c}") for c in range(CHUNKS)]
        chunks_used = sem("chunks_used")
        parts_done = sem("parts_done")
        colsum_done = sem("colsum_done")
        dchain = sem("dchain")
        stats_done, norm_done = sem("stats_done"), sem("norm_done")
        pchain = sem("pchain")
        xn_done, tr_done, xnT_done, mm_done, sup_done = (sem(n) for n in ("xn", "tr", "xnT", "mm", "sup"))
        deg_mm, deg_done, dinv_done, sp_done, sh_done = (sem(n) for n in ("degmm", "deg", "dinv", "sp", "sh"))
        GROUPS = [(0, 4), (4, 8), (8, CHUNKS)]
        group_of = [next(k for k, (a, b) in enumerate(GROUPS) if a <= c < b) for c in range(CHUNKS)]

        block = ctx.enter_context(nc.Block())

        @block.sync
        def _(sp):
            sp.dma_start(g.x[:], x_in.rearrange("(t p) d -> p t d", p=P)).then_inc(x_loaded, 16)
            sp.dma_start(w[:], w0.rearrange("(k p) n -> p k n", p=P)).then_inc(w_loaded, 16)
            with sp.Fori(0, PANELS) as p:
                for c in range(CHUNKS):
                    if c in (a for a, _ in GROUPS):
                        sp.wait_ge(chunks_used, p * 3 + group_of[c] + 1)
                    sp.dma_start(ring[:, c, :], adjt[bass.ds((p * CHUNKS + c) * P, P), :]).then_inc(chunk_loaded[c], 16)

        @block.vector
        def _(dve):
            chain = Chain(dve, dchain)
            dve.sem_inc(chunks_used, 3)
            dve.sem_inc(colsum_done, 1)
            dve.wait_ge(x_loaded, 16)
            for t in range(NT):
                dve.bn_stats(stats[:, t, :], g.x[:, t, :]).then_inc(dchain, 1)
            chain.n = NT
            dve.wait_ge(dchain, NT)
            for t in range(NT):
                last = dve.bn_aggr(mv[:, t, :], stats[:, t, :])
            chain(last)
            dve.tensor_scalar(veps[:], mv[:, :, 1], LN_EPS, None, ALU.add).then_inc(stats_done, 1)
            with dve.Fori(0, PANELS) as p:
                for k, (a, b) in enumerate(GROUPS):
                    if k == 0:
                        dve.wait_ge(colsum_done, p + 1)
                    for c in range(a, b):
                        dve.wait_ge(chunk_loaded[c], p * 16 + 16)
                    blocks = ring[:, a:b, :].rearrange("p c (q i) -> p i (c q)", i=PANEL)
                    dve.tensor_reduce(part[:, k, :], blocks, AX.X, ALU.add).then_inc(chunks_used, 1)
                dve.wait_ge(chunks_used, p * 3 + 6)
                dve.tensor_reduce(colsum[:, bass.ds(p * PANEL, PANEL)], part[:].rearrange("p k i -> p i k"),
                                  AX.X, ALU.add).then_inc(colsum_done, 1)
            dve.wait_ge(deg_mm, 1)
            chain(dve.tensor_scalar(deg[:], psD[:], 1.0, None, ALU.add))
            dve.tensor_scalar(has[:], deg[:], 0.0, None, ALU.is_gt)
            dve.tensor_scalar(degc[:], deg[:], 1e-30, None, ALU.max).then_inc(deg_done, 1)
            for t in range(NT):
                if t == 0:
                    dve.wait_ge(dinv_done, 1)
                    dve.wait_ge(sup_done, NT)
                dve.tensor_scalar(sp_[:, t, :], sp_[:, t, :], g.dinv0[:, t:t + 1], None, ALU.mult).then_inc(sp_done, 1)
                if t >= 1:
                    dve.wait_ge(sh_done, t)
                    dve.tensor_tensor(sl[:, t - 1, :], sp_[:, t - 1, :], sh[:, t - 1, :].bitcast(F32), ALU.subtract)
            dve.wait_ge(sh_done, NT)
            dve.tensor_tensor(sl[:, NT - 1, :], sp_[:, NT - 1, :], sh[:, NT - 1, :].bitcast(F32), ALU.subtract)
            dve.wait_ge(dinv_done, 2)
            dve.tensor_tensor(g.dinv1[:], root[:], has[:], ALU.mult)

        @block.gpsimd
        def _(pool):
            chain = Chain(pool, pchain)
            pool.wait_ge(stats_done, 1)
            chain(pool.tensor_tensor(rstd[:], veps[:], g.mhalf[:, 0:NT], ALU.pow))
            chain(pool.tensor_tensor(shift[:], mv[:, :, 0], rstd[:], ALU.mult))
            pool.tensor_scalar(negshift[:], shift[:], -1.0, 0.0, ALU.mult, ALU.add).then_inc(norm_done, 1)
            pool.wait_ge(deg_done, 1)
            pool.tensor_tensor(g.dinv0[:], deg[:], g.mhalf[:, 0:NT], ALU.pow).then_inc(dinv_done, 1)
            pool.tensor_tensor(root[:], degc[:], g.mhalf[:, 0:NT], ALU.pow).then_inc(dinv_done, 1)

        @block.scalar
        def _(act):
            act.wait_ge(norm_done, 1)
            for t in range(NT + 1):
                if t < NT:
                    if t >= 2:
                        act.wait_ge(tr_done, t - 1)
                    act.activation(xn[:, t % 2, :], g.x[:, t, :], ACT.Identity, bias=negshift[:, t:t + 1],
                                   scale=rstd[:, t:t + 1]).then_inc(xn_done, 1)
                    act.wait_ge(tr_done, t + 1)
                    if t >= 2:
                        act.wait_ge(mm_done, t - 1)
                    act.activation(xnT[:, t % 2], psT[t % 2][:], ACT.Copy).then_inc(xnT_done, 1)
                if t >= 1:
                    act.wait_ge(mm_done, t)
                    act.activation(sp_[:, t - 1, :], psS[(t - 1) % 2][:], ACT.Copy).then_inc(sup_done, 1)
            for t in range(NT):
                act.wait_ge(sp_done, t + 1)
                act.activation(sh[:, t, :], sp_[:, t, :], ACT.Copy).then_inc(sh_done, 1)

        @block.tensor
        def _(pe):
            pe.wait_ge(w_loaded, 16)
            for t in range(NT):
                pe.wait_ge(xn_done, t + 1)
                if t >= 2:
                    pe.wait_ge(xnT_done, t - 1)
                for k in range(KD):
                    last = pe.transpose(psT[t % 2][:, k, :], xn[:, t % 2, k * P:(k + 1) * P], g.ident[:])
                last.then_inc(tr_done, 1)
                pe.wait_ge(xnT_done, t + 1)
                if t >= 2:
                    pe.wait_ge(sup_done, t - 1)
                for k in range(KD):
                    last = pe.matmul(psS[t % 2][:], xnT[:, t % 2, k, :], w[:, k, :], start=(k == 0), stop=(k == KD - 1))
                last.then_inc(mm_done, 1)
            pe.wait_ge(colsum_done, PANELS + 1)
            for t in range(NT):
                last = pe.matmul(psD[:, t:t + 1], colsum[:, t * P:(t + 1) * P], g.ones[:, 0:1], start=True, stop=True)
            last.then_inc(deg_mm, 1)


def graph_block(nc, g, tag, adjt, sh, sl, outT):
    with ExitStack() as ctx:
        sb, ps = tensors(nc, ctx)
        sem = semaphores(nc, ctx, tag)
        raw = sb(f"{tag}_raw", [P, CHUNKS, CW])
        hi = sb(f"{tag}_hi", [P, 2, CW], F32R)
        lo = sb(f"{tag}_lo", [P, 2, CW], F32R)
        acc = [[ps(f"{tag}_acc{b}{d}", [P, PANEL]) for d in range(KD)] for b in range(2)]

        chunk_loaded = [sem(f"chunk{c}") for c in range(CHUNKS)]
        hi_done = sem("hi_done")
        lo_done = sem("lo_done")
        mm_done = sem("mm_done")
        evicted = sem("evicted")

        block = ctx.enter_context(nc.Block())

        @block.sync
        def _(sp):
            with sp.Fori(0, PANELS) as p:
                for c in range(CHUNKS):
                    sp.wait_ge(lo_done, p * CHUNKS + c + 1)
                    sp.dma_start(raw[:, c, :], adjt[bass.ds((p * CHUNKS + c) * P, P), :]).then_inc(chunk_loaded[c], 16)

        def evict(act, i, half):
            act.wait_ge(mm_done, i * (2 * CHUNKS) + (half + 1) * CHUNKS + 2)
            for d in range(KD):
                last = act.activation(outT[:, d, bass.ds((i * 2 + half) * PANEL, PANEL)], acc[half][d][:], ACT.Copy)
            last.then_inc(evicted, 1)

        @block.scalar
        def _(act):
            with act.Fori(0, PANELS // 2) as i:
                for n in range(2 * CHUNKS):
                    half, c = divmod(n, CHUNKS)
                    act.wait_ge(chunk_loaded[c], i * 32 + half * 16 + 16)
                    act.wait_ge(mm_done, i * (2 * CHUNKS) + n + 1)
                    act.activation(hi[:, n % 2, :], raw[:, c, :], ACT.Copy).then_inc(hi_done, 1)
                    if n == CHUNKS + 1:
                        evict(act, i, 0)
                evict(act, i, 1)

        @block.vector
        def _(dve):
            dve.sem_inc(lo_done, CHUNKS)
            with dve.Fori(0, PANELS // 2) as i:
                for n in range(2 * CHUNKS):
                    dve.wait_ge(hi_done, i * (2 * CHUNKS) + n + 1)
                    dve.tensor_tensor(lo[:, n % 2, :], raw[:, n % CHUNKS, :], hi[:, n % 2, :].bitcast(F32),
                                      ALU.subtract).then_inc(lo_done, 1)

        @block.tensor
        def _(pe):
            pe.sem_inc(mm_done, 2)
            pe.sem_inc(evicted, 2)
            with pe.Fori(0, PANELS // 2) as i:
                for n in range(2 * CHUNKS):
                    half, c = divmod(n, CHUNKS)
                    if c == 0:
                        pe.wait_ge(evicted, i * 2 + half + 1)
                    pe.wait_ge(lo_done, i * (2 * CHUNKS) + n + 1 + CHUNKS)
                    for q in range(CT):
                        j = c * CT + q
                        cols = slice(q * PANEL, (q + 1) * PANEL)
                        for d in range(KD):
                            fs = slice(d * P, (d + 1) * P)
                            pairs = [(sh, hi), (sh, lo), (sl, hi)]
                            for m, (s, a) in enumerate(pairs):
                                last = pe.matmul(acc[half][d][:], s[:, j, fs], a[:, n % 2, cols],
                                                 start=(j == 0 and m == 0), stop=(j == NT - 1 and m == 2))
                    last.then_inc(mm_done, 1)


def residual_block(nc, g, tag, sp_, outT, dinv, relu, hn):
    with ExitStack() as ctx:
        sb, ps = tensors(nc, ctx)
        sem = semaphores(nc, ctx, tag)
        tmp = sb(f"{tag}_tmp", [P, 2, D])
        act_out = sb(f"{tag}_act", [P, 2, D])
        stats = sb(f"{tag}_stats", [P, NT, 6])
        mv = sb(f"{tag}_mv", [P, NT, 2])
        veps = sb(f"{tag}_veps", [P, NT])
        rstd = sb(f"{tag}_rstd", [P, NT])
        psT = [ps(f"{tag}_psT{k}", [P, D]) for k in range(2)]
        tr_done, add_done, act_done, x_done, st_done, veps_done, rstd_done, hn_done = (
            sem(n) for n in ("tr", "add", "act", "x", "stats", "veps", "rstd", "hn"))
        block = ctx.enter_context(nc.Block())

        @block.tensor
        def _(pe):
            for t in range(NT):
                if t >= 2:
                    pe.wait_ge(add_done, t - 1)
                for d in range(KD):
                    last = pe.transpose(psT[t % 2][:, d * P:(d + 1) * P], outT[:, d, t * P:(t + 1) * P], g.ident[:])
                last.then_inc(tr_done, 1)

        @block.scalar
        def _(act):
            for t in range(NT):
                act.wait_ge(add_done, t + 1)
                if t >= 2:
                    act.wait_ge(x_done, t - 1)
                act.activation(act_out[:, t % 2, :], tmp[:, t % 2, :], ACT.Relu if relu else ACT.Copy,
                               scale=dinv[:, t:t + 1]).then_inc(act_done, 1)

        @block.vector
        def _(dve):
            for t in range(NT + 2):
                if t < NT:
                    dve.wait_ge(tr_done, t + 1)
                    if t >= 2:
                        dve.wait_ge(act_done, t - 1)
                    dve.tensor_tensor(tmp[:, t % 2, :], psT[t % 2][:], sp_[:, t, :], ALU.add).then_inc(add_done, 1)
                if 1 <= t <= NT:
                    u = t - 1
                    dve.wait_ge(act_done, u + 1)
                    dve.tensor_tensor(g.x[:, u, :], g.x[:, u, :], act_out[:, u % 2, :], ALU.add).then_inc(x_done, 1)
                if t >= 2:
                    u = t - 2
                    dve.wait_ge(x_done, u + 1)
                    dve.bn_stats(stats[:, u, :], g.x[:, u, :]).then_inc(st_done, 1)
            dve.wait_ge(st_done, NT)
            for t in range(NT):
                last = dve.bn_aggr(mv[:, t, :], stats[:, t, :])
            last.then_inc(st_done, 1)
            dve.wait_ge(st_done, NT + 1)
            dve.tensor_scalar(veps[:], mv[:, :, 1], LN_EPS, None, ALU.add).then_inc(veps_done, 1)
            dve.wait_ge(rstd_done, 1)
            for t in range(NT):
                dve.tensor_scalar(hn[:, t, :], g.x[:, t, :], mv[:, t, 0:1], rstd[:, t:t + 1], ALU.subtract,
                                  ALU.mult).then_inc(hn_done, 1)

        @block.gpsimd
        def _(pool):
            pool.wait_ge(veps_done, 1)
            pool.tensor_tensor(rstd[:], veps[:], g.mhalf[:, 0:NT], ALU.pow).then_inc(rstd_done, 1)


def routing_block(nc, g, wg, bg, hn, xn_rows, x_rows, table, sched):
    with ExitStack() as ctx:
        sb, ps = tensors(nc, ctx)
        sem = semaphores(nc, ctx, "route")
        wg_sb = sb("rt_wg", [P, KD, E])
        bg_sb = sb("rt_bg", [1, E])
        zero = sb("rt_zero", [P, TW // P, D])
        hT = sb("rt_hT", [P, 2, KD, P])
        sc = sb("rt_scores", [P, NT, E])
        rev_i = sb("rt_rev_i", [P, E], I32)
        rev = sb("rt_rev", [P, E])
        reg_i = sb("rt_reg_i", [P, E], I32)
        reg = sb("rt_reg", [P, E])
        k_i = sb("rt_k_i", [P, KMAX], I32)
        kf = sb("rt_k", [P, KMAX])
        t_i = sb("rt_t_i", [P, TILES + 1], I32)
        tf = sb("rt_t", [P, TILES + 1])
        keep = sb("rt_keep", [P, E, NT])
        best = [sb(f"rt_best{k}", [P, NT]) for k in range(2)]
        first = [sb(f"rt_first{k}", [P, NT]) for k in range(2)]
        hot = [sb(f"rt_hot{k}", [P, NT, E]) for k in range(2)]
        work = sb("rt_work", [P, NT, E])
        sc2 = sb("rt_scores2", [P, NT, E])
        mask = sb("rt_mask", [P, NT, E])
        diff = sb("rt_diff", [P, NT])
        ex = sb("rt_ex", [P, NT])
        ex1 = sb("rt_ex1", [P, NT])
        prob = [sb(f"rt_prob{k}", [P, NT]) for k in range(2)]
        tot = sb("rt_tot", [P, E, NT])
        incl = sb("rt_incl", [P, E, NT])
        base = sb("rt_base", [P, E, NT])
        base2 = sb("rt_base2", [P, E, NT])
        pos = sb("rt_pos", [P, NT, E])
        slot_f = [sb(f"rt_slotf{k}", [P, NT]) for k in range(2)]
        slot = [sb(f"rt_slot{k}", [P, NT], U32) for k in range(2)]
        meta = sb("rt_meta", [P, 2, NT, 2], U32)
        init = sb("rt_init", [P, SLOTS // P, 2], U32)
        initf = sb("rt_initf", [P, SLOTS // P])
        ntl = sb("rt_ntl", [P, E])
        cmp = sb("rt_cmp", [P, E, KMAX])
        cum = sb("rt_cum", [P, E])
        le = sb("rt_le", [P, TILES + 1, E])
        le2 = sb("rt_le2", [P, TILES + 1, E])
        eidx = sb("rt_eidx", [P, TILES + 1])
        first_t = sb("rt_first_t", [P, TILES + 1])
        rowf = sb("rt_rowf", [P, TILES + 1])
        rowf2 = sb("rt_rowf2", [P, TILES + 1])
        psT = [ps(f"rt_psT{k}", [P, KD, P]) for k in range(2)]
        psG = ps("rt_psG", [P, NT, E])
        psR = ps("rt_psR", [P, NT * E])
        psC = ps("rt_psC", [P, NT * E])

        loaded, iotas, init_done = sem("loaded"), sem("iotas"), sem("init")
        zero_done, tr_done, hT_done, gate_done = sem("zero"), sem("tr"), sem("hT"), sem("gate")
        dchain, exp_in, exp_out, mask_done, rank_done = (sem(n) for n in ("dchain", "exp_in", "exp_out", "mask", "rank"))
        slots_done, sched_done, stored, scattered = (sem(n) for n in ("slots", "sched", "stored", "scattered"))

        block = ctx.enter_context(nc.Block())

        @block.sync
        def _(sp):
            sp.dma_start(wg_sb[:], wg.rearrange("(k p) e -> p k e", p=P)).then_inc(loaded, 16)
            sp.dma_start(bg_sb[:], bg).then_inc(loaded, 16)
            sp.dma_start(xn_rows[0:NPAD, :].rearrange("(t p) d -> p t d", p=P), hn[:]).then_inc(stored, 16)
            sp.dma_start(x_rows[0:NPAD, :].rearrange("(t p) d -> p t d", p=P), g.x[:]).then_inc(stored, 16)
            sp.wait_ge(zero_done, 1)
            sp.dma_start(xn_rows[NPAD:ROWS, :].rearrange("(t p) d -> p t d", p=P), zero[:]).then_inc(stored, 16)
            sp.wait_ge(init_done, 1)
            sp.dma_start(table.rearrange("(p m) c -> p m c", p=P), init[:]).then_inc(stored, 16)
            sp.wait_ge(stored, 64)

        @block.gpsimd
        def _(pool):
            pool.memset(zero[:], 0.0).then_inc(zero_done, 1)
            pool.iota(rev_i[:], [[-1, E]], base=E, channel_multiplier=0)
            pool.iota(reg_i[:], [[REG, E]], base=0, channel_multiplier=0)
            pool.iota(k_i[:], [[TW, KMAX]], base=0, channel_multiplier=0)
            pool.iota(t_i[:], [[1, TILES + 1]], base=0, channel_multiplier=0)
            pool.iota(meta[:, :, :, 0], [[0, 2], [P, NT]], base=0, channel_multiplier=1)
            pool.memset(keep[:], 1.0)
            pool.iota(init[:, :, 0], [[1, SLOTS // P]], base=0, channel_multiplier=SLOTS // P)
            pool.memset(init[:, :, 1], 0).then_inc(iotas, 1)
            pool.wait_ge(iotas, 1)
            pool.memset(keep[:, :, 0:1], 0.0).then_inc(iotas, 1)
            pool.wait_ge(slots_done, 1)
            pool.wait_ge(stored, 64)
            for t in range(NT):
                rows = P if t < NT - 1 else LAST
                for k in range(2):
                    pool.indirect_dma_start(table, bass.IndirectOffsetOnAxis(ap=slot[k][0:rows, t:t + 1], axis=0),
                                            meta[0:rows, k, t, :], None).then_inc(scattered, 16)
            pool.wait_ge(scattered, 16 * 2 * NT)

        @block.scalar
        def _(act):
            for t in range(NT):
                act.wait_ge(tr_done, t + 1)
                if t >= 2:
                    act.wait_ge(gate_done, t - 1)
                act.activation(hT[:, t % 2], psT[t % 2][:], ACT.Copy).then_inc(hT_done, 1)
            act.wait_ge(exp_in, 1)
            act.activation(ex[:], diff[:], ACT.Exp).then_inc(exp_out, 1)

        @block.tensor
        def _(pe):
            pe.wait_ge(loaded, 32)
            for t in range(NT + 1):
                if t < NT:
                    if t >= 2:
                        pe.wait_ge(hT_done, t - 1)
                    for k in range(KD):
                        last = pe.transpose(psT[t % 2][:, k, :], hn[:, t, k * P:(k + 1) * P], g.ident[:])
                    last.then_inc(tr_done, 1)
                if t >= 1:
                    u = t - 1
                    pe.wait_ge(hT_done, u + 1)
                    for k in range(KD):
                        pe.matmul(psG[:, u, :], hT[:, u % 2, k, :], wg_sb[:, k, :], start=(k == 0), stop=False)
                    pe.matmul(psG[:, u, :], g.ones[0:1, :], bg_sb[0:1, :], start=False, stop=True).then_inc(gate_done, 1)
            pe.wait_ge(mask_done, 1)
            flat = mask[:].rearrange("p t e -> p (t e)")
            pe.matmul(psR[:], g.before[:], flat, start=True, stop=True)
            pe.matmul(psC[:], g.ones[:], flat, start=True, stop=True).then_inc(rank_done, 1)

        @block.vector
        def _(dve):
            chain = Chain(dve, dchain)
            dve.wait_ge(iotas, 2)
            chain(dve.tensor_scalar(init[:, :, 0], init[:, :, 0], TW - 1, None, ALU.bitwise_and))
            chain(dve.tensor_scalar(initf[:], init[:, :, 0], float(NPAD), None, ALU.add))
            dve.tensor_copy(init[:, :, 0], initf[:]).then_inc(init_done, 1)
            dve.tensor_copy(rev[:], rev_i[:])
            dve.tensor_copy(reg[:], reg_i[:])
            dve.tensor_copy(kf[:], k_i[:])
            dve.tensor_copy(tf[:], t_i[:])
            dve.wait_ge(gate_done, NT)
            chain(dve.tensor_copy(sc[:], psG[:]))
            bc = [P, NT, E]
            scores = [sc, sc2]
            revb = rev[:].unsqueeze(1).broadcast_to(bc)
            for k in range(2):
                s = scores[k]
                chain(dve.tensor_reduce(best[k][:], s[:], AX.X, ALU.max))
                chain(dve.tensor_tensor(work[:], s[:], best[k][:].unsqueeze(2).broadcast_to(bc), ALU.is_equal))
                chain(dve.tensor_tensor(work[:], work[:], revb, ALU.mult))
                chain(dve.tensor_reduce(first[k][:], work[:], AX.X, ALU.max))
                chain(dve.tensor_tensor(hot[k][:], revb, first[k][:].unsqueeze(2).broadcast_to(bc), ALU.is_equal))
                if k == 0:
                    chain(dve.scalar_tensor_tensor(out=sc2[:], in0=hot[0][:], scalar=-3.0e38, in1=sc[:],
                                                   op0=ALU.mult, op1=ALU.add))
            dve.tensor_tensor(diff[:], best[1][:], best[0][:], ALU.subtract).then_inc(exp_in, 1)
            chain(dve.tensor_tensor(mask[:], hot[0][:], hot[1][:], ALU.add))
            dve.tensor_scalar(mask[:, NT - 1, :], mask[:, NT - 1, :], g.valid[:, 0:1], None, ALU.mult).then_inc(mask_done, 1)
            dve.wait_ge(exp_out, 1)
            chain(dve.tensor_scalar(ex1[:], ex[:], 1.0, None, ALU.add))
            chain(dve.reciprocal(prob[0][:], ex1[:]))
            chain(dve.tensor_tensor(prob[1][:], ex[:], prob[0][:], ALU.mult))
            for k in range(2):
                dve.tensor_copy(meta[:, k, :, 1].bitcast(F32), prob[k][:])
            dve.wait_ge(rank_done, 1)
            chain(dve.tensor_copy(tot[:], psC[:].rearrange("p (t e) -> p e t", e=E)))
            chain(dve.tensor_tensor_scan(incl[:].rearrange("p e t -> p (e t)"), keep[:].rearrange("p e t -> p (e t)"),
                                         tot[:].rearrange("p e t -> p (e t)"), 0.0, ALU.mult, ALU.add))
            chain(dve.tensor_tensor(base[:], incl[:], tot[:], ALU.subtract))
            chain(dve.tensor_tensor(base2[:], base[:], reg[:].unsqueeze(2).broadcast_to([P, E, NT]), ALU.add))
            chain(dve.tensor_tensor(pos[:], psR[:].rearrange("p (t e) -> p t e", e=E),
                                    base2[:].rearrange("p e t -> p t e"), ALU.add))
            for k in range(2):
                chain(dve.tensor_tensor(work[:], hot[k][:], pos[:], ALU.mult))
                chain(dve.tensor_reduce(slot_f[k][:], work[:], AX.X, ALU.add))
                last = dve.tensor_copy(slot[k][:], slot_f[k][:])
            last.then_inc(slots_done, 1)
            counts = incl[:, :, NT - 1:NT].broadcast_to([P, E, KMAX])
            chain(dve.tensor_tensor(cmp[:], counts, kf[:].unsqueeze(1).broadcast_to([P, E, KMAX]), ALU.is_gt))
            chain(dve.tensor_reduce(ntl[:], cmp[:], AX.X, ALU.add))
            chain(dve.tensor_tensor_scan(cum[:], g.ones[:, 0:E], ntl[:], 0.0, ALU.mult, ALU.add))
            tb = [P, TILES + 1, E]
            chain(dve.tensor_tensor(le[:], cum[:].unsqueeze(1).broadcast_to(tb),
                                    tf[:].unsqueeze(2).broadcast_to(tb), ALU.is_le))
            chain(dve.tensor_reduce(eidx[:], le[:], AX.X, ALU.add))
            chain(dve.tensor_tensor(le2[:], le[:], ntl[:].unsqueeze(1).broadcast_to(tb), ALU.mult))
            chain(dve.tensor_reduce(first_t[:], le2[:], AX.X, ALU.add))
            chain(dve.tensor_tensor(rowf[:], tf[:], first_t[:], ALU.subtract))
            chain(dve.tensor_scalar(rowf2[:], rowf[:], float(TW), None, ALU.mult))
            chain(dve.scalar_tensor_tensor(out=rowf[:], in0=eidx[:], scalar=float(REG), in1=rowf2[:],
                                           op0=ALU.mult, op1=ALU.add))
            dve.tensor_copy(sched[:, 0, :], rowf[0:1, :])
            chain(dve.tensor_scalar(first_t[:], eidx[:], float(E - 1), None, ALU.min))
            dve.tensor_copy(sched[:, 1, :], first_t[0:1, :])


def experts_block(nc, g, wall, b1, b2, xn_rows, x_rows, table, sched):
    with ExitStack() as ctx:
        sb, ps = tensors(nc, ctx)
        sem = semaphores(nc, ctx, "moe")
        HALF = TW // P
        W1 = KD * H
        WA = 2 * W1
        CHW = 512
        NCH = WA // CHW
        POOL_CH = (3, 7)
        wraw = sb("moe_wraw", [P, 2, WA])
        wh = sb("moe_wh", [P, 2, WA], F32R)
        wl = sb("moe_wl", [P, 2, WA], F32R)
        b1s = sb("moe_b1", [P, 2, HB])
        b2s = sb("moe_b2", [P, 2, D])
        meta = sb("moe_meta", [P, 2, HALF, 2], U32)
        meta2 = sb("moe_meta2", [P, 2, HALF, 2], U32)
        xg = sb("moe_xg", [P, 2, HALF, D])
        xh = sb("moe_xh", [P, KD, TW], F32R)
        xl = sb("moe_xl", [P, KD, TW], F32R)
        hr = sb("moe_hr", [P, HB, TW])
        hh = sb("moe_hh", [P, HB, TW], F32R)
        hl = sb("moe_hl", [P, HB, TW], F32R)
        zero = sb("moe_zero", [(ROWS - NPAD) // 4, D])
        yb = sb("moe_yb", [P, 2, HALF, D])
        y = sb("moe_y", [P, 2, HALF, D])
        psX = ps("moe_psX", [P, KD, TW])
        psH = [ps(f"moe_psH{k}", [P, 2, TW]) for k in range(HB // 2)]
        psY = [ps(f"moe_psY{k}", [P, HALF, D]) for k in range(2)]

        w_loaded = [sem(f"w_loaded{k}") for k in range(2)]
        small_loaded = [sem(f"small_loaded{k}") for k in range(2)]
        meta_loaded = [sem(f"meta_loaded{k}") for k in range(2)]
        gathered = [sem(f"gathered{k}") for k in range(2)]
        wh_done = sem("wh_done")
        wl_done = sem("wl_done")
        wlp_done = sem("wlp_done")
        turned = sem("turned")
        xh_done, xl_done = sem("xh_done"), sem("xl_done")
        l1_done = sem("l1_done")
        relu_done = sem("relu_done")
        hh_done = sem("hh_done")
        hl_done = sem("hl_done")
        l2_done = sem("l2_done")
        yb_done = sem("yb_done")
        y_done = sem("y_done")
        copied = sem("copied")
        added = [sem(f"added{k}") for k in range(2)]
        zeroed = sem("zeroed")
        issued = sem("issued")
        passed = sem("passed")
        pairs = HB // 2
        DCH = NCH - len(POOL_CH)

        block = ctx.enter_context(nc.Block())

        def load_weights(sp, t, b):
            e = sp.value_load(sched[0:1, 1, bass.ds(t, 1)] if not isinstance(t, int) else sched[0:1, 1, t:t + 1],
                              min_val=0, max_val=E - 1)
            for k in range(2):
                sp.dma_start(wraw[:, b, k * W1:(k + 1) * W1],
                             wall[bass.ds(e * P, P), k * W1:(k + 1) * W1]).then_inc(w_loaded[b], 16)

        def load_small(sp, t, b):
            e = sp.value_load(sched[0:1, 1, bass.ds(t, 1)] if not isinstance(t, int) else sched[0:1, 1, t:t + 1],
                              min_val=0, max_val=E - 1)
            sp.dma_start(b1s[:, b, :], b1[bass.ds(e * P, P), :]).then_inc(small_loaded[b], 16)
            sp.dma_start(b2s[:, b, :], b2[bass.ds(e, 1), :].broadcast_to([P, D])).then_inc(small_loaded[b], 16)

        def load_meta(sp, t, b):
            r = sp.value_load(sched[0:1, 0, bass.ds(t, 1)] if not isinstance(t, int) else sched[0:1, 0, t:t + 1],
                              min_val=0, max_val=SLOTS - TW)
            sp.dma_start(meta[:, b, :, :], table[bass.ds(r, TW), :].rearrange("(p h) c -> p h c", h=HALF)
                         ).then_inc(meta_loaded[b], 16)

        @block.sync
        def _(sp):
            for t in range(2):
                load_weights(sp, t, t)
                load_meta(sp, t, t)
                load_small(sp, t, t)

            def ahead(t, b, weights=True, small=True, metas=True):
                o = 1 - b
                if weights:
                    sp.wait_ge(wl_done, t * DCH + 2 * DCH)
                    wait_apart(sp, wlp_done, t * len(POOL_CH) + 2 * len(POOL_CH), passed)
                    load_weights(sp, t + 3, o)
                if metas:
                    sp.wait_ge(issued, t + 2)
                    wait_apart(sp, copied, t + 2, passed)
                    load_meta(sp, t + 3, o)
                if small:
                    sp.wait_ge(relu_done, t * HB + 2 * HB)
                    wait_apart(sp, yb_done, t + 3, passed)
                    load_small(sp, t + 2, b)

            ahead(-1, 1, small=False)
            with sp.Fori(0, (TILES - 3) // 2) as i:
                for b in range(2):
                    ahead(i * 2 + b, b)
            t = TILES - 3
            ahead(t, t % 2, weights=False)

        @block.gpsimd
        def _(pool):
            quarter = (ROWS - NPAD) // 4
            pool.memset(zero[:], 0.0).then_inc(zeroed, 1)
            pool.wait_ge(zeroed, 1)
            for k in range(4):
                pool.dma_start(x_rows[NPAD + k * quarter:NPAD + (k + 1) * quarter, :], zero[:]).then_inc(added[k % 2], 16)

            def gather(t, b, use):
                wait_apart(pool, meta_loaded[b], use * 16 + 16, passed)
                for h in range(HALF):
                    pool.indirect_dma_start(xg[:, b, h, :], None, xn_rows,
                                            bass.IndirectOffsetOnAxis(ap=meta[:, b, h, 0:1], axis=0)
                                            ).then_inc(gathered[b], 16)

            def split_low(c, b):
                cols = slice(c * CHW, (c + 1) * CHW)
                return pool.tensor_tensor(wl[:, b, cols], wraw[:, b, cols], wh[:, b, cols].bitcast(F32), ALU.subtract)

            gather(0, 0, 0)
            gather(1, 1, 0)
            pool.wait_ge(gathered[0], 32)
            pool.sem_inc(issued, 1)
            for c in POOL_CH:
                pool.wait_ge(wh_done, c + 1)
                split_low(c, 0).then_inc(wlp_done, 1)

            def step(t, i, b, ahead=True):
                o = 1 - b
                if ahead:
                    for k, c in enumerate(POOL_CH):
                        pool.wait_ge(wh_done, t * NCH + NCH + c + 1)
                        split_low(c, o).then_inc(wlp_done, 1)
                    pool.wait_ge(turned, t + 1)
                    gather(t + 2, b, i + 1)
                    pool.wait_ge(gathered[o], i * 32 + (32 if b == 0 else 64))
                    pool.sem_inc(issued, 1)
                pool.wait_ge(y_done, t + 3)
                wait_apart(pool, added[o], i * 32 + (32 if b == 0 else 64), passed)
                for h in range(HALF):
                    pool.indirect_dma_start(x_rows, bass.IndirectOffsetOnAxis(ap=meta2[:, b, h, 0:1], axis=0),
                                            y[:, b, h, :], None, compute_op=ALU.add).then_inc(added[b], 16)

            with pool.Fori(0, TILES // 2) as i:
                for b in range(2):
                    step(i * 2 + b, i, b)
            step(TILES - 1, TILES // 2, 0, ahead=False)
            pool.wait_ge(added[0], 32 * (TILES // 2 + 1) + 32)
            pool.wait_ge(added[1], 32 * (TILES // 2) + 32)
            pool.wait_ge(gathered[1], 32 * (TILES // 2 + 1))

        def split_high(act, c, b):
            cols = slice(c * CHW, (c + 1) * CHW)
            act.activation(wh[:, b, cols], wraw[:, b, cols], ACT.Copy).then_inc(wh_done, 1)

        @block.scalar
        def _(act):
            act.wait_ge(w_loaded[0], 32)
            for c in range(NCH):
                split_high(act, c, 0)
            act.wait_ge(turned, 1)
            act.activation(xh[:], psX[:], ACT.Copy).then_inc(xh_done, 1)

            def step(t, i, b, ahead=True):
                o = 1 - b
                for hb in range(HB):
                    if ahead:
                        if hb == 0:
                            act.wait_ge(w_loaded[o], i * 32 + (32 if b == 0 else 64))
                            act.wait_ge(l2_done, t + 1)
                        split_high(act, hb, o)
                    if hb == 0:
                        act.wait_ge(small_loaded[b], i * 32 + 32)
                    act.wait_ge(l1_done, t * HB + hb // 2 * 2 + 2)
                    act.wait_ge(hl_done, t * pairs + hb // 2 + 1)
                    act.activation(hr[:, hb, :], psH[hb // 2][:, hb % 2, :], ACT.Relu,
                                   bias=b1s[:, b, hb:hb + 1]).then_inc(relu_done, 1)
                if ahead:
                    act.wait_ge(turned, t + 2)
                    act.wait_ge(l1_done, t * HB + HB)
                    act.activation(xh[:], psX[:], ACT.Copy).then_inc(xh_done, 1)
                act.wait_ge(yb_done, t + 3)
                act.wait_ge(added[b], i * 32 + 32)
                for h in range(HALF):
                    last = act.activation(y[:, b, h, :], yb[:, b, h, :], ACT.Copy,
                                          scale=meta2[:, b, h, 1:2].bitcast(F32))
                last.then_inc(y_done, 1)

            with act.Fori(0, TILES // 2) as i:
                for b in range(2):
                    step(i * 2 + b, i, b)
            step(TILES - 1, TILES // 2, 0, ahead=False)

        @block.vector
        def _(dve):
            dve.sem_inc(hl_done, pairs)
            dve.sem_inc(yb_done, 2)
            dve.sem_inc(relu_done, HB)
            dve.sem_inc(y_done, 2)

            def split_low(c, b):
                cols = slice(c * CHW, (c + 1) * CHW)
                dve.tensor_tensor(wl[:, b, cols], wraw[:, b, cols], wh[:, b, cols].bitcast(F32),
                                  ALU.subtract).then_inc(wl_done, 1)

            for c in range(NCH):
                if c not in POOL_CH:
                    dve.wait_ge(wh_done, c + 1)
                    split_low(c, 0)
            dve.wait_ge(xh_done, 1)
            dve.tensor_tensor(xl[:], psX[:], xh[:].bitcast(F32), ALU.subtract).then_inc(xl_done, 1)
            dve.wait_ge(meta_loaded[0], 16)
            dve.tensor_copy(meta2[:, 0], meta[:, 0]).then_inc(copied, 1)

            def step(t, i, b, ahead=True):
                o = 1 - b
                for k in range(pairs):
                    for c in (2 * k, 2 * k + 1):
                        if ahead and c not in POOL_CH:
                            dve.wait_ge(wh_done, t * NCH + NCH + c + 1)
                            split_low(c, o)
                    blocks = slice(2 * k, 2 * k + 2)
                    dve.wait_ge(relu_done, t * HB + 2 * k + 2 + HB)
                    if k == 0:
                        dve.wait_ge(l2_done, t + 1)
                    dve.tensor_copy(hh[:, blocks, :], hr[:, blocks, :]).then_inc(hh_done, 1)
                    dve.wait_ge(hh_done, t * pairs + k + 1)
                    dve.tensor_tensor(hl[:, blocks, :], hr[:, blocks, :], hh[:, blocks, :].bitcast(F32),
                                      ALU.subtract).then_inc(hl_done, 1)
                if ahead:
                    dve.wait_ge(xh_done, t + 2)
                    dve.tensor_tensor(xl[:], psX[:], xh[:].bitcast(F32), ALU.subtract).then_inc(xl_done, 1)
                    dve.wait_ge(meta_loaded[o], i * 16 + (16 if b == 0 else 32))
                    dve.wait_ge(added[o], i * 32 + (32 if b == 0 else 64))
                    dve.tensor_copy(meta2[:, o], meta[:, o]).then_inc(copied, 1)
                dve.wait_ge(l2_done, t + 2)
                dve.wait_ge(small_loaded[b], i * 32 + 32)
                dve.wait_ge(y_done, t + 1)
                dve.tensor_tensor(yb[:, b], psY[b][:], b2s[:, b, :].unsqueeze(1).broadcast_to([P, HALF, D]),
                                  ALU.add).then_inc(yb_done, 1)

            with dve.Fori(0, TILES // 2) as i:
                for b in range(2):
                    step(i * 2 + b, i, b)
            step(TILES - 1, TILES // 2, 0, ahead=False)

        @block.tensor
        def _(pe):
            pe.sem_inc(l2_done, 1)

            def turn(b):
                for h in range(HALF):
                    for k in range(KD):
                        last = pe.transpose(psX[:, k, h * P:(h + 1) * P], xg[:, b, h, k * P:(k + 1) * P], g.ident[:])
                last.then_inc(turned, 1)

            pe.wait_ge(gathered[0], 32)
            turn(0)

            def step(t, i, b, ahead=True):
                o = 1 - b
                pe.wait_ge(xl_done, t + 1)
                pe.wait_ge(wl_done, t * DCH + DCH)
                pe.wait_ge(wlp_done, t * len(POOL_CH) + len(POOL_CH))
                for hb in range(HB):
                    if hb % 2 == 0:
                        pe.wait_ge(relu_done, t * HB + hb + 2)
                    n = 0
                    for k in range(KD):
                        cols = slice(k * H + hb * P, k * H + (hb + 1) * P)
                        for w, x in ((wh, xh), (wh, xl), (wl, xh)):
                            last = pe.matmul(psH[hb // 2][:, hb % 2, :], w[:, b, cols], x[:, k, :],
                                             start=(n == 0), stop=(n == 3 * KD - 1))
                            n += 1
                    last.then_inc(l1_done, 1)
                if ahead:
                    pe.wait_ge(gathered[o], i * 32 + (32 if b == 0 else 64))
                    turn(o)
                pe.wait_ge(yb_done, t + 1)
                for hb in range(HB):
                    if hb % 2 == 0:
                        pe.wait_ge(hl_done, t * pairs + hb // 2 + 1 + pairs)
                    for h in range(HALF):
                        rows = slice(h * P, (h + 1) * P)
                        w2 = slice(W1 + hb * D, W1 + (hb + 1) * D)
                        for m, (hx, w) in enumerate(((hh, wh), (hh, wl), (hl, wh))):
                            last = pe.matmul(psY[b][:, h, :], hx[:, hb, rows], w[:, b, w2],
                                             start=(hb == 0 and h == 0 and m == 0), stop=(hb == HB - 1 and m == 2),
                                             skip_group_check=True)
                last.then_inc(l2_done, 1)

            with pe.Fori(0, TILES // 2) as i:
                for b in range(2):
                    step(i * 2 + b, i, b)
            step(TILES - 1, TILES // 2, 0, ahead=False)


def standardise_block(nc, g, x_rows, w1, b1, sp_, sh, sl):
    with ExitStack() as ctx:
        sb, ps = tensors(nc, ctx)
        sem = semaphores(nc, ctx, "std")
        w = sb("std_w", [P, KD, D])
        b = sb("std_b", [1, D])
        stats = sb("std_stats", [P, NT, 6])
        mv = sb("std_mv", [P, NT, 2])
        veps = sb("std_veps", [P, NT])
        rstd = sb("std_rstd", [P, NT])
        shift = sb("std_shift", [P, NT])
        negshift = sb("std_negshift", [P, NT])
        xn = sb("std_xn", [P, 2, D])
        xnT = sb("std_xnT", [P, 2, KD, P])
        sq = sb("std_sq", [P, 2, D])
        mean = sb("std_mean", [P, D])
        var = sb("std_var", [P, KD])
        half = sb("std_half", [P, KD])
        std = sb("std_std", [P, KD])
        stde = sb("std_stde", [P, KD])
        rinv = sb("std_rinv", [P, KD])
        diag = sb("std_diag", [P, KD, P])
        rb = sb("std_rb", [P, D])
        psT = [ps(f"std_psT{k}", [P, KD, P]) for k in range(2)]
        psZ = [ps(f"std_psZ{k}", [P, D]) for k in range(2)]
        psM = ps("std_psM", [P, D])
        psV = [ps(f"std_psV{k}", [P, 1]) for k in range(KD)]
        psB = psM

        x_loaded = [sem(f"x_loaded{k}") for k in range(2)]
        w_loaded = sem("w_loaded")
        dchain, stats_done, pchain, norm_done = sem("dchain"), sem("stats"), sem("pchain"), sem("norm")
        xn_done, tr_done, xnT_done, mm_done, z_done = (sem(n) for n in ("xn", "tr", "xnT", "mm", "z"))
        sum_done, mean_done, zc_done, sq_done, var_mm = (sem(n) for n in ("sum", "mean", "zc", "sq", "varmm"))
        var_done, root_done, diag_done, bc_done, s_done, sh_done = (
            sem(n) for n in ("var", "root", "diag", "bc", "s", "sh"))
        block = ctx.enter_context(nc.Block())
        FIRST = NT // 2

        @block.sync
        def _(sp):
            rows = x_rows[0:NPAD, :].rearrange("(t p) d -> p t d", p=P)
            sp.dma_start(g.x[:, 0:FIRST, :], rows[:, 0:FIRST, :]).then_inc(x_loaded[0], 16)
            sp.dma_start(g.x[:, FIRST:NT, :], rows[:, FIRST:NT, :]).then_inc(x_loaded[1], 16)
            sp.dma_start(w[:], w1.rearrange("(k p) n -> p k n", p=P)).then_inc(w_loaded, 16)
            sp.dma_start(b[:], b1).then_inc(w_loaded, 16)

        @block.vector
        def _(dve):
            chain = Chain(dve, dchain)
            for t in range(NT):
                if t in (0, FIRST):
                    dve.wait_ge(x_loaded[t // FIRST], 16)
                dve.bn_stats(stats[:, t, :], g.x[:, t, :]).then_inc(dchain, 1)
            chain.n = NT
            dve.wait_ge(dchain, NT)
            for t in range(NT):
                last = dve.bn_aggr(mv[:, t, :], stats[:, t, :])
            chain(last)
            dve.tensor_scalar(veps[:], mv[:, :, 1], LN_EPS, None, ALU.add).then_inc(stats_done, 1)
            dve.memset(half[:], 0.5)
            dve.wait_ge(sum_done, 1)
            dve.tensor_scalar(mean[:], psM[:], 1.0 / N, None, ALU.mult).then_inc(mean_done, 1)
            dve.wait_ge(mean_done, 1)
            for t in range(NT):
                dve.tensor_tensor(sp_[:, t, :], sp_[:, t, :], mean[:], ALU.subtract).then_inc(zc_done, 1)
            dve.wait_ge(var_mm, NT)
            for k in range(KD):
                last = dve.tensor_scalar(var[:, k:k + 1], psV[k][:], 1.0 / (N - 1), None, ALU.mult)
            last.then_inc(var_done, 1)
            dve.wait_ge(root_done, 1)
            chain(dve.tensor_scalar(stde[:], std[:], 1e-6, None, ALU.add))
            chain(dve.reciprocal(rinv[:], stde[:]))
            for k in range(KD):
                last = dve.tensor_scalar(diag[:, k, :], g.ident[:], rinv[:, k:k + 1], None, ALU.mult)
            last.then_inc(diag_done, 1)
            dve.wait_ge(bc_done, 1)
            chain(dve.tensor_copy(rb[:], psB[:]))
            for t in range(NT + 1):
                if t < NT:
                    dve.scalar_tensor_tensor(out=sp_[:, t, :], in0=sp_[:, t, :], scalar=g.dinv1[:, t:t + 1], in1=rb[:],
                                             op0=ALU.mult, op1=ALU.mult).then_inc(s_done, 1)
                if t >= 1:
                    dve.wait_ge(sh_done, t)
                    dve.tensor_tensor(sl[:, t - 1, :], sp_[:, t - 1, :], sh[:, t - 1, :].bitcast(F32), ALU.subtract)

        @block.gpsimd
        def _(pool):
            chain = Chain(pool, pchain)
            pool.wait_ge(stats_done, 1)
            chain(pool.tensor_tensor(rstd[:], veps[:], g.mhalf[:, 0:NT], ALU.pow))
            chain(pool.tensor_tensor(shift[:], mv[:, :, 0], rstd[:], ALU.mult))
            pool.tensor_scalar(negshift[:], shift[:], -1.0, 0.0, ALU.mult, ALU.add).then_inc(norm_done, 1)
            pool.wait_ge(var_done, 1)
            pool.tensor_tensor(std[:], var[:], half[:], ALU.pow).then_inc(root_done, 1)

        @block.scalar
        def _(act):
            act.wait_ge(norm_done, 1)
            for t in range(NT + 1):
                if t < NT:
                    if t >= 2:
                        act.wait_ge(tr_done, t - 1)
                    act.activation(xn[:, t % 2, :], g.x[:, t, :], ACT.Identity, bias=negshift[:, t:t + 1],
                                   scale=rstd[:, t:t + 1]).then_inc(xn_done, 1)
                    act.wait_ge(tr_done, t + 1)
                    if t >= 2:
                        act.wait_ge(mm_done, t - 1)
                    act.activation(xnT[:, t % 2], psT[t % 2][:], ACT.Copy).then_inc(xnT_done, 1)
                if t >= 1:
                    act.wait_ge(mm_done, t)
                    act.activation(sp_[:, t - 1, :], psZ[(t - 1) % 2][:], ACT.Copy).then_inc(z_done, 1)
            for t in range(NT):
                act.wait_ge(zc_done, t + 1)
                if t >= 2:
                    act.wait_ge(var_mm, t - 1)
                act.activation(sq[:, t % 2, :], sp_[:, t, :], ACT.Square).then_inc(sq_done, 1)
            for t in range(NT):
                act.wait_ge(s_done, t + 1)
                act.activation(sh[:, t, :], sp_[:, t, :], ACT.Copy).then_inc(sh_done, 1)

        def column_sum(pe, t):
            rows = g.valid if t == NT - 1 else g.ones
            pe.wait_ge(z_done, t + 1)
            return pe.matmul(psM[:], rows[:], sp_[:, t, :], start=(t == 0), stop=(t == NT - 1))

        @block.tensor
        def _(pe):
            pe.wait_ge(w_loaded, 32)
            for t in range(NT):
                pe.wait_ge(xn_done, t + 1)
                if t >= 2:
                    pe.wait_ge(xnT_done, t - 1)
                for k in range(KD):
                    last = pe.transpose(psT[t % 2][:, k, :], xn[:, t % 2, k * P:(k + 1) * P], g.ident[:])
                last.then_inc(tr_done, 1)
                if t >= 1:
                    last = column_sum(pe, t - 1)
                pe.wait_ge(xnT_done, t + 1)
                if t >= 2:
                    pe.wait_ge(z_done, t - 1)
                for k in range(KD):
                    pe.matmul(psZ[t % 2][:], xnT[:, t % 2, k, :], w[:, k, :], start=(k == 0), stop=False)
                pe.matmul(psZ[t % 2][:], g.ones[0:1, :], b[0:1, :], start=False, stop=True).then_inc(mm_done, 1)
            column_sum(pe, NT - 1).then_inc(sum_done, 1)
            for t in range(NT):
                rows = g.valid if t == NT - 1 else g.ones
                pe.wait_ge(sq_done, t + 1)
                for k in range(KD):
                    last = pe.matmul(psV[k][:], sq[:, t % 2, k * P:(k + 1) * P], rows[:, 0:1],
                                     start=(t == 0), stop=(t == NT - 1))
                last.then_inc(var_mm, 1)
            pe.wait_ge(diag_done, 1)
            for k in range(KD):
                last = pe.matmul(psB[:, k * P:(k + 1) * P], g.ones[:], diag[:, k, :], start=True, stop=True)
            last.then_inc(bc_done, 1)


def steps_block(nc, g, wt_in, lw_in, lb_in, b_in, h0, out):
    with ExitStack() as ctx:
        sb, ps = tensors(nc, ctx)
        sem = semaphores(nc, ctx, "ffn")
        Q = 2
        G = NT // Q
        W = Q * D
        BODY = 4
        R = 4
        wt = sb("ffn_wt", [P, KD, D])
        lw = sb("ffn_lw", [P, KD])
        lb = sb("ffn_lb", [P, KD])
        bias = sb("ffn_bias", [1, D])
        wlw = sb("ffn_wlw", [P, KD, D])
        lbm = sb("ffn_lbm", [P, KD, P])
        w2 = sb("ffn_w2", [P, KD, D])
        w2h = sb("ffn_w2h", [P, KD, D], F32R)
        w2l = sb("ffn_w2l", [P, KD, D], F32R)
        vT = sb("ffn_vT", [P, 2, Q * KD, P])
        vTh = sb("ffn_vTh", [P, 2, Q * KD, P], F32R)
        vTl = sb("ffn_vTl", [P, 2, Q * KD, P], F32R)
        th = sb("ffn_th", [P, R, W])
        u = sb("ffn_u", [P, R, W])
        stats = sb("ffn_stats", [P, NT, 6])
        mv = sb("ffn_mv", [P, NT, 2])
        veps = sb("ffn_veps", [P, NT])
        rstd = sb("ffn_rstd", [P, NT])
        mr = sb("ffn_mr", [P, NT])
        shift = sb("ffn_shift", [P, NT])
        vn = sb("ffn_vn", [P, NT, D])
        warm = sb("ffn_warm", [P, 1])
        psT = [ps(f"ffn_psT{k}", [P, Q * KD, P]) for k in range(R)]
        psH = [ps(f"ffn_psH{k}", [P, W]) for k in range(R)]
        psW = psT[0][:, 0:Q, :]

        loaded, wprep, delta_done, w_ready = sem("loaded"), sem("wprep"), sem("delta"), sem("w_ready")
        wlw_done = sem("wlw")
        turned, copied, lo_done = sem("turned"), sem("copied"), sem("lo")
        mm_done, th_done, u_done, v_done = sem("mm"), sem("th"), sem("u"), sem("v")
        st_done, aggr_done, eps_done, rstd_done = sem("stats"), sem("aggr"), sem("eps"), sem("rstd")
        mr_done, shift_done, vn_done = sem("mr"), sem("shift"), sem("vn")
        summed, stored = sem("summed"), sem("stored")
        passed = sem("passed")
        ALL = STEPS * G
        END = (STEPS + 1) * G
        LOW, MM, TANH, U, SILU, STATS, NORM = 1, 3, 4, 4, 5, 6, 8

        block = ctx.enter_context(nc.Block())

        def run(eng, slot):
            for n in range(2 * G):
                slot(n, n, lambda k: k // 2)
            with eng.Fori(0, (STEPS - 2) // BODY) as i:
                for k in range(BODY * G):
                    slot(i * (BODY * G) + (2 * G + k), 2 * G + k, lambda m: i * (BODY * G // 2) + m // 2)
            for n in range(STEPS * G, END + NORM):
                slot(n, n, lambda k: k // 2)

        def tiles(m):
            return slice(m % G * Q, m % G * Q + Q)

        def chained(m, lag):
            return 0 <= m - lag < ALL

        def split(m):
            return m % 2 == 1

        def lows(half, m):
            odd = m if m % 2 else m - 1
            return half(odd) - G // 2 + 1

        @block.sync
        def _(sp):
            sp.dma_start(wt[:], wt_in.rearrange("(k p) n -> p k n", p=P)).then_inc(loaded, 16)
            sp.dma_start(lw[:], lw_in).then_inc(loaded, 16)
            sp.dma_start(lb[:], lb_in).then_inc(loaded, 16)
            sp.dma_start(bias[:], b_in).then_inc(loaded, 16)
            for k in range(G):
                sp.wait_ge(summed, k + 1)
                rows = out[k * Q * P:(k + 1) * Q * P, :] if k < G - 1 else out[k * Q * P:k * Q * P + P, :]
                n = Q if k < G - 1 else 1
                sp.dma_start(rows.rearrange("(q p) d -> p q d", p=P), vn[:, k * Q:k * Q + n, :]).then_inc(stored, 16)
            sp.dma_start(out[(NT - 1) * P:N, :], vn[0:LAST, NT - 1, :]).then_inc(stored, 16)
            sp.wait_ge(stored, (G + 1) * 16)

        @block.tensor
        def _(pe):
            delta = psW.rearrange("p q n -> p (q n)")
            pe.wait_ge(wprep, 2)
            for k in range(KD):
                pe.matmul(delta, lbm[:, k, :], wt[:, k, :], start=(k == 0), stop=False)
            for k in range(KD):
                pe.matmul(delta, g.negones[:], wlw[:, k, :], start=False, stop=False)
            pe.matmul(delta, g.ones[0:1, :], bias[0:1, :], start=False, stop=True).then_inc(delta_done, 1)
            pe.wait_ge(w_ready, 3 * KD)

            def slot(n, m, half):
                if m < G:
                    if m >= R:
                        pe.wait_ge(u_done, n - R + 1)
                    for q in range(Q):
                        last = pe.matmul(psH[m % R][:, q * D:(q + 1) * D], g.ident[:], h0[:, m * Q + q, :],
                                         start=True, stop=True)
                    last.then_inc(mm_done, 1)
                    return
                if m < END:
                    gr = m % G
                    pe.wait_ge(vn_done, n - G + 1)
                    if m - R >= G:
                        pe.wait_ge(copied, n - R - G + 1)
                        if split(m):
                            pe.wait_ge(lo_done, lows(half, m - R))
                    for q in range(Q):
                        for k in range(KD):
                            last = pe.transpose(psT[m % R][:, q * KD + k, :], vn[:, gr * Q + q, k * P:(k + 1) * P],
                                                g.ident[:])
                    last.then_inc(turned, 1)
                if G <= m - MM < END:
                    w = m - MM
                    if w - R < ALL:
                        pe.wait_ge(u_done, n - MM - R + 1)
                    else:
                        pe.wait_ge(summed, n - MM - R - ALL + 1)
                    if split(w):
                        pe.wait_ge(lo_done, lows(half, w))
                        s = w // 2 % 2
                        pairs = ((vTh, w2h), (vTh, w2l), (vTl, w2h))
                    else:
                        pe.wait_ge(copied, n - MM - G + 1)
                        s = w // 2 % 2
                        pairs = ((vT, w2),)
                    for q in range(Q):
                        for k in range(KD):
                            for j, (a, b) in enumerate(pairs):
                                last = pe.matmul(psH[w % R][:, q * D:(q + 1) * D], a[:, s, q * KD + k, :], b[:, k, :],
                                                 start=(k == 0 and j == 0), stop=(k == KD - 1 and j == len(pairs) - 1))
                    last.then_inc(mm_done, 1)

            run(pe, slot)

        @block.scalar
        def _(act):
            act.wait_ge(w_ready, KD)
            for k in range(KD):
                act.activation(w2h[:, k, :], w2[:, k, :], ACT.Copy).then_inc(w_ready, 1)
            act.activation(warm[:], w2[:, 0, 0:1], ACT.Silu)

            def slot(n, m, half):
                if G <= m < END:
                    act.wait_ge(turned, n - G + 1)
                    if m - R >= 0:
                        act.wait_ge(mm_done, n - R + 1)
                    to = vTh if split(m) else vT
                    act.activation(to[:, m // 2 % 2], psT[m % R][:], ACT.Copy).then_inc(copied, 1)
                if chained(m, TANH):
                    a = (m - TANH) % R
                    act.wait_ge(mm_done, n - TANH + 1)
                    if m - TANH >= R:
                        act.wait_ge(u_done, n - TANH - R + 1)
                    act.activation(th[:, a], psH[a][:], ACT.Tanh).then_inc(th_done, 1)
                if chained(m, SILU):
                    act.wait_ge(u_done, n - SILU + 1)
                    act.activation(vn[:, tiles(m - SILU)].rearrange("p q d -> p (q d)"), u[:, (m - SILU) % R],
                                   ACT.Silu).then_inc(v_done, 1)

            run(act, slot)

        @block.vector
        def _(dve):
            dve.wait_ge(loaded, 64)
            for k in range(KD):
                dve.tensor_scalar(wlw[:, k, :], wt[:, k, :], lw[:, k:k + 1], None, ALU.mult).then_inc(wlw_done, 1)
                last = dve.tensor_scalar(lbm[:, k, :], g.ones[:], lb[:, k:k + 1], None, ALU.mult)
            last.then_inc(wprep, 2)
            dve.wait_ge(wlw_done, KD)
            dve.wait_ge(delta_done, 1)
            for k in range(KD):
                dve.scalar_tensor_tensor(out=w2[:, k, :], in0=psW.rearrange("p q n -> p (q n)"), scalar=1.0 / D,
                                         in1=wlw[:, k, :], op0=ALU.mult, op1=ALU.add).then_inc(w_ready, 1)
            dve.wait_ge(w_ready, 2 * KD)
            for k in range(KD):
                dve.tensor_tensor(w2l[:, k, :], w2[:, k, :], w2h[:, k, :].bitcast(F32), ALU.subtract).then_inc(w_ready, 1)

            def slot(n, m, half):
                if chained(m, NORM):
                    q = tiles(m - NORM)
                    dve.wait_ge(rstd_done, n - NORM + 1)
                    dve.tensor_tensor(mr[:, q], mv[:, q, 0], rstd[:, q], ALU.mult).then_inc(mr_done, 1)
                if chained(m, STATS):
                    dve.wait_ge(v_done, n - STATS + 1)
                    for q in range(Q):
                        t = (m - STATS) % G * Q + q
                        last = dve.bn_stats(stats[:, t, :], vn[:, t, :])
                    last.then_inc(st_done, 1)
                if chained(m, NORM):
                    q = tiles(m - NORM)
                    dve.wait_ge(mr_done, n - NORM + 1)
                    dve.tensor_scalar(shift[:, q], mr[:, q], -1.0, 1.0, ALU.mult, ALU.add).then_inc(shift_done, 1)
                if G <= m - LOW < END and split(m - LOW):
                    w = m - LOW
                    dve.wait_ge(copied, n - LOW - G + 1)
                    dve.tensor_tensor(vTl[:, w // 2 % 2], psT[w % R][:], vTh[:, w // 2 % 2].bitcast(F32),
                                      ALU.subtract).then_inc(lo_done, 1)
                if chained(m, U):
                    a = (m - U) % R
                    dve.wait_ge(th_done, n - U + 1)
                    if m - U >= R:
                        dve.wait_ge(v_done, n - U - R + 1)
                    dve.scalar_tensor_tensor(out=u[:, a], in0=th[:, a], scalar=0.01, in1=psH[a][:],
                                             op0=ALU.mult, op1=ALU.add).then_inc(u_done, 1)
                if chained(m, STATS):
                    wait_apart(dve, st_done, n - STATS + 1, passed)
                    for q in range(Q):
                        t = (m - STATS) % G * Q + q
                        last = dve.bn_aggr(mv[:, t, :], stats[:, t, :])
                    last.then_inc(aggr_done, 1)
                if ALL <= m - U < END:
                    dve.wait_ge(mm_done, n - U + 1)
                    dve.tensor_tensor(vn[:, tiles(m - U), :], g.x[:, tiles(m - U), :],
                                      psH[(m - U) % R][:].rearrange("p (q d) -> p q d", q=Q),
                                      ALU.add).then_inc(summed, 1)

            run(dve, slot)

        @block.gpsimd
        def _(pool):
            def slot(n, m, half):
                if chained(m, STATS):
                    q = tiles(m - STATS)
                    wait_apart(pool, aggr_done, n - STATS + 1, passed)
                    pool.tensor_scalar(veps[:, q], mv[:, q, 1], 1.0, LN_EPS, ALU.mult, ALU.add).then_inc(eps_done, 1)
                    pool.wait_ge(eps_done, n - STATS + 1)
                    pool.tensor_tensor(rstd[:, q], veps[:, q], g.mhalf[:, 0:Q], ALU.pow).then_inc(rstd_done, 1)
                if chained(m, NORM):
                    wait_apart(pool, shift_done, n - NORM + 1, passed)
                    for q in range(Q):
                        t = (m - NORM) % G * Q + q
                        last = pool.tensor_scalar(vn[:, t, :], vn[:, t, :], rstd[:, t:t + 1], shift[:, t:t + 1],
                                                  ALU.mult, ALU.add)
                    last.then_inc(vn_done, 1)

            run(pool, slot)


def two_layer_graph_network(nc, x, adjt, w0, wg, bg, wall, eb1, eb2, w1, b1, ffw, lw, lb, fb, out):
    xn_rows = nc.dram_tensor("xn_rows", (ROWS, D), F32, kind="Internal").ap()
    x_rows = nc.dram_tensor("x_rows", (ROWS, D), F32, kind="Internal").ap()
    table = nc.dram_tensor("slot_table", (SLOTS, 2), U32, kind="Internal").ap()
    with ExitStack() as ctx:
        sb, _ = tensors(nc, ctx)
        g = Shared(sb)
        sched = sb("sched", [1, 2, TILES + 1], I32)
        constants_block(nc, g)
        with ExitStack() as layer0:
            sb0, _ = tensors(nc, layer0)
            s_row = sb0("l0_s", [P, NT, D])
            with ExitStack() as conv:
                sbc, _ = tensors(nc, conv)
                outT = sbc("l0_outT", [P, KD, NPAD])
                with ExitStack() as split:
                    sbs, _ = tensors(nc, split)
                    sh = sbs("l0_sh", [P, NT, D], F32R)
                    sl = sbs("l0_sl", [P, NT, D], F32R)
                    support_block(nc, g, x, w0, adjt, s_row, sh, sl)
                    graph_block(nc, g, "g0", adjt, sh, sl, outT)
                hn = sbc("l0_hn", [P, NT, D])
                residual_block(nc, g, "res0", s_row, outT, g.dinv0, True, hn)
                routing_block(nc, g, wg, bg, hn, xn_rows, x_rows, table, sched)
        experts_block(nc, g, wall, eb1, eb2, xn_rows, x_rows, table, sched)
        with ExitStack() as layer1:
            sb1, _ = tensors(nc, layer1)
            s_row = sb1("l1_s", [P, NT, D])
            outT = sb1("l1_outT", [P, KD, NPAD])
            with ExitStack() as split:
                sbs, _ = tensors(nc, split)
                sh = sbs("l1_sh", [P, NT, D], F32R)
                sl = sbs("l1_sl", [P, NT, D], F32R)
                standardise_block(nc, g, x_rows, w1, b1, s_row, sh, sl)
                graph_block(nc, g, "g1", adjt, sh, sl, outT)
            h0 = sb1("l1_h0", [P, NT, D])
            residual_block(nc, g, "res1", s_row, outT, g.dinv1, False, h0)
            steps_block(nc, g, ffw, lw, lb, fb, h0, out)


def kernel(x, adj, L0_gnn_W, L0_ffn_Wg, L0_ffn_bg, L0_ffn_W1, L0_ffn_b1, L0_ffn_W2, L0_ffn_b2, L1_gnn_W, L1_gnn_b,
           L1_ffn_ln_w, L1_ffn_ln_b, L1_ffn_W, L1_ffn_b):
    import numpy as np
    from concourse import bacc
    from concourse.bass_utils import run_bass_kernel_spmd

    f = lambda a: np.asarray(a)
    c = np.ascontiguousarray
    xp = np.zeros((NPAD, D), np.float32)
    xp[:N] = f(x)
    at = np.zeros((NPAD, NPAD), np.float32)
    at[:N, :N] = f(adj).T
    at = at.reshape(CHUNKS, CT, P, PANELS, PANEL).transpose(3, 0, 2, 1, 4).reshape(PANELS * CHUNKS * P, CW)
    w1 = f(L0_ffn_W1).transpose(0, 2, 1).reshape(E, KD, P, H).transpose(0, 2, 1, 3).reshape(E * P, KD * H)
    w2 = f(L0_ffn_W2).transpose(0, 2, 1).reshape(E, HB, P, D).transpose(0, 2, 1, 3).reshape(E * P, HB * D)
    arrays = {
        "x": xp, "adjt": c(at), "w0": c(f(L0_gnn_W).T), "wg": c(f(L0_ffn_Wg).T), "bg": c(f(L0_ffn_bg).reshape(1, E)),
        "wall": c(np.concatenate([w1, w2], 1)),
        "eb1": c(f(L0_ffn_b1).reshape(E, HB, P).transpose(0, 2, 1).reshape(E * P, HB)), "eb2": c(f(L0_ffn_b2)),
        "w1": c(f(L1_gnn_W).T), "b1": c(f(L1_gnn_b).reshape(1, D)), "ffw": c(f(L1_ffn_W).T),
        "lw": c(f(L1_ffn_ln_w).reshape(KD, P).T), "lb": c(f(L1_ffn_ln_b).reshape(KD, P).T),
        "fb": c(f(L1_ffn_b).reshape(1, D)),
    }
    nc = bacc.Bacc("TRN2", target_bir_lowering=False, num_devices=1)
    aps = {k: nc.dram_tensor(f"in_{k}", a.shape, mybir.dt.from_np(a.dtype), kind="ExternalInput").ap()
           for k, a in arrays.items()}
    out = nc.dram_tensor("out", (N, D), F32, kind="ExternalOutput").ap()
    two_layer_graph_network(nc, **aps, out=out)
    r = run_bass_kernel_spmd(nc, [{f"in_{k}": a for k, a in arrays.items()}], core_ids=[0])
    return r.results[0]["out"]
```

```python
from contextlib import ExitStack

import concourse.bass as bass
from concourse import mybir

F32 = mybir.dt.float32
F32R = mybir.dt.float32r
U32 = mybir.dt.uint32
I32 = mybir.dt.int32
ALU = mybir.AluOpType
ACT = mybir.ActivationFunctionType
AX = mybir.AxisListType

P = 128
N = 3327
NT = (N + P - 1) // P
NPAD = NT * P
LAST = N - (NT - 1) * P
D = 256
KD = D // P
E = 8
H = 1024
HB = H // P
LN_EPS = 1e-5
STEPS = 30

PT = 3
PANEL = PT * P
PANELS = NT // PT
LT = NT - PANELS * PT
LPANEL = LT * P
CT = 2
CHUNKS = NT // CT
CW = CT * PANEL
LCW = CT * LPANEL

TW = 256
REG = ((N + TW - 1) // TW + 1) * TW
TILES = (2 * N + E * (TW - 1)) // TW
SLOTS = E * REG + (TILES + 1) * TW
ROWS = NPAD + TW
KMAX = (N + TW - 1) // TW
INITP = SLOTS // (2 * TW)


class Shared:

    def __init__(self, sb):
        self.ident = sb("ident", [P, P])
        self.ones = sb("ones", [P, P])
        self.negones = sb("negones", [P, P])
        self.before = sb("before", [P, P])
        self.valid = sb("valid", [P, P])
        self.mhalf = sb("mhalf", [P, NT])
        self.dinv0 = sb("dinv0", [P, NT])
        self.dinv1 = sb("dinv1", [P, NT])
        self.x = sb("x", [P, NT, D])


class Routing:

    def __init__(self, sb, wg, bg, xn_rows, x_rows, table, sched):
        self.wg, self.bg, self.xn_rows, self.x_rows, self.table, self.sched = wg, bg, xn_rows, x_rows, table, sched
        self.wg_sb = sb("rt_wg", [P, KD, E])
        self.bg_sb = sb("rt_bg", [1, E])
        self.rev_i = sb("rt_rev_i", [P, E], I32)
        self.rev = sb("rt_rev", [P, E])
        self.reg_i = sb("rt_reg_i", [P, E], I32)
        self.reg = sb("rt_reg", [P, E])
        self.k_i = sb("rt_k_i", [P, KMAX], I32)
        self.kf = sb("rt_k", [P, KMAX])
        self.t_i = sb("rt_t_i", [P, TILES + 1], I32)
        self.tf = sb("rt_t", [P, TILES + 1])
        self.token = sb("rt_token", [P, NT], U32)
        self.free = sb("rt_free", [P, PT + 1, E])


class Chain:

    def __init__(self, eng, sem, passed=None):
        self.eng, self.sem, self.n, self.passed = eng, sem, 0, passed

    def __call__(self, ins):
        self.n = self.n + 1
        ins.then_inc(self.sem, 1)
        if self.passed is None:
            self.eng.wait_ge(self.sem, self.n)
        else:
            wait_apart(self.eng, self.sem, self.n, self.passed)


def wait_apart(eng, sem, value, passed):
    eng.wait_ge(sem, value)
    eng.sem_inc(passed, 1)


def tensors(nc, stack):
    def sb(name, shape, dt=F32):
        return stack.enter_context(nc.sbuf_tensor(name, shape, dt))

    def ps(name, shape, dt=F32):
        return stack.enter_context(nc.psum_tensor(name, shape, dt))

    return sb, ps


def semaphores(nc, stack, tag):
    held = []

    def clear():
        nc.clear_and_free_semaphores(held)
        nc.all_engine_barrier()

    stack.callback(clear)

    def sem(name):
        held.append(nc.alloc_semaphore(f"{tag}_{name}"))
        return held[-1]

    return sem


def constants_block(nc, g):
    with ExitStack() as ctx:
        sem = semaphores(nc, ctx, "const")
        filled = sem("filled")
        block = ctx.enter_context(nc.Block())

        @block.gpsimd
        def _(pool):
            pool.memset(g.ident[:], 0.0)
            pool.memset(g.ones[:], 1.0)
            pool.memset(g.negones[:], -1.0)
            pool.memset(g.mhalf[:], -0.5).then_inc(filled, 1)
            pool.wait_ge(filled, 1)
            pool.affine_select(out=g.ident[:], in_=g.ident[:], compare_op=ALU.not_equal, fill=1.0, base=0,
                               pattern=[[-1, P]], channel_multiplier=1)
            pool.affine_select(out=g.before[:], in_=g.ones[:], compare_op=ALU.is_gt, fill=0.0, base=0,
                               pattern=[[1, P]], channel_multiplier=-1)
            pool.affine_select(out=g.valid[:], in_=g.ones[:], compare_op=ALU.is_ge, fill=0.0, base=LAST - 1,
                               pattern=[[0, P]], channel_multiplier=-1).then_inc(filled, 1)
            pool.wait_ge(filled, 2)


def support_block(nc, g, x_in, w0, adjt, adjl, sp_, route):
    with ExitStack() as ctx:
        sb, ps = tensors(nc, ctx)
        sem = semaphores(nc, ctx, "sup")
        ring = sb("deg_ring", [P, CHUNKS, CW])
        part = sb("deg_part", [P, 3, PANEL])
        colsum = sb("deg_colsum", [P, NPAD])
        w = sb("sup_w", [P, KD, D])
        stats = sb("sup_stats", [P, NT, 6])
        mv = sb("sup_mv", [P, NT, 2])
        veps = sb("sup_veps", [P, NT])
        rstd = sb("sup_rstd", [P, NT])
        shift = sb("sup_shift", [P, NT])
        negshift = sb("sup_negshift", [P, NT])
        xn = sb("sup_xn", [P, 2, D])
        xnT = sb("sup_xnT", [P, 2, KD, P])
        deg = sb("sup_deg", [P, NT])
        degc = sb("sup_degc", [P, NT])
        has = sb("sup_has", [P, NT])
        root = sb("sup_root", [P, NT])
        psT = [ps(f"sup_psT{k}", [P, KD, P]) for k in range(2)]
        psS = [ps(f"sup_psS{k}", [P, D]) for k in range(2)]
        psD = ps("sup_psD", [P, NT])
        init = sb("rt_init", [INITP, 2, TW, 2], U32)
        zero = sb("rt_zero", [P, TW // P, D])
        filled, stored = sem("filled"), sem("stored")

        x_loaded, w_loaded = sem("x_loaded"), sem("w_loaded")
        chunk_loaded = [sem(f"chunk{c}") for c in range(CHUNKS)]
        chunks_used = sem("chunks_used")
        parts_done = sem("parts_done")
        colsum_done = sem("colsum_done")
        dchain = sem("dchain")
        stats_done, norm_done = sem("stats_done"), sem("norm_done")
        pchain = sem("pchain")
        xn_done, tr_done, xnT_done, mm_done, sup_done = (sem(n) for n in ("xn", "tr", "xnT", "mm", "sup"))
        deg_mm, deg_done, dinv_done = (sem(n) for n in ("degmm", "deg", "dinv"))
        GROUPS = [(0, 4), (4, 8), (8, CHUNKS)]
        group_of = [next(k for k, (a, b) in enumerate(GROUPS) if a <= c < b) for c in range(CHUNKS)]

        block = ctx.enter_context(nc.Block())

        @block.sync
        def _(sp):
            sp.dma_start(g.x[:], x_in.rearrange("(t p) d -> p t d", p=P)).then_inc(x_loaded, 16)
            sp.dma_start(w[:], w0.rearrange("(k p) n -> p k n", p=P)).then_inc(w_loaded, 16)
            with sp.Fori(0, PANELS) as p:
                for c in range(CHUNKS):
                    if c in (a for a, _ in GROUPS):
                        sp.wait_ge(chunks_used, p * 3 + group_of[c] + 1)
                    sp.dma_start(ring[:, c, :], adjt[bass.ds((p * CHUNKS + c) * P, P), :]).then_inc(chunk_loaded[c], 16)
            for c in range(CHUNKS):
                if c in (a for a, _ in GROUPS):
                    sp.wait_ge(chunks_used, PANELS * 3 + group_of[c] + 1)
                sp.dma_start(ring[:, c, 0:LCW], adjl[c * P:(c + 1) * P, :]).then_inc(chunk_loaded[c], 16)
            sp.wait_ge(filled, 2)
            sp.dma_start(route.xn_rows[NPAD:ROWS, :].rearrange("(t p) d -> p t d", p=P), zero[:]).then_inc(stored, 16)
            sp.dma_start(route.table.rearrange("(p m) c -> p m c", p=INITP),
                         init[:].rearrange("p a m c -> p (a m) c")).then_inc(stored, 16)
            sp.dma_start(route.wg_sb[:], route.wg.rearrange("(k p) e -> p k e", p=P)).then_inc(stored, 16)
            sp.dma_start(route.bg_sb[:], route.bg).then_inc(stored, 16)
            sp.wait_ge(stored, 64)

        @block.vector
        def _(dve):
            chain = Chain(dve, dchain)
            dve.sem_inc(chunks_used, 3)
            dve.sem_inc(colsum_done, 1)
            dve.wait_ge(x_loaded, 16)
            for t in range(NT):
                dve.bn_stats(stats[:, t, :], g.x[:, t, :]).then_inc(dchain, 1)
            chain.n = NT
            dve.wait_ge(dchain, NT)
            for t in range(NT):
                last = dve.bn_aggr(mv[:, t, :], stats[:, t, :])
            chain(last)
            dve.tensor_scalar(veps[:], mv[:, :, 1], LN_EPS, None, ALU.add).then_inc(stats_done, 1)
            dve.wait_ge(filled, 1)
            dve.tensor_copy(route.rev[:], route.rev_i[:])
            dve.tensor_copy(route.reg[:], route.reg_i[:])
            dve.tensor_copy(route.free[:, PT, :], route.reg_i[:])
            dve.tensor_copy(route.kf[:], route.k_i[:])
            dve.tensor_copy(route.tf[:], route.t_i[:])
            with dve.Fori(0, PANELS) as p:
                for k, (a, b) in enumerate(GROUPS):
                    if k == 0:
                        dve.wait_ge(colsum_done, p + 1)
                    for c in range(a, b):
                        dve.wait_ge(chunk_loaded[c], p * 16 + 16)
                    blocks = ring[:, a:b, :].rearrange("p c (q i) -> p i (c q)", i=PANEL)
                    dve.tensor_reduce(part[:, k, :], blocks, AX.X, ALU.add).then_inc(chunks_used, 1)
                dve.wait_ge(chunks_used, p * 3 + 6)
                dve.tensor_reduce(colsum[:, bass.ds(p * PANEL, PANEL)], part[:].rearrange("p k i -> p i k"),
                                  AX.X, ALU.add).then_inc(colsum_done, 1)
            dve.wait_ge(colsum_done, PANELS + 1)
            for k, (a, b) in enumerate(GROUPS):
                for c in range(a, b):
                    dve.wait_ge(chunk_loaded[c], PANELS * 16 + 16)
                blocks = ring[:, a:b, 0:LCW].rearrange("p c (q i) -> p i c q", i=LPANEL)
                dve.tensor_reduce(part[:, k, 0:LPANEL], blocks, AX.XY, ALU.add).then_inc(chunks_used, 1)
            dve.wait_ge(chunks_used, PANELS * 3 + 6)
            dve.tensor_reduce(colsum[:, PANELS * PANEL:NPAD], part[:, :, 0:LPANEL].rearrange("p k i -> p i k"),
                              AX.X, ALU.add).then_inc(colsum_done, 1)
            dve.wait_ge(deg_mm, 1)
            chain(dve.tensor_scalar(deg[:], psD[:], 1.0, None, ALU.add))
            dve.tensor_scalar(has[:], deg[:], 0.0, None, ALU.is_gt)
            dve.tensor_scalar(degc[:], deg[:], 1e-30, None, ALU.max).then_inc(deg_done, 1)
            dve.wait_ge(dinv_done, 2)
            dve.tensor_tensor(g.dinv1[:], root[:], has[:], ALU.mult)

        @block.gpsimd
        def _(pool):
            chain = Chain(pool, pchain)
            pool.iota(route.rev_i[:], [[-1, E]], base=E, channel_multiplier=0)
            pool.iota(route.reg_i[:], [[REG, E]], base=0, channel_multiplier=0)
            pool.iota(route.k_i[:], [[TW, KMAX]], base=0, channel_multiplier=0)
            pool.iota(route.t_i[:], [[1, TILES + 1]], base=0, channel_multiplier=0).then_inc(filled, 1)
            pool.iota(route.token[:], [[P, NT]], base=0, channel_multiplier=1)
            pool.iota(init[:, :, :, 0], [[0, 2], [1, TW]], base=NPAD, channel_multiplier=0)
            pool.memset(init[:, :, :, 1], 0)
            pool.memset(zero[:], 0.0).then_inc(filled, 1)
            pool.wait_ge(stats_done, 1)
            chain(pool.tensor_tensor(rstd[:], veps[:], g.mhalf[:, 0:NT], ALU.pow))
            chain(pool.tensor_tensor(shift[:], mv[:, :, 0], rstd[:], ALU.mult))
            pool.tensor_scalar(negshift[:], shift[:], -1.0, 0.0, ALU.mult, ALU.add).then_inc(norm_done, 1)
            pool.wait_ge(deg_done, 1)
            pool.tensor_tensor(g.dinv0[:], deg[:], g.mhalf[:, 0:NT], ALU.pow).then_inc(dinv_done, 1)
            pool.tensor_tensor(root[:], degc[:], g.mhalf[:, 0:NT], ALU.pow).then_inc(dinv_done, 1)

        @block.scalar
        def _(act):
            act.wait_ge(norm_done, 1)
            for t in range(NT + 1):
                if t < NT:
                    if t >= 2:
                        act.wait_ge(tr_done, t - 1)
                    act.activation(xn[:, t % 2, :], g.x[:, t, :], ACT.Identity, bias=negshift[:, t:t + 1],
                                   scale=rstd[:, t:t + 1]).then_inc(xn_done, 1)
                    act.wait_ge(tr_done, t + 1)
                    if t >= 2:
                        act.wait_ge(mm_done, t - 1)
                    act.activation(xnT[:, t % 2], psT[t % 2][:], ACT.Copy).then_inc(xnT_done, 1)
                if t >= 1:
                    act.wait_ge(mm_done, t)
                    act.activation(sp_[:, t - 1, :], psS[(t - 1) % 2][:], ACT.Copy).then_inc(sup_done, 1)

        @block.tensor
        def _(pe):
            pe.wait_ge(w_loaded, 16)
            for t in range(NT):
                pe.wait_ge(xn_done, t + 1)
                if t >= 2:
                    pe.wait_ge(xnT_done, t - 1)
                for k in range(KD):
                    last = pe.transpose(psT[t % 2][:, k, :], xn[:, t % 2, k * P:(k + 1) * P], g.ident[:])
                last.then_inc(tr_done, 1)
                pe.wait_ge(xnT_done, t + 1)
                if t >= 2:
                    pe.wait_ge(sup_done, t - 1)
                for k in range(KD):
                    last = pe.matmul(psS[t % 2][:], xnT[:, t % 2, k, :], w[:, k, :], start=(k == 0), stop=(k == KD - 1))
                last.then_inc(mm_done, 1)
            pe.wait_ge(colsum_done, PANELS + 2)
            for t in range(NT):
                last = pe.matmul(psD[:, t:t + 1], colsum[:, t * P:(t + 1) * P], g.ones[:, 0:1], start=True, stop=True)
            last.then_inc(deg_mm, 1)


def graph_block(nc, g, tag, adjt, adjl, s_row, dinv, column_scale, relu, hn, route=None):
    with ExitStack() as ctx:
        sb, ps = tensors(nc, ctx)
        sem = semaphores(nc, ctx, tag)
        SPLITS = 4
        sh = sb(f"{tag}_sh", [P, NT, D], F32R)
        sl = sb(f"{tag}_sl", [P, NT, D], F32R)
        raw = sb(f"{tag}_raw", [P, CHUNKS, CW])
        hi = sb(f"{tag}_hi", [P, SPLITS, PANEL], F32R)
        lo = sb(f"{tag}_lo", [P, SPLITS, PANEL], F32R)
        out_t = sb(f"{tag}_out_t", [P, KD, PANEL])
        dscale = sb(f"{tag}_dscale", [P, PT])
        plus_s = sb(f"{tag}_plus_s", [P, PT, D])
        delta = sb(f"{tag}_delta", [P, PT, D])
        stats = sb(f"{tag}_stats", [P, PT, 6])
        mv = sb(f"{tag}_mv", [P, PT, 2])
        veps = sb(f"{tag}_veps", [P, PT])
        rstd = sb(f"{tag}_rstd", [P, PT])
        mr = sb(f"{tag}_mr", [P, PT])
        shift = sb(f"{tag}_shift", [P, PT])
        if route:
            n2 = [P, PT]
            hn = sb("rt_hn", [P, 2, PT, D])
            hT = sb("rt_hT", [P, PT, D])
            sc = sb("rt_scores", [P, PT, E])
            sc2 = sb("rt_scores2", [P, PT, E])
            best = [sb(f"rt_best{k}", n2) for k in range(2)]
            first_one = [sb(f"rt_first{k}", n2) for k in range(2)]
            hot = [sb(f"rt_hot{k}", [P, PT, E]) for k in range(2)]
            work = [sb(f"rt_work{k}", [P, PT, E]) for k in range(2)]
            chosen = sb("rt_chosen", [P, PT, E])
            diff = sb("rt_diff", n2)
            ex = sb("rt_ex", n2)
            ex1 = sb("rt_ex1", n2)
            pos = sb("rt_pos", [P, PT, E])
            slot_f = [sb(f"rt_slotf{k}", n2) for k in range(2)]
            slot = [sb(f"rt_slot{k}", n2, U32) for k in range(2)]
            prob = [sb(f"rt_prob{k}", n2) for k in range(2)]
            meta = sb("rt_meta", [P, 2, PT, 2], U32)
            psR = ps("rt_psR", [P, 3, PT * E])
            hback, hT_done, gate_done, chosen_done = sem("hback"), sem("hT"), sem("gate"), sem("chosen")
            exp_in, exp_out, rank_done, slots_done = sem("exp_in"), sem("exp_out"), sem("rank"), sem("slots")
            dchain, stored, scattered, slots_used = sem("dchain"), sem("stored"), sem("scattered"), sem("slots_used")
        acc = [[ps(f"{tag}_acc{b}{d}", [P, PANEL]) for d in range(KD)] for b in range(2)]
        psT = ps(f"{tag}_psT", [P, PT, 512])

        chunk_loaded = [sem(f"chunk{c}") for c in range(CHUNKS)]
        s_done, sh_done, sl_done = sem("s"), sem("sh"), sem("sl")
        hi_done, lo_done, mm_done = sem("hi"), sem("lo"), sem("mm")
        evicted, tr_done, add_done, act_done, x_done = (sem(n) for n in ("evicted", "tr", "add", "act", "x"))
        dscale_done, st_done, aggr_done, hn_done = sem("dscale"), sem("stats"), sem("aggr"), sem("hn")
        eps_done, rstd_done, mr_done, shift_done = sem("eps"), sem("rstd"), sem("mr"), sem("shift")
        passed = sem("passed")
        LINKS = 12 + 3 + 1 + PT + 1 + 4

        block = ctx.enter_context(nc.Block())

        def run(eng, panel, finish):
            for p in range(2):
                panel(p, p)
            with eng.Fori(0, (PANELS - 2) // 2) as i:
                for m in (2, 3):
                    panel(i * 2 + m, m)
            panel(PANELS, PANELS)
            finish(PANELS + 1, PANELS + 1)
            if route:
                finish(PANELS + 2, PANELS + 2)

        def width(m):
            return PANEL if m < PANELS else LPANEL

        def split_slot(m, j):
            return (m * NT + j) % SPLITS

        def rows(p, m):
            n = PT if m <= PANELS else LT
            first = (p - 1) * PT
            return n, (slice(first, first + n) if isinstance(p, int) else bass.ds(first, n))

        def routed(m):
            return 0 if m < 2 else PT if m <= PANELS + 1 else LT

        @block.sync
        def _(sp):
            def store(p, m):
                n = routed(m)
                if not route or not n:
                    return
                first = (p - 2) * PT
                tiles = slice(first, first + n) if isinstance(p, int) else bass.ds(first, n)
                rows_of = slice(first * P, (first + n) * P) if isinstance(p, int) else bass.ds(first * P, n * P)
                sp.wait_ge(hn_done, p - 1)
                for to, rows_ in ((route.xn_rows, hn[:, m % 2, 0:n, :]), (route.x_rows, g.x[:, tiles, :])):
                    sp.dma_start(to[rows_of, :].rearrange("(t p) d -> p t d", p=P), rows_).then_inc(stored, 16)

            def finish(p, m):
                store(p, m)
                if route and m == PANELS + 2:
                    sp.wait_ge(stored, 32 * (PANELS + 2))

            def panel(p, m):
                for c in range(CHUNKS):
                    if c == 4:
                        store(p, m)
                    if m >= 1:
                        sp.wait_ge(lo_done, p * NT + ((c + 1) * CT - NT))
                    if m < PANELS:
                        row = (p * CHUNKS + c) * P
                        src = adjt[row:row + P, :] if isinstance(p, int) else adjt[bass.ds(row, P), :]
                    else:
                        src = adjl[c * P:(c + 1) * P, :]
                    sp.dma_start(raw[:, c, 0:CT * width(m)], src).then_inc(chunk_loaded[c], 16)

            run(sp, panel, finish)

        @block.scalar
        def _(act):
            if route:
                for counted, by in ((hback, 1), (gate_done, 1), (slots_done, 1), (slots_used, 1), (stored, 32)):
                    act.sem_inc(counted, by)

            def round_s(c):
                act.wait_ge(s_done, c + 1)
                act.activation(sh[:, c * CT:(c + 1) * CT, :], s_row[:, c * CT:(c + 1) * CT, :],
                               ACT.Copy).then_inc(sh_done, 1)

            def evict(p, m):
                act.wait_ge(mm_done, p * NT)
                if m >= 2:
                    act.wait_ge(tr_done, p - 1)
                w = width(m - 1)
                for d in range(KD):
                    last = act.activation(out_t[:, d, 0:w], acc[(m - 1) % 2][d][:, 0:w], ACT.Copy)
                last.then_inc(evicted, 1)

            def scale(p, m):
                n, _ = rows(p, m)
                act.wait_ge(add_done, p)
                act.wait_ge(dscale_done, p)
                if m >= 2:
                    act.wait_ge(x_done, p - 1)
                for t in range(n):
                    last = act.activation(delta[:, t, :], plus_s[:, t, :], ACT.Relu if relu else ACT.Copy,
                                          scale=dscale[:, t:t + 1])
                last.then_inc(act_done, 1)

            def normalise(p, m):
                n, _ = rows(p, m)
                first = (p - 1) * PT
                act.wait_ge(shift_done, p)
                if route and m >= 2:
                    act.wait_ge(stored, (p - 1) * 32)
                    act.wait_ge(hback, p - 1)
                for t in range(n):
                    tile = slice(first + t, first + t + 1) if isinstance(p, int) else bass.ds(first + t, 1)
                    to = hn[:, (m - 1) % 2, t:t + 1, :] if route else hn[:, tile, :]
                    last = act.activation(to, g.x[:, tile, :], ACT.Identity, scale=rstd[:, t:t + 1],
                                          bias=shift[:, t:t + 1])
                last.then_inc(hn_done, 1)

            def copy_turned(p, m):
                n = routed(m)
                act.wait_ge(hback, p)
                act.wait_ge(gate_done, p - 1)
                act.activation(hT[:, 0:n, :], psT[:, 0:n, D:2 * D], ACT.Copy).then_inc(hT_done, 1)

            def exponent(p, m):
                n = routed(m)
                act.wait_ge(exp_in, p - 1)
                act.activation(ex[:, 0:n], diff[:, 0:n], ACT.Exp).then_inc(exp_out, 1)

            def panel(p, m):
                if m == 0:
                    round_s(0)
                for c in range(CHUNKS):
                    w = width(m)
                    act.wait_ge(chunk_loaded[c], p * 16 + 16)
                    for q in range(CT):
                        j = c * CT + q
                        if m * NT + j >= SPLITS:
                            act.wait_ge(mm_done, p * NT + (j + 1 - SPLITS))
                        act.activation(hi[:, split_slot(m, j), 0:w], raw[:, c, q * w:(q + 1) * w],
                                       ACT.Copy).then_inc(hi_done, 1)
                    if m == 0 and c + 1 < CHUNKS:
                        round_s(c + 1)
                    if m >= 1 and c == 1:
                        evict(p, m)
                    if m >= 1 and c == 7:
                        scale(p, m)
                    if route and m >= 2 and c == 2:
                        copy_turned(p, m)
                    if route and m >= 2 and c == 9:
                        exponent(p, m)
                    if m >= 1 and c == CHUNKS - 1:
                        normalise(p, m)

            def finish(p, m):
                if m == PANELS + 1:
                    evict(p, m)
                if route:
                    copy_turned(p, m)
                if m == PANELS + 1:
                    scale(p, m)
                    normalise(p, m)
                if route:
                    exponent(p, m)

            run(act, panel, finish)

        @block.vector
        def _(dve):
            def scale_s(c):
                for t in range(c * CT, (c + 1) * CT):
                    if column_scale is None:
                        last = dve.tensor_scalar(s_row[:, t, :], s_row[:, t, :], dinv[:, t:t + 1], None, ALU.mult)
                    else:
                        last = dve.scalar_tensor_tensor(out=s_row[:, t, :], in0=s_row[:, t, :], scalar=dinv[:, t:t + 1],
                                                        in1=column_scale[:], op0=ALU.mult, op1=ALU.mult)
                last.then_inc(s_done, 1)

            def rest_of_s(c):
                tiles = slice(c * CT, (c + 1) * CT)
                dve.wait_ge(sh_done, c + 1)
                dve.tensor_tensor(sl[:, tiles, :], s_row[:, tiles, :], sh[:, tiles, :].bitcast(F32),
                                  ALU.subtract).then_inc(sl_done, 1)

            def add_s(p, m):
                n, tiles = rows(p, m)
                if m >= 2:
                    dve.wait_ge(act_done, p - 1)
                dve.tensor_copy(dscale[:, 0:n], dinv[:, tiles]).then_inc(dscale_done, 1)
                dve.wait_ge(tr_done, p)
                if m == 1:
                    dve.wait_ge(s_done, CHUNKS)
                dve.tensor_tensor(plus_s[:, 0:n, :], psT[:, 0:n, 0:D], s_row[:, tiles, :], ALU.add).then_inc(add_done, 1)

            def add_to_x(p, m):
                n, tiles = rows(p, m)
                dve.wait_ge(act_done, p)
                dve.tensor_tensor(g.x[:, tiles, :], g.x[:, tiles, :], delta[:, 0:n, :], ALU.add).then_inc(x_done, 1)

            def statistics(p, m):
                n, tiles = rows(p, m)
                first = (p - 1) * PT
                if m >= 2:
                    dve.wait_ge(aggr_done, p - 1)
                wait_apart(dve, x_done, p, passed)
                for t in range(n):
                    x = g.x[:, first + t, :] if isinstance(p, int) else g.x[:, bass.ds(first + t, 1), :]
                    last = dve.bn_stats(stats[:, t, :], x)
                last.then_inc(st_done, 1)

            def aggregate(p, m):
                n, _ = rows(p, m)
                if m >= 2:
                    dve.wait_ge(shift_done, p - 1)
                wait_apart(dve, st_done, p, passed)
                for t in range(n):
                    last = dve.bn_aggr(mv[:, t, :], stats[:, t, :])
                last.then_inc(aggr_done, 1)

            def chain_from(p, k):
                c = Chain(dve, dchain, passed)
                c.n = (p - 2) * LINKS + k
                return c

            def best_scores(p, m, k):
                n = routed(m)
                bc = [P, n, E]
                chain = chain_from(p, k * 6)
                s = (sc, sc2)[k]
                if k == 0:
                    wait_apart(dve, gate_done, p, passed)
                    chain(dve.tensor_copy(sc[:, 0:n, :], psR[:, 0, 0:n * E].rearrange("p (t e) -> p t e", e=E)))
                else:
                    chain(dve.scalar_tensor_tensor(out=sc2[:, 0:n, :], in0=hot[0][:, 0:n, :], scalar=-3.0e38,
                                                   in1=sc[:, 0:n, :], op0=ALU.mult, op1=ALU.add))
                chain(dve.tensor_reduce(best[k][:, 0:n], s[:, 0:n, :], AX.X, ALU.max))
                chain(dve.tensor_tensor(work[0][:, 0:n, :], s[:, 0:n, :],
                                        best[k][:, 0:n].unsqueeze(2).broadcast_to(bc), ALU.is_equal))

            def best_expert(p, m, k):
                n = routed(m)
                bc = [P, n, E]
                chain = chain_from(p, k * 6 + 3)
                revb = route.rev[:].unsqueeze(1).broadcast_to(bc)
                chain(dve.tensor_tensor(work[1][:, 0:n, :], work[0][:, 0:n, :], revb, ALU.mult))
                chain(dve.tensor_reduce(first_one[k][:, 0:n], work[1][:, 0:n, :], AX.X, ALU.max))
                chain(dve.tensor_tensor(hot[k][:, 0:n, :], revb,
                                        first_one[k][:, 0:n].unsqueeze(2).broadcast_to(bc), ALU.is_equal))

            def choose(p, m):
                n = routed(m)
                dve.tensor_tensor(diff[:, 0:n], best[1][:, 0:n], best[0][:, 0:n], ALU.subtract).then_inc(exp_in, 1)
                last = dve.tensor_tensor(chosen[:, 0:n, :], hot[0][:, 0:n, :], hot[1][:, 0:n, :], ALU.add)
                if m == PANELS + 2:
                    chain_from(p, 12)(last)
                    last = dve.tensor_scalar(chosen[:, n - 1, :], chosen[:, n - 1, :], g.valid[:, 0:1], None, ALU.mult)
                last.then_inc(chosen_done, 1)

            def count(p, m):
                n = routed(m)
                chain = chain_from(p, 12 + (m == PANELS + 2))
                free = route.free
                wait_apart(dve, rank_done, p - 1, passed)
                chain(dve.tensor_copy(free[:, 0, :], free[:, PT, :]))
                for t in range(n):
                    chain(dve.tensor_tensor(free[:, t + 1, :], free[:, t, :], psR[:, 2, t * E:(t + 1) * E], ALU.add))

            def weigh(p, m):
                n = routed(m)
                first = (p - 2) * PT
                tiles = slice(first, first + n) if isinstance(p, int) else bass.ds(first, n)
                chain = chain_from(p, 13 + n + (m == PANELS + 2))
                wait_apart(dve, exp_out, p - 1, passed)
                chain(dve.tensor_scalar(ex1[:, 0:n], ex[:, 0:n], 1.0, None, ALU.add))
                chain(dve.reciprocal(prob[0][:, 0:n], ex1[:, 0:n]))
                chain(dve.tensor_tensor(prob[1][:, 0:n], ex[:, 0:n], prob[0][:, 0:n], ALU.mult))
                wait_apart(dve, slots_used, p - 1, passed)
                for k in range(2):
                    dve.tensor_copy(meta[:, k, 0:n, 0], route.token[:, tiles])
                    dve.tensor_copy(meta[:, k, 0:n, 1].bitcast(F32), prob[k][:, 0:n])

            def give_slots(p, m):
                n = routed(m)
                chain = chain_from(p, 16 + n + (m == PANELS + 2))
                chain(dve.tensor_tensor(pos[:, 0:n, :], route.free[:, 0:n, :],
                                        psR[:, 1, 0:n * E].rearrange("p (t e) -> p t e", e=E), ALU.add))
                for k in range(2):
                    last = dve.tensor_tensor(work[k][:, 0:n, :], hot[k][:, 0:n, :], pos[:, 0:n, :], ALU.mult)
                    last.then_inc(dchain, 1)
                chain.n = chain.n + 2
                wait_apart(dve, dchain, chain.n, passed)
                for k in range(2):
                    last = dve.tensor_reduce(slot_f[k][:, 0:n], work[k][:, 0:n, :], AX.X, ALU.add)
                    last.then_inc(dchain, 1)
                chain.n = chain.n + 2
                wait_apart(dve, dchain, chain.n, passed)
                for k in range(2):
                    last = dve.tensor_copy(slot[k][:, 0:n], slot_f[k][:, 0:n])
                last.then_inc(slots_done, 1)

            def schedule():
                chain = chain_from(PANELS + 2, LINKS + 1 + LT - PT)
                count = sb("rt_count", [P, E])
                cmp = sb("rt_cmp", [P, E, KMAX])
                ntl = sb("rt_ntl", [P, E])
                cum = sb("rt_cum", [P, E])
                tb = [P, TILES + 1, E]
                le = sb("rt_le", tb)
                le2 = sb("rt_le2", tb)
                eidx = sb("rt_eidx", [P, TILES + 1])
                first_t = sb("rt_first_t", [P, TILES + 1])
                rowf = [sb(f"rt_rowf{k}", [P, TILES + 1]) for k in range(4)]
                chain(dve.tensor_tensor(count[:], route.free[:, LT, :], route.reg[:], ALU.subtract))
                bc = [P, E, KMAX]
                chain(dve.tensor_tensor(cmp[:], count[:].unsqueeze(2).broadcast_to(bc),
                                        route.kf[:].unsqueeze(1).broadcast_to(bc), ALU.is_gt))
                chain(dve.tensor_reduce(ntl[:], cmp[:], AX.X, ALU.add))
                chain(dve.tensor_tensor_scan(cum[:], g.ones[:, 0:E], ntl[:], 0.0, ALU.mult, ALU.add))
                chain(dve.tensor_tensor(le[:], cum[:].unsqueeze(1).broadcast_to(tb),
                                        route.tf[:].unsqueeze(2).broadcast_to(tb), ALU.is_le))
                dve.tensor_reduce(eidx[:], le[:], AX.X, ALU.add)
                chain(dve.tensor_tensor(le2[:], le[:], ntl[:].unsqueeze(1).broadcast_to(tb), ALU.mult))
                chain(dve.tensor_reduce(first_t[:], le2[:], AX.X, ALU.add))
                chain(dve.tensor_tensor(rowf[0][:], route.tf[:], first_t[:], ALU.subtract))
                chain(dve.tensor_scalar(rowf[1][:], rowf[0][:], float(TW), None, ALU.mult))
                dve.tensor_scalar(rowf[3][:], eidx[:], float(E - 1), None, ALU.min)
                chain(dve.scalar_tensor_tensor(out=rowf[2][:], in0=eidx[:], scalar=float(REG), in1=rowf[1][:],
                                               op0=ALU.mult, op1=ALU.add))
                dve.tensor_copy(route.sched[:, 0, :], rowf[2][0:1, :])
                dve.tensor_copy(route.sched[:, 1, :], rowf[3][0:1, :])

            def panel(p, m):
                if m == 0:
                    scale_s(0)
                    scale_s(1)
                    rest_of_s(0)
                for c in range(CHUNKS):
                    w = width(m)
                    for q in range(CT):
                        j = c * CT + q
                        b = split_slot(m, j)
                        dve.wait_ge(hi_done, p * NT + (j + 1))
                        dve.tensor_tensor(lo[:, b, 0:w], raw[:, c, q * w:(q + 1) * w], hi[:, b, 0:w].bitcast(F32),
                                          ALU.subtract).then_inc(lo_done, 1)
                    if m == 0 and c + 2 < CHUNKS:
                        scale_s(c + 2)
                    if m == 0 and c + 1 < CHUNKS:
                        rest_of_s(c + 1)
                    if m >= 1:
                        stage = {5: add_s, 9: add_to_x, 10: statistics, 11: aggregate}.get(c)
                        if stage:
                            stage(p, m)
                    if route and m >= 2:
                        if c in (5, 7):
                            best_scores(p, m, (c - 5) // 2)
                        if c in (6, 8):
                            best_expert(p, m, (c - 6) // 2)
                        stage = {8: choose, 10: count, 11: weigh, 12: give_slots}.get(c)
                        if stage:
                            stage(p, m)

            def finish(p, m):
                if m == PANELS + 1:
                    add_s(p, m)
                    add_to_x(p, m)
                    statistics(p, m)
                    aggregate(p, m)
                if route:
                    for k in range(2):
                        best_scores(p, m, k)
                        best_expert(p, m, k)
                    choose(p, m)
                    count(p, m)
                    weigh(p, m)
                    give_slots(p, m)
                if m == PANELS + 2:
                    schedule()

            run(dve, panel, finish)

        @block.gpsimd
        def _(pool):
            def scale_and_shift(p, m):
                n, _ = rows(p, m)
                wait_apart(pool, aggr_done, p, passed)
                pool.tensor_scalar(veps[:, 0:n], mv[:, 0:n, 1], 1.0, LN_EPS, ALU.mult, ALU.add).then_inc(eps_done, 1)
                if m >= 2:
                    pool.wait_ge(hn_done, p - 1)
                pool.wait_ge(eps_done, p)
                pool.tensor_tensor(rstd[:, 0:n], veps[:, 0:n], g.mhalf[:, 0:n], ALU.pow).then_inc(rstd_done, 1)
                pool.wait_ge(rstd_done, p)
                pool.tensor_tensor(mr[:, 0:n], mv[:, 0:n, 0], rstd[:, 0:n], ALU.mult).then_inc(mr_done, 1)
                wait_apart(pool, mr_done, p, passed)
                pool.tensor_scalar(shift[:, 0:n], mr[:, 0:n], -1.0, 0.0, ALU.mult, ALU.add).then_inc(shift_done, 1)

            def scatter(p, m):
                n = routed(m)
                wait_apart(pool, slots_done, p, passed)
                for t in range(n):
                    rows_ = LAST if m == PANELS + 2 and t == n - 1 else P
                    for k in range(2):
                        pool.indirect_dma_start(route.table,
                                                bass.IndirectOffsetOnAxis(ap=slot[k][0:rows_, t:t + 1], axis=0),
                                                meta[0:rows_, k, t, :], None).then_inc(scattered, 16)
                if m < PANELS + 2:
                    pool.wait_ge(scattered, (p - 1) * (2 * PT * 16))
                    pool.sem_inc(slots_used, 1)

            def panel(p, m):
                if 1 <= m <= PANELS + 1:
                    scale_and_shift(p, m)
                if route and m >= 2:
                    scatter(p, m)
                if route and m == PANELS + 2:
                    pool.wait_ge(scattered, 2 * NT * 16)

            run(pool, panel, panel)

        @block.tensor
        def _(pe):
            def turn_back(p, m):
                n, _ = rows(p, m)
                pe.wait_ge(evicted, p)
                if m >= 2:
                    pe.wait_ge(add_done, p - 1)
                    if route:
                        pe.wait_ge(hT_done, p - 1)
                for t in range(n):
                    for d in range(KD):
                        last = pe.transpose(psT[:, t, d * P:(d + 1) * P], out_t[:, d, t * P:(t + 1) * P], g.ident[:])
                last.then_inc(tr_done, 1)

            def turn_normed(p, m):
                pe.wait_ge(hn_done, p - 1)
                pe.wait_ge(add_done, p - 1)
                for t in range(routed(m)):
                    for k in range(KD):
                        last = pe.transpose(psT[:, t, D + k * P:D + (k + 1) * P], hn[:, m % 2, t, k * P:(k + 1) * P],
                                            g.ident[:])
                last.then_inc(hback, 1)

            def gate(p, m):
                pe.wait_ge(hT_done, p - 1)
                pe.wait_ge(slots_done, p - 1)
                for t in range(routed(m)):
                    to = psR[:, 0, t * E:(t + 1) * E]
                    for k in range(KD):
                        pe.matmul(to, hT[:, t, k * P:(k + 1) * P], route.wg_sb[:, k, :], start=(k == 0), stop=False)
                    last = pe.matmul(to, g.ones[0:1, :], route.bg_sb[0:1, :], start=False, stop=True)
                last.then_inc(gate_done, 1)

            def rank(p, m):
                n = routed(m)
                flat = chosen[:, 0:n, :].rearrange("p t e -> p (t e)")
                pe.wait_ge(chosen_done, p - 1)
                pe.matmul(psR[:, 1, 0:n * E], g.before[:], flat, start=True, stop=True)
                pe.matmul(psR[:, 2, 0:n * E], g.ones[:], flat, start=True, stop=True).then_inc(rank_done, 1)

            def finish(p, m):
                if m == PANELS + 1:
                    if route:
                        turn_normed(p, m)
                    turn_back(p, m)
                elif route:
                    turn_normed(p, m)
                if route:
                    gate(p, m)
                    rank(p, m)

            def panel(p, m):
                w = width(m)
                for c in range(CHUNKS):
                    if m >= 2 and c == 0:
                        pe.wait_ge(evicted, p - 1)
                    if m == 0:
                        pe.wait_ge(sl_done, c + 1)
                    for j in range(c * CT, (c + 1) * CT):
                        pe.wait_ge(lo_done, p * NT + (j + 1))
                        b = split_slot(m, j)
                        for d in range(KD):
                            fs = slice(d * P, (d + 1) * P)
                            for k, (s, a) in enumerate(((sh, hi), (sh, lo), (sl, hi))):
                                last = pe.matmul(acc[m % 2][d][:, 0:w], s[:, j, fs], a[:, b, 0:w],
                                                 start=(j == 0 and k == 0), stop=(j == NT - 1 and k == 2))
                        last.then_inc(mm_done, 1)
                    if route and m >= 2 and c == 0:
                        turn_normed(p, m)
                    if m >= 1 and c == 3:
                        turn_back(p, m)
                    if route and m >= 2 and c == 3:
                        gate(p, m)
                    if route and m >= 2 and c == 8:
                        rank(p, m)

            run(pe, panel, finish)


def experts_block(nc, g, wall, b1, b2, xn_rows, x_rows, table, sched):
    with ExitStack() as ctx:
        sb, ps = tensors(nc, ctx)
        sem = semaphores(nc, ctx, "moe")
        HALF = TW // P
        W1 = KD * H
        WA = 2 * W1
        CHW = 512
        NCH = WA // CHW
        FIRST = W1 // CHW
        POOL_CH = (FIRST - 1, NCH - 1)
        wraw = sb("moe_wraw", [P, 2, WA])
        wh = sb("moe_wh", [P, 2, WA], F32R)
        wl = sb("moe_wl", [P, 2, WA], F32R)
        b1s = sb("moe_b1", [P, 2, HB])
        b2s = sb("moe_b2", [P, 2, D])
        meta = sb("moe_meta", [P, 2, HALF, 2], U32)
        meta2 = sb("moe_meta2", [P, 2, HALF, 2], U32)
        xg = sb("moe_xg", [P, 2, HALF, D])
        xh = sb("moe_xh", [P, KD, TW], F32R)
        xl = sb("moe_xl", [P, KD, TW], F32R)
        hr = sb("moe_hr", [P, HB, TW])
        hh = sb("moe_hh", [P, HB, TW], F32R)
        hl = sb("moe_hl", [P, HB, TW], F32R)
        zero = sb("moe_zero", [(ROWS - NPAD) // 4, D])
        yb = sb("moe_yb", [P, 2, HALF, D])
        y = sb("moe_y", [P, 2, HALF, D])
        psX = ps("moe_psX", [P, KD, TW])
        psH = [ps(f"moe_psH{k}", [P, 2, TW]) for k in range(HB // 2)]
        psY = [ps(f"moe_psY{k}", [P, HALF, D]) for k in range(2)]

        w_loaded = [[sem(f"w{k}_loaded{b}") for b in range(2)] for k in range(2)]
        small_loaded = [sem(f"small_loaded{k}") for k in range(2)]
        meta_loaded = [sem(f"meta_loaded{k}") for k in range(2)]
        gathered = [sem(f"gathered{k}") for k in range(2)]
        wh_done = sem("wh_done")
        wl_done = sem("wl_done")
        wlp_done = sem("wlp_done")
        turned = sem("turned")
        xh_done, xl_done = sem("xh_done"), sem("xl_done")
        l1_done = sem("l1_done")
        relu_done = sem("relu_done")
        hh_done = sem("hh_done")
        hl_done = sem("hl_done")
        l2_done = sem("l2_done")
        yb_done = sem("yb_done")
        y_done = sem("y_done")
        copied = sem("copied")
        added = [sem(f"added{k}") for k in range(2)]
        zeroed = sem("zeroed")
        issued = sem("issued")
        passed = sem("passed")
        pairs = HB // 2
        DCH = NCH - len(POOL_CH)

        block = ctx.enter_context(nc.Block())

        def load_weights(sp, t, b, which=range(2)):
            e = sp.value_load(sched[0:1, 1, bass.ds(t, 1)] if not isinstance(t, int) else sched[0:1, 1, t:t + 1],
                              min_val=0, max_val=E - 1)
            for k in which:
                sp.dma_start(wraw[:, b, k * W1:(k + 1) * W1],
                             wall[bass.ds(e * P, P), k * W1:(k + 1) * W1]).then_inc(w_loaded[k][b], 16)

        def load_small(sp, t, b):
            e = sp.value_load(sched[0:1, 1, bass.ds(t, 1)] if not isinstance(t, int) else sched[0:1, 1, t:t + 1],
                              min_val=0, max_val=E - 1)
            sp.dma_start(b1s[:, b, :], b1[bass.ds(e * P, P), :]).then_inc(small_loaded[b], 16)
            sp.dma_start(b2s[:, b, :], b2[bass.ds(e, 1), :].broadcast_to([P, D])).then_inc(small_loaded[b], 16)

        def load_meta(sp, t, b):
            r = sp.value_load(sched[0:1, 0, bass.ds(t, 1)] if not isinstance(t, int) else sched[0:1, 0, t:t + 1],
                              min_val=0, max_val=SLOTS - TW)
            sp.dma_start(meta[:, b, :, :], table[bass.ds(r, TW), :].rearrange("(p h) c -> p h c", h=HALF)
                         ).then_inc(meta_loaded[b], 16)

        @block.sync
        def _(sp):
            for t in range(2):
                load_meta(sp, t, t)
            for t in range(2):
                load_small(sp, t, t)
                load_weights(sp, t, t)

            def ahead(t, b, weights=True, small=True, metas=True):
                o = 1 - b
                if metas:
                    sp.wait_ge(issued, t + 2)
                    wait_apart(sp, copied, t + 2, passed)
                    load_meta(sp, t + 3, o)
                if weights:
                    wait_apart(sp, wl_done, t * DCH + DCH + FIRST - 1, passed)
                    wait_apart(sp, wlp_done, t * len(POOL_CH) + len(POOL_CH) + 1, passed)
                    load_weights(sp, t + 3, o, [0])
                if small:
                    sp.wait_ge(relu_done, t * HB + 2 * HB)
                    wait_apart(sp, yb_done, t + 3, passed)
                    load_small(sp, t + 2, b)
                if weights:
                    wait_apart(sp, wl_done, t * DCH + 2 * DCH, passed)
                    wait_apart(sp, wlp_done, t * len(POOL_CH) + 2 * len(POOL_CH), passed)
                    load_weights(sp, t + 3, o, [1])

            ahead(-1, 1, small=False)
            with sp.Fori(0, (TILES - 3) // 2) as i:
                for b in range(2):
                    ahead(i * 2 + b, b)
            t = TILES - 3
            ahead(t, t % 2, weights=False)

        @block.gpsimd
        def _(pool):
            quarter = (ROWS - NPAD) // 4
            pool.memset(zero[:], 0.0).then_inc(zeroed, 1)
            pool.wait_ge(zeroed, 1)
            for k in range(4):
                pool.dma_start(x_rows[NPAD + k * quarter:NPAD + (k + 1) * quarter, :], zero[:]).then_inc(added[k % 2], 16)

            def gather(t, b, use):
                wait_apart(pool, meta_loaded[b], use * 16 + 16, passed)
                for h in range(HALF):
                    pool.indirect_dma_start(xg[:, b, h, :], None, xn_rows,
                                            bass.IndirectOffsetOnAxis(ap=meta[:, b, h, 0:1], axis=0)
                                            ).then_inc(gathered[b], 16)

            def split_low(c, b):
                cols = slice(c * CHW, (c + 1) * CHW)
                return pool.tensor_tensor(wl[:, b, cols], wraw[:, b, cols], wh[:, b, cols].bitcast(F32), ALU.subtract)

            gather(0, 0, 0)
            gather(1, 1, 0)
            pool.wait_ge(gathered[0], 32)
            pool.sem_inc(issued, 1)
            pool.wait_ge(wh_done, FIRST)
            split_low(POOL_CH[0], 0).then_inc(wlp_done, 1)

            def step(t, i, b, ahead=True):
                o = 1 - b
                pool.wait_ge(wh_done, t * NCH + NCH)
                split_low(POOL_CH[1], b).then_inc(wlp_done, 1)
                if ahead:
                    pool.wait_ge(turned, t + 1)
                    gather(t + 2, b, i + 1)
                    pool.wait_ge(gathered[o], i * 32 + (32 if b == 0 else 64))
                    pool.sem_inc(issued, 1)
                if ahead:
                    pool.wait_ge(wh_done, t * NCH + NCH + FIRST)
                    split_low(POOL_CH[0], o).then_inc(wlp_done, 1)
                wait_apart(pool, yb_done, t + 3, passed)
                wait_apart(pool, added[b], i * 32 + 32, passed)
                for h in range(HALF):
                    last = pool.tensor_scalar(y[:, b, h, :], yb[:, b, h, :], meta2[:, b, h, 1:2].bitcast(F32), 0.0,
                                              ALU.mult, ALU.add)
                last.then_inc(y_done, 1)
                pool.wait_ge(y_done, t + 3)
                wait_apart(pool, added[o], i * 32 + (32 if b == 0 else 64), passed)
                for h in range(HALF):
                    pool.indirect_dma_start(x_rows, bass.IndirectOffsetOnAxis(ap=meta2[:, b, h, 0:1], axis=0),
                                            y[:, b, h, :], None, compute_op=ALU.add).then_inc(added[b], 16)

            with pool.Fori(0, TILES // 2) as i:
                for b in range(2):
                    step(i * 2 + b, i, b)
            step(TILES - 1, TILES // 2, 0, ahead=False)
            pool.wait_ge(added[0], 32 * (TILES // 2 + 1) + 32)
            pool.wait_ge(added[1], 32 * (TILES // 2) + 32)
            pool.wait_ge(gathered[1], 32 * (TILES // 2 + 1))

        def split_high(act, c, b):
            cols = slice(c * CHW, (c + 1) * CHW)
            act.activation(wh[:, b, cols], wraw[:, b, cols], ACT.Copy).then_inc(wh_done, 1)

        @block.scalar
        def _(act):
            for c in range(NCH):
                if c % FIRST == 0:
                    act.wait_ge(w_loaded[c // FIRST][0], 16)
                split_high(act, c, 0)
            act.wait_ge(turned, 1)
            act.activation(xh[:], psX[:], ACT.Copy).then_inc(xh_done, 1)

            def step(t, i, b, ahead=True):
                o = 1 - b
                for hb in range(HB):
                    if hb == 0:
                        act.wait_ge(small_loaded[b], i * 32 + 32)
                    act.wait_ge(l1_done, t * HB + hb // 2 * 2 + 2)
                    act.wait_ge(hl_done, t * pairs + hb // 2 + 1)
                    act.activation(hr[:, hb, :], psH[hb // 2][:, hb % 2, :], ACT.Relu,
                                   bias=b1s[:, b, hb:hb + 1]).then_inc(relu_done, 1)
                    if ahead and hb % 2 == 1:
                        if hb == 1:
                            act.wait_ge(w_loaded[0][o], i * 16 + (16 if b == 0 else 32))
                            act.wait_ge(l2_done, t + 1)
                        split_high(act, hb // 2, o)
                if ahead:
                    act.wait_ge(turned, t + 2)
                    act.wait_ge(l1_done, t * HB + HB)
                    act.activation(xh[:], psX[:], ACT.Copy).then_inc(xh_done, 1)
                    act.wait_ge(w_loaded[1][o], i * 16 + (16 if b == 0 else 32))
                    for c in range(FIRST, NCH):
                        split_high(act, c, o)

            with act.Fori(0, TILES // 2) as i:
                for b in range(2):
                    step(i * 2 + b, i, b)
            step(TILES - 1, TILES // 2, 0, ahead=False)

        @block.vector
        def _(dve):
            dve.sem_inc(hl_done, pairs)
            dve.sem_inc(yb_done, 2)
            dve.sem_inc(relu_done, HB)
            dve.sem_inc(y_done, 2)

            def split_low(c, b):
                cols = slice(c * CHW, (c + 1) * CHW)
                dve.tensor_tensor(wl[:, b, cols], wraw[:, b, cols], wh[:, b, cols].bitcast(F32),
                                  ALU.subtract).then_inc(wl_done, 1)

            for c in range(FIRST):
                if c not in POOL_CH:
                    dve.wait_ge(wh_done, c + 1)
                    split_low(c, 0)
            dve.wait_ge(xh_done, 1)
            dve.tensor_tensor(xl[:], psX[:], xh[:].bitcast(F32), ALU.subtract).then_inc(xl_done, 1)
            dve.wait_ge(meta_loaded[0], 16)
            dve.tensor_copy(meta2[:, 0], meta[:, 0]).then_inc(copied, 1)

            def step(t, i, b, ahead=True):
                o = 1 - b
                for c in range(FIRST, NCH):
                    if c not in POOL_CH:
                        dve.wait_ge(wh_done, t * NCH + c + 1)
                        split_low(c, b)
                for k in range(pairs):
                    blocks = slice(2 * k, 2 * k + 2)
                    dve.wait_ge(relu_done, t * HB + 2 * k + 2 + HB)
                    if k == 0:
                        dve.wait_ge(l2_done, t + 1)
                    dve.tensor_copy(hh[:, blocks, :], hr[:, blocks, :]).then_inc(hh_done, 1)
                    dve.wait_ge(hh_done, t * pairs + k + 1)
                    dve.tensor_tensor(hl[:, blocks, :], hr[:, blocks, :], hh[:, blocks, :].bitcast(F32),
                                      ALU.subtract).then_inc(hl_done, 1)
                    if ahead and k not in POOL_CH:
                        dve.wait_ge(wh_done, t * NCH + NCH + k + 1)
                        split_low(k, o)
                if ahead:
                    dve.wait_ge(xh_done, t + 2)
                    dve.tensor_tensor(xl[:], psX[:], xh[:].bitcast(F32), ALU.subtract).then_inc(xl_done, 1)
                    dve.wait_ge(meta_loaded[o], i * 16 + (16 if b == 0 else 32))
                    dve.wait_ge(added[o], i * 32 + (32 if b == 0 else 64))
                    dve.tensor_copy(meta2[:, o], meta[:, o]).then_inc(copied, 1)
                dve.wait_ge(l2_done, t + 2)
                dve.wait_ge(small_loaded[b], i * 32 + 32)
                dve.wait_ge(y_done, t + 1)
                dve.tensor_tensor(yb[:, b], psY[b][:], b2s[:, b, :].unsqueeze(1).broadcast_to([P, HALF, D]),
                                  ALU.add).then_inc(yb_done, 1)

            with dve.Fori(0, TILES // 2) as i:
                for b in range(2):
                    step(i * 2 + b, i, b)
            step(TILES - 1, TILES // 2, 0, ahead=False)

        @block.tensor
        def _(pe):
            pe.sem_inc(l2_done, 1)

            def turn(b):
                for h in range(HALF):
                    for k in range(KD):
                        last = pe.transpose(psX[:, k, h * P:(h + 1) * P], xg[:, b, h, k * P:(k + 1) * P], g.ident[:])
                last.then_inc(turned, 1)

            pe.wait_ge(gathered[0], 32)
            turn(0)

            def step(t, i, b, ahead=True):
                o = 1 - b
                pe.wait_ge(xl_done, t + 1)
                pe.wait_ge(wl_done, t * DCH + FIRST - 1)
                pe.wait_ge(wlp_done, t * len(POOL_CH) + 1)
                for hb in range(HB):
                    if hb % 2 == 0:
                        pe.wait_ge(relu_done, t * HB + hb + 2)
                    n = 0
                    for k in range(KD):
                        cols = slice(k * H + hb * P, k * H + (hb + 1) * P)
                        for w, x in ((wh, xh), (wh, xl), (wl, xh)):
                            last = pe.matmul(psH[hb // 2][:, hb % 2, :], w[:, b, cols], x[:, k, :],
                                             start=(n == 0), stop=(n == 3 * KD - 1))
                            n += 1
                    last.then_inc(l1_done, 1)
                if ahead:
                    pe.wait_ge(gathered[o], i * 32 + (32 if b == 0 else 64))
                    turn(o)
                pe.wait_ge(yb_done, t + 1)
                pe.wait_ge(wl_done, t * DCH + DCH)
                pe.wait_ge(wlp_done, t * len(POOL_CH) + 2)
                for hb in range(HB):
                    if hb % 2 == 0:
                        pe.wait_ge(hl_done, t * pairs + hb // 2 + 1 + pairs)
                    for h in range(HALF):
                        rows = slice(h * P, (h + 1) * P)
                        w2 = slice(W1 + hb * D, W1 + (hb + 1) * D)
                        for m, (hx, w) in enumerate(((hh, wh), (hh, wl), (hl, wh))):
                            last = pe.matmul(psY[b][:, h, :], hx[:, hb, rows], w[:, b, w2],
                                             start=(hb == 0 and h == 0 and m == 0), stop=(hb == HB - 1 and m == 2),
                                             skip_group_check=True)
                last.then_inc(l2_done, 1)

            with pe.Fori(0, TILES // 2) as i:
                for b in range(2):
                    step(i * 2 + b, i, b)
            step(TILES - 1, TILES // 2, 0, ahead=False)


def standardise_block(nc, g, x_rows, w1, b1, sp_, rb):
    with ExitStack() as ctx:
        sb, ps = tensors(nc, ctx)
        sem = semaphores(nc, ctx, "std")
        w = sb("std_w", [P, KD, D])
        b = sb("std_b", [1, D])
        stats = sb("std_stats", [P, NT, 6])
        mv = sb("std_mv", [P, NT, 2])
        veps = sb("std_veps", [P, NT])
        rstd = sb("std_rstd", [P, NT])
        shift = sb("std_shift", [P, NT])
        negshift = sb("std_negshift", [P, NT])
        xn = sb("std_xn", [P, 2, D])
        xnT = sb("std_xnT", [P, 2, KD, P])
        sq = sb("std_sq", [P, 2, D])
        mean = sb("std_mean", [P, D])
        var = sb("std_var", [P, KD])
        half = sb("std_half", [P, KD])
        std = sb("std_std", [P, KD])
        stde = sb("std_stde", [P, KD])
        rinv = sb("std_rinv", [P, KD])
        diag = sb("std_diag", [P, KD, P])
        psT = [ps(f"std_psT{k}", [P, KD, P]) for k in range(2)]
        psZ = [ps(f"std_psZ{k}", [P, D]) for k in range(2)]
        psM = ps("std_psM", [P, D])
        psV = [ps(f"std_psV{k}", [P, 1]) for k in range(KD)]
        psB = psM

        x_loaded = [sem(f"x_loaded{k}") for k in range(2)]
        w_loaded = sem("w_loaded")
        dchain, stats_done, pchain, norm_done = sem("dchain"), sem("stats"), sem("pchain"), sem("norm")
        xn_done, tr_done, xnT_done, mm_done, z_done = (sem(n) for n in ("xn", "tr", "xnT", "mm", "z"))
        sum_done, mean_done, zc_done, sq_done, var_mm = (sem(n) for n in ("sum", "mean", "zc", "sq", "varmm"))
        var_done, root_done, diag_done, bc_done = (sem(n) for n in ("var", "root", "diag", "bc"))
        block = ctx.enter_context(nc.Block())
        FIRST = NT // 2

        @block.sync
        def _(sp):
            rows = x_rows[0:NPAD, :].rearrange("(t p) d -> p t d", p=P)
            sp.dma_start(g.x[:, 0:FIRST, :], rows[:, 0:FIRST, :]).then_inc(x_loaded[0], 16)
            sp.dma_start(g.x[:, FIRST:NT, :], rows[:, FIRST:NT, :]).then_inc(x_loaded[1], 16)
            sp.dma_start(w[:], w1.rearrange("(k p) n -> p k n", p=P)).then_inc(w_loaded, 16)
            sp.dma_start(b[:], b1).then_inc(w_loaded, 16)

        @block.vector
        def _(dve):
            chain = Chain(dve, dchain)
            for t in range(NT):
                if t in (0, FIRST):
                    dve.wait_ge(x_loaded[t // FIRST], 16)
                dve.bn_stats(stats[:, t, :], g.x[:, t, :]).then_inc(dchain, 1)
            chain.n = NT
            dve.wait_ge(dchain, NT)
            for t in range(NT):
                last = dve.bn_aggr(mv[:, t, :], stats[:, t, :])
            chain(last)
            dve.tensor_scalar(veps[:], mv[:, :, 1], LN_EPS, None, ALU.add).then_inc(stats_done, 1)
            dve.memset(half[:], 0.5)
            dve.wait_ge(sum_done, 1)
            dve.tensor_scalar(mean[:], psM[:], 1.0 / N, None, ALU.mult).then_inc(mean_done, 1)
            dve.wait_ge(mean_done, 1)
            for t in range(NT):
                dve.tensor_tensor(sp_[:, t, :], sp_[:, t, :], mean[:], ALU.subtract).then_inc(zc_done, 1)
            dve.wait_ge(var_mm, NT)
            for k in range(KD):
                last = dve.tensor_scalar(var[:, k:k + 1], psV[k][:], 1.0 / (N - 1), None, ALU.mult)
            last.then_inc(var_done, 1)
            dve.wait_ge(root_done, 1)
            chain(dve.tensor_scalar(stde[:], std[:], 1e-6, None, ALU.add))
            chain(dve.reciprocal(rinv[:], stde[:]))
            for k in range(KD):
                last = dve.tensor_scalar(diag[:, k, :], g.ident[:], rinv[:, k:k + 1], None, ALU.mult)
            last.then_inc(diag_done, 1)
            dve.wait_ge(bc_done, 1)
            dve.tensor_copy(rb[:], psB[:])

        @block.gpsimd
        def _(pool):
            chain = Chain(pool, pchain)
            pool.wait_ge(stats_done, 1)
            chain(pool.tensor_tensor(rstd[:], veps[:], g.mhalf[:, 0:NT], ALU.pow))
            chain(pool.tensor_tensor(shift[:], mv[:, :, 0], rstd[:], ALU.mult))
            pool.tensor_scalar(negshift[:], shift[:], -1.0, 0.0, ALU.mult, ALU.add).then_inc(norm_done, 1)
            pool.wait_ge(var_done, 1)
            pool.tensor_tensor(std[:], var[:], half[:], ALU.pow).then_inc(root_done, 1)

        @block.scalar
        def _(act):
            act.wait_ge(norm_done, 1)
            for t in range(NT + 1):
                if t < NT:
                    if t >= 2:
                        act.wait_ge(tr_done, t - 1)
                    act.activation(xn[:, t % 2, :], g.x[:, t, :], ACT.Identity, bias=negshift[:, t:t + 1],
                                   scale=rstd[:, t:t + 1]).then_inc(xn_done, 1)
                    act.wait_ge(tr_done, t + 1)
                    if t >= 2:
                        act.wait_ge(mm_done, t - 1)
                    act.activation(xnT[:, t % 2], psT[t % 2][:], ACT.Copy).then_inc(xnT_done, 1)
                if t >= 1:
                    act.wait_ge(mm_done, t)
                    act.activation(sp_[:, t - 1, :], psZ[(t - 1) % 2][:], ACT.Copy).then_inc(z_done, 1)
            for t in range(NT):
                act.wait_ge(zc_done, t + 1)
                if t >= 2:
                    act.wait_ge(var_mm, t - 1)
                act.activation(sq[:, t % 2, :], sp_[:, t, :], ACT.Square).then_inc(sq_done, 1)

        def column_sum(pe, t):
            rows = g.valid if t == NT - 1 else g.ones
            pe.wait_ge(z_done, t + 1)
            return pe.matmul(psM[:], rows[:], sp_[:, t, :], start=(t == 0), stop=(t == NT - 1))

        @block.tensor
        def _(pe):
            pe.wait_ge(w_loaded, 32)
            for t in range(NT):
                pe.wait_ge(xn_done, t + 1)
                if t >= 2:
                    pe.wait_ge(xnT_done, t - 1)
                for k in range(KD):
                    last = pe.transpose(psT[t % 2][:, k, :], xn[:, t % 2, k * P:(k + 1) * P], g.ident[:])
                last.then_inc(tr_done, 1)
                if t >= 1:
                    last = column_sum(pe, t - 1)
                pe.wait_ge(xnT_done, t + 1)
                if t >= 2:
                    pe.wait_ge(z_done, t - 1)
                for k in range(KD):
                    pe.matmul(psZ[t % 2][:], xnT[:, t % 2, k, :], w[:, k, :], start=(k == 0), stop=False)
                pe.matmul(psZ[t % 2][:], g.ones[0:1, :], b[0:1, :], start=False, stop=True).then_inc(mm_done, 1)
            column_sum(pe, NT - 1).then_inc(sum_done, 1)
            for t in range(NT):
                rows = g.valid if t == NT - 1 else g.ones
                pe.wait_ge(sq_done, t + 1)
                for k in range(KD):
                    last = pe.matmul(psV[k][:], sq[:, t % 2, k * P:(k + 1) * P], rows[:, 0:1],
                                     start=(t == 0), stop=(t == NT - 1))
                last.then_inc(var_mm, 1)
            pe.wait_ge(diag_done, 1)
            for k in range(KD):
                last = pe.matmul(psB[:, k * P:(k + 1) * P], g.ones[:], diag[:, k, :], start=True, stop=True)
            last.then_inc(bc_done, 1)


def steps_block(nc, g, wt_in, lw_in, lb_in, b_in, h0, out):
    with ExitStack() as ctx:
        sb, ps = tensors(nc, ctx)
        sem = semaphores(nc, ctx, "ffn")
        Q = 2
        G = NT // Q
        W = Q * D
        BODY = 4
        R = 4
        wt = sb("ffn_wt", [P, KD, D])
        lw = sb("ffn_lw", [P, KD])
        lb = sb("ffn_lb", [P, KD])
        bias = sb("ffn_bias", [1, D])
        wlw = sb("ffn_wlw", [P, KD, D])
        lbm = sb("ffn_lbm", [P, KD, P])
        w2 = sb("ffn_w2", [P, KD, D])
        w2h = sb("ffn_w2h", [P, KD, D], F32R)
        w2l = sb("ffn_w2l", [P, KD, D], F32R)
        vT = sb("ffn_vT", [P, 2, Q * KD, P])
        vTh = sb("ffn_vTh", [P, 2, Q * KD, P], F32R)
        vTl = sb("ffn_vTl", [P, 2, Q * KD, P], F32R)
        th = sb("ffn_th", [P, R, W])
        u = sb("ffn_u", [P, R, W])
        stats = sb("ffn_stats", [P, NT, 6])
        mv = sb("ffn_mv", [P, NT, 2])
        veps = sb("ffn_veps", [P, NT])
        rstd = sb("ffn_rstd", [P, NT])
        mr = sb("ffn_mr", [P, NT])
        shift = sb("ffn_shift", [P, NT])
        vn = sb("ffn_vn", [P, NT, D])
        warm = sb("ffn_warm", [P, 1])
        psT = [ps(f"ffn_psT{k}", [P, Q * KD, P]) for k in range(R)]
        psH = [ps(f"ffn_psH{k}", [P, W]) for k in range(R)]
        psW = psT[0][:, 0:Q, :]

        loaded, wprep, delta_done, w_ready = sem("loaded"), sem("wprep"), sem("delta"), sem("w_ready")
        wlw_done = sem("wlw")
        turned, copied, lo_done = sem("turned"), sem("copied"), sem("lo")
        mm_done, th_done, u_done, v_done = sem("mm"), sem("th"), sem("u"), sem("v")
        st_done, aggr_done, eps_done, rstd_done = sem("stats"), sem("aggr"), sem("eps"), sem("rstd")
        mr_done, shift_done, vn_done = sem("mr"), sem("shift"), sem("vn")
        summed, stored = sem("summed"), sem("stored")
        passed = sem("passed")
        ALL = STEPS * G
        END = (STEPS + 1) * G
        LOW, MM, TANH, U, SILU, STATS, NORM = 1, 3, 4, 4, 5, 6, 8

        block = ctx.enter_context(nc.Block())

        def run(eng, slot):
            for n in range(2 * G):
                slot(n, n, lambda k: k // 2)
            with eng.Fori(0, (STEPS - 2) // BODY) as i:
                for k in range(BODY * G):
                    slot(i * (BODY * G) + (2 * G + k), 2 * G + k, lambda m: i * (BODY * G // 2) + m // 2)
            for n in range(STEPS * G, END + NORM):
                slot(n, n, lambda k: k // 2)

        def tiles(m):
            return slice(m % G * Q, m % G * Q + Q)

        def chained(m, lag):
            return 0 <= m - lag < ALL

        def split(m):
            return m % 2 == 1

        def lows(half, m):
            odd = m if m % 2 else m - 1
            return half(odd) - G // 2 + 1

        @block.sync
        def _(sp):
            sp.dma_start(wt[:], wt_in.rearrange("(k p) n -> p k n", p=P)).then_inc(loaded, 16)
            sp.dma_start(lw[:], lw_in).then_inc(loaded, 16)
            sp.dma_start(lb[:], lb_in).then_inc(loaded, 16)
            sp.dma_start(bias[:], b_in).then_inc(loaded, 16)
            for k in range(G):
                sp.wait_ge(summed, k + 1)
                rows = out[k * Q * P:(k + 1) * Q * P, :] if k < G - 1 else out[k * Q * P:k * Q * P + P, :]
                n = Q if k < G - 1 else 1
                sp.dma_start(rows.rearrange("(q p) d -> p q d", p=P), vn[:, k * Q:k * Q + n, :]).then_inc(stored, 16)
            sp.dma_start(out[(NT - 1) * P:N, :], vn[0:LAST, NT - 1, :]).then_inc(stored, 16)
            sp.wait_ge(stored, (G + 1) * 16)

        @block.tensor
        def _(pe):
            delta = psW.rearrange("p q n -> p (q n)")
            pe.wait_ge(wprep, 2)
            for k in range(KD):
                pe.matmul(delta, lbm[:, k, :], wt[:, k, :], start=(k == 0), stop=False)
            for k in range(KD):
                pe.matmul(delta, g.negones[:], wlw[:, k, :], start=False, stop=False)
            pe.matmul(delta, g.ones[0:1, :], bias[0:1, :], start=False, stop=True).then_inc(delta_done, 1)
            pe.wait_ge(w_ready, 3 * KD)

            def slot(n, m, half):
                if m < G:
                    if m >= R:
                        pe.wait_ge(u_done, n - R + 1)
                    for q in range(Q):
                        last = pe.matmul(psH[m % R][:, q * D:(q + 1) * D], g.ident[:], h0[:, m * Q + q, :],
                                         start=True, stop=True)
                    last.then_inc(mm_done, 1)
                    return
                if m < END:
                    gr = m % G
                    pe.wait_ge(vn_done, n - G + 1)
                    if m - R >= G:
                        pe.wait_ge(copied, n - R - G + 1)
                        if split(m):
                            pe.wait_ge(lo_done, lows(half, m - R))
                    for q in range(Q):
                        for k in range(KD):
                            last = pe.transpose(psT[m % R][:, q * KD + k, :], vn[:, gr * Q + q, k * P:(k + 1) * P],
                                                g.ident[:])
                    last.then_inc(turned, 1)
                if G <= m - MM < END:
                    w = m - MM
                    if w - R < ALL:
                        pe.wait_ge(u_done, n - MM - R + 1)
                    else:
                        pe.wait_ge(summed, n - MM - R - ALL + 1)
                    if split(w):
                        pe.wait_ge(lo_done, lows(half, w))
                        s = w // 2 % 2
                        pairs = ((vTh, w2h), (vTh, w2l), (vTl, w2h))
                    else:
                        pe.wait_ge(copied, n - MM - G + 1)
                        s = w // 2 % 2
                        pairs = ((vT, w2),)
                    for q in range(Q):
                        for k in range(KD):
                            for j, (a, b) in enumerate(pairs):
                                last = pe.matmul(psH[w % R][:, q * D:(q + 1) * D], a[:, s, q * KD + k, :], b[:, k, :],
                                                 start=(k == 0 and j == 0), stop=(k == KD - 1 and j == len(pairs) - 1))
                    last.then_inc(mm_done, 1)

            run(pe, slot)

        @block.scalar
        def _(act):
            act.wait_ge(w_ready, KD)
            for k in range(KD):
                act.activation(w2h[:, k, :], w2[:, k, :], ACT.Copy).then_inc(w_ready, 1)
            act.activation(warm[:], w2[:, 0, 0:1], ACT.Silu)

            def slot(n, m, half):
                if G <= m < END:
                    act.wait_ge(turned, n - G + 1)
                    if m - R >= 0:
                        act.wait_ge(mm_done, n - R + 1)
                    to = vTh if split(m) else vT
                    act.activation(to[:, m // 2 % 2], psT[m % R][:], ACT.Copy).then_inc(copied, 1)
                if chained(m, TANH):
                    a = (m - TANH) % R
                    act.wait_ge(mm_done, n - TANH + 1)
                    if m - TANH >= R:
                        act.wait_ge(u_done, n - TANH - R + 1)
                    act.activation(th[:, a], psH[a][:], ACT.Tanh).then_inc(th_done, 1)
                if chained(m, SILU):
                    act.wait_ge(u_done, n - SILU + 1)
                    act.activation(vn[:, tiles(m - SILU)].rearrange("p q d -> p (q d)"), u[:, (m - SILU) % R],
                                   ACT.Silu).then_inc(v_done, 1)

            run(act, slot)

        @block.vector
        def _(dve):
            dve.wait_ge(loaded, 64)
            for k in range(KD):
                dve.tensor_scalar(wlw[:, k, :], wt[:, k, :], lw[:, k:k + 1], None, ALU.mult).then_inc(wlw_done, 1)
                last = dve.tensor_scalar(lbm[:, k, :], g.ones[:], lb[:, k:k + 1], None, ALU.mult)
            last.then_inc(wprep, 2)
            dve.wait_ge(wlw_done, KD)
            dve.wait_ge(delta_done, 1)
            for k in range(KD):
                dve.scalar_tensor_tensor(out=w2[:, k, :], in0=psW.rearrange("p q n -> p (q n)"), scalar=1.0 / D,
                                         in1=wlw[:, k, :], op0=ALU.mult, op1=ALU.add).then_inc(w_ready, 1)
            dve.wait_ge(w_ready, 2 * KD)
            for k in range(KD):
                dve.tensor_tensor(w2l[:, k, :], w2[:, k, :], w2h[:, k, :].bitcast(F32), ALU.subtract).then_inc(w_ready, 1)

            def slot(n, m, half):
                if chained(m, NORM):
                    q = tiles(m - NORM)
                    dve.wait_ge(rstd_done, n - NORM + 1)
                    dve.tensor_tensor(mr[:, q], mv[:, q, 0], rstd[:, q], ALU.mult).then_inc(mr_done, 1)
                if chained(m, STATS):
                    dve.wait_ge(v_done, n - STATS + 1)
                    for q in range(Q):
                        t = (m - STATS) % G * Q + q
                        last = dve.bn_stats(stats[:, t, :], vn[:, t, :])
                    last.then_inc(st_done, 1)
                if chained(m, NORM):
                    q = tiles(m - NORM)
                    dve.wait_ge(mr_done, n - NORM + 1)
                    dve.tensor_scalar(shift[:, q], mr[:, q], -1.0, 1.0, ALU.mult, ALU.add).then_inc(shift_done, 1)
                if G <= m - LOW < END and split(m - LOW):
                    w = m - LOW
                    dve.wait_ge(copied, n - LOW - G + 1)
                    dve.tensor_tensor(vTl[:, w // 2 % 2], psT[w % R][:], vTh[:, w // 2 % 2].bitcast(F32),
                                      ALU.subtract).then_inc(lo_done, 1)
                if chained(m, U):
                    a = (m - U) % R
                    dve.wait_ge(th_done, n - U + 1)
                    if m - U >= R:
                        dve.wait_ge(v_done, n - U - R + 1)
                    dve.scalar_tensor_tensor(out=u[:, a], in0=th[:, a], scalar=0.01, in1=psH[a][:],
                                             op0=ALU.mult, op1=ALU.add).then_inc(u_done, 1)
                if chained(m, STATS):
                    wait_apart(dve, st_done, n - STATS + 1, passed)
                    for q in range(Q):
                        t = (m - STATS) % G * Q + q
                        last = dve.bn_aggr(mv[:, t, :], stats[:, t, :])
                    last.then_inc(aggr_done, 1)
                if ALL <= m - U < END:
                    dve.wait_ge(mm_done, n - U + 1)
                    dve.tensor_tensor(vn[:, tiles(m - U), :], g.x[:, tiles(m - U), :],
                                      psH[(m - U) % R][:].rearrange("p (q d) -> p q d", q=Q),
                                      ALU.add).then_inc(summed, 1)

            run(dve, slot)

        @block.gpsimd
        def _(pool):
            def slot(n, m, half):
                if chained(m, STATS):
                    q = tiles(m - STATS)
                    wait_apart(pool, aggr_done, n - STATS + 1, passed)
                    pool.tensor_scalar(veps[:, q], mv[:, q, 1], 1.0, LN_EPS, ALU.mult, ALU.add).then_inc(eps_done, 1)
                    pool.wait_ge(eps_done, n - STATS + 1)
                    pool.tensor_tensor(rstd[:, q], veps[:, q], g.mhalf[:, 0:Q], ALU.pow).then_inc(rstd_done, 1)
                if chained(m, NORM):
                    wait_apart(pool, shift_done, n - NORM + 1, passed)
                    for q in range(Q):
                        t = (m - NORM) % G * Q + q
                        last = pool.tensor_scalar(vn[:, t, :], vn[:, t, :], rstd[:, t:t + 1], shift[:, t:t + 1],
                                                  ALU.mult, ALU.add)
                    last.then_inc(vn_done, 1)

            run(pool, slot)


def two_layer_graph_network(nc, x, adjt, adjl, w0, wg, bg, wall, eb1, eb2, w1, b1, ffw, lw, lb, fb, out):
    xn_rows = nc.dram_tensor("xn_rows", (ROWS, D), F32, kind="Internal").ap()
    x_rows = nc.dram_tensor("x_rows", (ROWS, D), F32, kind="Internal").ap()
    table = nc.dram_tensor("slot_table", (SLOTS, 2), U32, kind="Internal").ap()
    with ExitStack() as ctx:
        sb, _ = tensors(nc, ctx)
        g = Shared(sb)
        sched = sb("sched", [1, 2, TILES + 1], I32)
        constants_block(nc, g)
        with ExitStack() as layer0:
            sb0, _ = tensors(nc, layer0)
            s_row = sb0("l0_s", [P, NT, D])
            route = Routing(sb0, wg, bg, xn_rows, x_rows, table, sched)
            support_block(nc, g, x, w0, adjt, adjl, s_row, route)
            graph_block(nc, g, "g0", adjt, adjl, s_row, g.dinv0, None, True, None, route)
        experts_block(nc, g, wall, eb1, eb2, xn_rows, x_rows, table, sched)
        with ExitStack() as layer1:
            sb1, _ = tensors(nc, layer1)
            s_row = sb1("l1_s", [P, NT, D])
            h0 = sb1("l1_h0", [P, NT, D])
            column_scale = sb1("l1_column_scale", [P, D])
            standardise_block(nc, g, x_rows, w1, b1, s_row, column_scale)
            graph_block(nc, g, "g1", adjt, adjl, s_row, g.dinv1, column_scale, False, h0)
            steps_block(nc, g, ffw, lw, lb, fb, h0, out)


def kernel(x, adj, L0_gnn_W, L0_ffn_Wg, L0_ffn_bg, L0_ffn_W1, L0_ffn_b1, L0_ffn_W2, L0_ffn_b2, L1_gnn_W, L1_gnn_b,
           L1_ffn_ln_w, L1_ffn_ln_b, L1_ffn_W, L1_ffn_b):
    import numpy as np
    from concourse import bacc
    from concourse.bass_utils import run_bass_kernel_spmd

    f = lambda a: np.asarray(a)
    c = np.ascontiguousarray
    xp = np.zeros((NPAD, D), np.float32)
    xp[:N] = f(x)
    at = np.zeros((NPAD, NPAD), np.float32)
    at[:N, :N] = f(adj).T
    whole = PANELS * PANEL
    al = at[:, whole:].reshape(CHUNKS, CT, P, LPANEL).transpose(0, 2, 1, 3).reshape(CHUNKS * P, LCW)
    at = at[:, :whole].reshape(CHUNKS, CT, P, PANELS, PANEL).transpose(3, 0, 2, 1, 4).reshape(PANELS * CHUNKS * P, CW)
    w1 = f(L0_ffn_W1).transpose(0, 2, 1).reshape(E, KD, P, H).transpose(0, 2, 1, 3).reshape(E * P, KD * H)
    w2 = f(L0_ffn_W2).transpose(0, 2, 1).reshape(E, HB, P, D).transpose(0, 2, 1, 3).reshape(E * P, HB * D)
    arrays = {
        "x": xp, "adjt": c(at), "adjl": c(al), "w0": c(f(L0_gnn_W).T), "wg": c(f(L0_ffn_Wg).T), "bg": c(f(L0_ffn_bg).reshape(1, E)),
        "wall": c(np.concatenate([w1, w2], 1)),
        "eb1": c(f(L0_ffn_b1).reshape(E, HB, P).transpose(0, 2, 1).reshape(E * P, HB)), "eb2": c(f(L0_ffn_b2)),
        "w1": c(f(L1_gnn_W).T), "b1": c(f(L1_gnn_b).reshape(1, D)), "ffw": c(f(L1_ffn_W).T),
        "lw": c(f(L1_ffn_ln_w).reshape(KD, P).T), "lb": c(f(L1_ffn_ln_b).reshape(KD, P).T),
        "fb": c(f(L1_ffn_b).reshape(1, D)),
    }
    nc = bacc.Bacc("TRN2", target_bir_lowering=False, num_devices=1)
    aps = {k: nc.dram_tensor(f"in_{k}", a.shape, mybir.dt.from_np(a.dtype), kind="ExternalInput").ap()
           for k, a in arrays.items()}
    out = nc.dram_tensor("out", (N, D), F32, kind="ExternalOutput").ap()
    two_layer_graph_network(nc, **aps, out=out)
    r = run_bass_kernel_spmd(nc, [{f"in_{k}": a for k, a in arrays.items()}], core_ids=[0])
    return r.results[0]["out"]
```

```python
from contextlib import ExitStack

import concourse.bass as bass
from concourse import mybir

F32 = mybir.dt.float32
F32R = mybir.dt.float32r
U32 = mybir.dt.uint32
I32 = mybir.dt.int32
ALU = mybir.AluOpType
ACT = mybir.ActivationFunctionType
AX = mybir.AxisListType

P = 128
N = 3327
NT = (N + P - 1) // P
NPAD = NT * P
LAST = N - (NT - 1) * P
D = 256
KD = D // P
E = 8
H = 1024
HB = H // P
LN_EPS = 1e-5
STEPS = 30

PT = 3
PANEL = PT * P
PANELS = NT // PT
LT = NT - PANELS * PT
LPANEL = LT * P
CT = 2
CHUNKS = NT // CT
CW = CT * PANEL
LCW = CT * LPANEL

TW = 256
REG = ((N + TW - 1) // TW + 1) * TW
TILES = (2 * N + E * (TW - 1)) // TW
SLOTS = E * REG + (TILES + 1) * TW
ROWS = NPAD + TW
KMAX = (N + TW - 1) // TW
INITP = SLOTS // (2 * TW)


class Shared:

    def __init__(self, sb):
        self.ident = sb("ident", [P, P])
        self.ones = sb("ones", [P, P])
        self.negones = sb("negones", [P, P])
        self.before = sb("before", [P, P])
        self.valid = sb("valid", [P, P])
        self.mhalf = sb("mhalf", [P, NT])
        self.dinv0 = sb("dinv0", [P, NT])
        self.dinv1 = sb("dinv1", [P, NT])
        self.x = sb("x", [P, NT, D])


class Routing:

    def __init__(self, sb, wg, bg, xn_rows, x_rows, table, sched):
        self.wg, self.bg, self.xn_rows, self.x_rows, self.table, self.sched = wg, bg, xn_rows, x_rows, table, sched
        self.wg_sb = sb("rt_wg", [P, KD, E])
        self.bg_sb = sb("rt_bg", [P, E])
        self.rev_i = sb("rt_rev_i", [P, E], I32)
        self.rev = sb("rt_rev", [P, E])
        self.reg_i = sb("rt_reg_i", [P, E], I32)
        self.reg = sb("rt_reg", [P, E])
        self.k_i = sb("rt_k_i", [P, KMAX], I32)
        self.kf = sb("rt_k", [P, KMAX])
        self.t_i = sb("rt_t_i", [P, TILES + 1], I32)
        self.tf = sb("rt_t", [P, TILES + 1])
        self.token = sb("rt_token", [P, NT], U32)
        self.free = sb("rt_free", [P, PT + 1, E])


class Chain:

    def __init__(self, eng, sem, passed=None):
        self.eng, self.sem, self.n, self.passed = eng, sem, 0, passed

    def __call__(self, ins):
        self.n = self.n + 1
        ins.then_inc(self.sem, 1)
        if self.passed is None:
            self.eng.wait_ge(self.sem, self.n)
        else:
            wait_apart(self.eng, self.sem, self.n, self.passed)


def wait_apart(eng, sem, value, passed):
    eng.wait_ge(sem, value)
    eng.sem_inc(passed, 1)


def tensors(nc, stack):
    def sb(name, shape, dt=F32):
        return stack.enter_context(nc.sbuf_tensor(name, shape, dt))

    def ps(name, shape, dt=F32):
        return stack.enter_context(nc.psum_tensor(name, shape, dt))

    return sb, ps


def semaphores(nc, stack, tag):
    held = []

    def clear():
        nc.clear_and_free_semaphores(held)
        nc.all_engine_barrier()

    stack.callback(clear)

    def sem(name):
        held.append(nc.alloc_semaphore(f"{tag}_{name}"))
        return held[-1]

    return sem


def constants_block(nc, g):
    with ExitStack() as ctx:
        sem = semaphores(nc, ctx, "const")
        filled = sem("filled")
        block = ctx.enter_context(nc.Block())

        @block.gpsimd
        def _(pool):
            pool.memset(g.ident[:], 0.0)
            pool.memset(g.ones[:], 1.0)
            pool.memset(g.negones[:], -1.0)
            pool.memset(g.mhalf[:], -0.5).then_inc(filled, 1)
            pool.wait_ge(filled, 1)
            pool.affine_select(out=g.ident[:], in_=g.ident[:], compare_op=ALU.not_equal, fill=1.0, base=0,
                               pattern=[[-1, P]], channel_multiplier=1)
            pool.affine_select(out=g.before[:], in_=g.ones[:], compare_op=ALU.is_gt, fill=0.0, base=0,
                               pattern=[[1, P]], channel_multiplier=-1)
            pool.affine_select(out=g.valid[:], in_=g.ones[:], compare_op=ALU.is_ge, fill=0.0, base=LAST - 1,
                               pattern=[[0, P]], channel_multiplier=-1).then_inc(filled, 1)
            pool.wait_ge(filled, 2)


def support_block(nc, g, x_in, w0, adjt, adjl, sp_, route):
    with ExitStack() as ctx:
        sb, ps = tensors(nc, ctx)
        sem = semaphores(nc, ctx, "sup")
        ring = sb("deg_ring", [P, CHUNKS, CW])
        part = sb("deg_part", [P, 3, PANEL])
        colsum = sb("deg_colsum", [P, NPAD])
        w = sb("sup_w", [P, KD, D])
        stats = sb("sup_stats", [P, NT, 6])
        mv = sb("sup_mv", [P, NT, 2])
        veps = sb("sup_veps", [P, NT])
        rstd = sb("sup_rstd", [P, NT])
        shift = sb("sup_shift", [P, NT])
        negshift = sb("sup_negshift", [P, NT])
        xn = sb("sup_xn", [P, 2, D])
        xnT = sb("sup_xnT", [P, 2, KD, P])
        deg = sb("sup_deg", [P, NT])
        degc = sb("sup_degc", [P, NT])
        has = sb("sup_has", [P, NT])
        root = sb("sup_root", [P, NT])
        psT = [ps(f"sup_psT{k}", [P, KD, P]) for k in range(2)]
        psS = [ps(f"sup_psS{k}", [P, D]) for k in range(2)]
        psD = ps("sup_psD", [P, NT])
        init = sb("rt_init", [INITP, 2, TW, 2], U32)
        zero = sb("rt_zero", [P, TW // P, D])
        filled, stored = sem("filled"), sem("stored")

        x_loaded, w_loaded = sem("x_loaded"), sem("w_loaded")
        chunk_loaded = [sem(f"chunk{c}") for c in range(CHUNKS)]
        chunks_used = sem("chunks_used")
        colsum_done = sem("colsum_done")
        dchain = sem("dchain")
        stats_done, norm_done = sem("stats_done"), sem("norm_done")
        pchain = sem("pchain")
        xn_done, tr_done, xnT_done, mm_done, sup_done = (sem(n) for n in ("xn", "tr", "xnT", "mm", "sup"))
        deg_mm, deg_added, deg_done, dinv_done = (sem(n) for n in ("degmm", "degadd", "deg", "dinv"))
        GROUPS = [(0, 4), (4, 8), (8, CHUNKS)]
        WHOLE = PANELS * PT
        group_of = [next(k for k, (a, b) in enumerate(GROUPS) if a <= c < b) for c in range(CHUNKS)]

        block = ctx.enter_context(nc.Block())

        @block.sync
        def _(sp):
            sp.dma_start(g.x[:], x_in.rearrange("(t p) d -> p t d", p=P)).then_inc(x_loaded, 16)
            sp.dma_start(w[:], w0.rearrange("(k p) n -> p k n", p=P)).then_inc(w_loaded, 16)
            with sp.Fori(0, PANELS) as p:
                for c in range(CHUNKS):
                    if c in (a for a, _ in GROUPS):
                        sp.wait_ge(chunks_used, p * 3 + group_of[c] + 1)
                    sp.dma_start(ring[:, c, :], adjt[bass.ds((p * CHUNKS + c) * P, P), :]).then_inc(chunk_loaded[c], 16)
            for c in range(CHUNKS):
                if c in (a for a, _ in GROUPS):
                    sp.wait_ge(chunks_used, PANELS * 3 + group_of[c] + 1)
                sp.dma_start(ring[:, c, 0:LCW], adjl[c * P:(c + 1) * P, :]).then_inc(chunk_loaded[c], 16)
            sp.wait_ge(filled, 2)
            sp.dma_start(route.xn_rows[NPAD:ROWS, :].rearrange("(t p) d -> p t d", p=P), zero[:]).then_inc(stored, 16)
            sp.dma_start(route.table.rearrange("(p m) c -> p m c", p=INITP),
                         init[:].rearrange("p a m c -> p (a m) c")).then_inc(stored, 16)
            sp.dma_start(route.wg_sb[:], route.wg.rearrange("(k p) e -> p k e", p=P)).then_inc(stored, 16)
            sp.dma_start(route.bg_sb[:], route.bg.broadcast_to([P, E])).then_inc(stored, 16)
            sp.wait_ge(stored, 64)

        @block.vector
        def _(dve):
            chain = Chain(dve, dchain)
            dve.sem_inc(chunks_used, 3)
            dve.sem_inc(colsum_done, 1)
            dve.wait_ge(x_loaded, 16)
            for t in range(NT):
                dve.bn_stats(stats[:, t, :], g.x[:, t, :]).then_inc(dchain, 1)
            chain.n = NT
            dve.wait_ge(dchain, NT)
            for t in range(NT):
                last = dve.bn_aggr(mv[:, t, :], stats[:, t, :])
            chain(last)
            dve.tensor_scalar(veps[:], mv[:, :, 1], LN_EPS, None, ALU.add).then_inc(stats_done, 1)
            dve.wait_ge(filled, 1)
            dve.tensor_copy(route.rev[:], route.rev_i[:])
            dve.tensor_copy(route.reg[:], route.reg_i[:])
            dve.tensor_copy(route.free[:, PT, :], route.reg_i[:])
            dve.tensor_copy(route.kf[:], route.k_i[:])
            dve.tensor_copy(route.tf[:], route.t_i[:])
            with dve.Fori(0, PANELS) as p:
                for k, (a, b) in enumerate(GROUPS):
                    if k == 0:
                        dve.wait_ge(colsum_done, p + 1)
                    for c in range(a, b):
                        dve.wait_ge(chunk_loaded[c], p * 16 + 16)
                    blocks = ring[:, a:b, :].rearrange("p c (q i) -> p i (c q)", i=PANEL)
                    dve.tensor_reduce(part[:, k, :], blocks, AX.X, ALU.add).then_inc(chunks_used, 1)
                dve.wait_ge(chunks_used, p * 3 + 6)
                dve.tensor_reduce(colsum[:, bass.ds(p * PANEL, PANEL)], part[:].rearrange("p k i -> p i k"),
                                  AX.X, ALU.add).then_inc(colsum_done, 1)
            def degrees(k, tiles):
                dve.wait_ge(deg_mm, k + 1)
                dve.tensor_scalar(deg[:, tiles], psD[:, tiles], 1.0, None, ALU.add).then_inc(deg_added, 1)
                dve.wait_ge(deg_added, k + 1)
                dve.tensor_scalar(has[:, tiles], deg[:, tiles], 0.0, None, ALU.is_gt)
                dve.tensor_scalar(degc[:, tiles], deg[:, tiles], 1e-30, None, ALU.max).then_inc(deg_done, 1)

            for k, (a, b) in enumerate(GROUPS):
                if k == 0:
                    dve.wait_ge(colsum_done, PANELS + 1)
                for c in range(a, b):
                    dve.wait_ge(chunk_loaded[c], PANELS * 16 + 16)
                blocks = ring[:, a:b, 0:LCW].rearrange("p c (q i) -> p i c q", i=LPANEL)
                dve.tensor_reduce(part[:, k, 0:LPANEL], blocks, AX.XY, ALU.add).then_inc(chunks_used, 1)
                if k == 0:
                    degrees(0, slice(0, WHOLE))
            dve.wait_ge(chunks_used, PANELS * 3 + 6)
            dve.tensor_reduce(colsum[:, PANELS * PANEL:NPAD], part[:, :, 0:LPANEL].rearrange("p k i -> p i k"),
                              AX.X, ALU.add).then_inc(colsum_done, 1)
            degrees(1, slice(WHOLE, NT))
            dve.wait_ge(dinv_done, 4)
            dve.tensor_tensor(g.dinv1[:], root[:], has[:], ALU.mult)

        @block.gpsimd
        def _(pool):
            chain = Chain(pool, pchain)
            pool.iota(route.rev_i[:], [[-1, E]], base=E, channel_multiplier=0)
            pool.iota(route.reg_i[:], [[REG, E]], base=0, channel_multiplier=0)
            pool.iota(route.k_i[:], [[TW, KMAX]], base=0, channel_multiplier=0)
            pool.iota(route.t_i[:], [[1, TILES + 1]], base=0, channel_multiplier=0).then_inc(filled, 1)
            pool.iota(route.token[:], [[P, NT]], base=0, channel_multiplier=1)
            pool.iota(init[:, :, :, 0], [[0, 2], [1, TW]], base=NPAD, channel_multiplier=0)
            pool.memset(init[:, :, :, 1], 0)
            pool.memset(zero[:], 0.0).then_inc(filled, 1)
            pool.wait_ge(stats_done, 1)
            chain(pool.tensor_tensor(rstd[:], veps[:], g.mhalf[:, 0:NT], ALU.pow))
            chain(pool.tensor_tensor(shift[:], mv[:, :, 0], rstd[:], ALU.mult))
            pool.tensor_scalar(negshift[:], shift[:], -1.0, 0.0, ALU.mult, ALU.add).then_inc(norm_done, 1)
            for k, tiles in enumerate((slice(0, WHOLE), slice(WHOLE, NT))):
                pool.wait_ge(deg_done, k + 1)
                pool.tensor_tensor(g.dinv0[:, tiles], deg[:, tiles], g.mhalf[:, tiles], ALU.pow).then_inc(dinv_done, 1)
                pool.tensor_tensor(root[:, tiles], degc[:, tiles], g.mhalf[:, tiles], ALU.pow).then_inc(dinv_done, 1)

        @block.scalar
        def _(act):
            act.wait_ge(norm_done, 1)
            for t in range(NT + 1):
                if t < NT:
                    if t >= 2:
                        act.wait_ge(tr_done, t - 1)
                    act.activation(xn[:, t % 2, :], g.x[:, t, :], ACT.Identity, bias=negshift[:, t:t + 1],
                                   scale=rstd[:, t:t + 1]).then_inc(xn_done, 1)
                    act.wait_ge(tr_done, t + 1)
                    if t >= 2:
                        act.wait_ge(mm_done, t - 1)
                    act.activation(xnT[:, t % 2], psT[t % 2][:], ACT.Copy).then_inc(xnT_done, 1)
                if t >= 1:
                    act.wait_ge(mm_done, t)
                    act.activation(sp_[:, t - 1, :], psS[(t - 1) % 2][:], ACT.Copy).then_inc(sup_done, 1)

        @block.tensor
        def _(pe):
            pe.wait_ge(w_loaded, 16)
            for t in range(NT):
                pe.wait_ge(xn_done, t + 1)
                if t >= 2:
                    pe.wait_ge(xnT_done, t - 1)
                for k in range(KD):
                    last = pe.transpose(psT[t % 2][:, k, :], xn[:, t % 2, k * P:(k + 1) * P], g.ident[:])
                last.then_inc(tr_done, 1)
                pe.wait_ge(xnT_done, t + 1)
                if t >= 2:
                    pe.wait_ge(sup_done, t - 1)
                for k in range(KD):
                    last = pe.matmul(psS[t % 2][:], xnT[:, t % 2, k, :], w[:, k, :], start=(k == 0), stop=(k == KD - 1))
                last.then_inc(mm_done, 1)
            for t in range(NT):
                if t % PT == 0:
                    pe.wait_ge(colsum_done, t // PT + 2)
                last = pe.matmul(psD[:, t:t + 1], colsum[:, t * P:(t + 1) * P], g.ones[:, 0:1], start=True, stop=True)
                if t in (WHOLE - 1, NT - 1):
                    last.then_inc(deg_mm, 1)


def graph_block(nc, g, tag, adjt, adjl, s_row, dinv, column_scale, relu, hn, route=None):
    with ExitStack() as ctx:
        sb, ps = tensors(nc, ctx)
        sem = semaphores(nc, ctx, tag)
        SPLITS = 4
        sh = sb(f"{tag}_sh", [P, NT, D], F32R)
        sl = sb(f"{tag}_sl", [P, NT, D], F32R)
        raw = sb(f"{tag}_raw", [P, CHUNKS, CW])
        hi = sb(f"{tag}_hi", [P, SPLITS, PANEL], F32R)
        lo = sb(f"{tag}_lo", [P, SPLITS, PANEL], F32R)
        out_t = sb(f"{tag}_out_t", [P, KD, PANEL])
        dscale = sb(f"{tag}_dscale", [P, PT])
        plus_s = sb(f"{tag}_plus_s", [P, PT, D])
        delta = sb(f"{tag}_delta", [P, PT, D])
        stats = sb(f"{tag}_stats", [P, PT, 6])
        mv = sb(f"{tag}_mv", [P, PT, 2])
        veps = sb(f"{tag}_veps", [P, PT])
        rstd = sb(f"{tag}_rstd", [P, PT])
        mr = sb(f"{tag}_mr", [P, PT])
        shift = sb(f"{tag}_shift", [P, PT])
        if route:
            n2 = [P, PT]
            hn = sb("rt_hn", [P, 2, PT, D])
            hT = sb("rt_hT", [P, PT, D])
            sc = sb("rt_scores", [P, PT, E])
            sc2 = sb("rt_scores2", [P, PT, E])
            best = [sb(f"rt_best{k}", n2) for k in range(2)]
            first_one = [sb(f"rt_first{k}", n2) for k in range(2)]
            hot = [sb(f"rt_hot{k}", [P, PT, E]) for k in range(2)]
            work = [sb(f"rt_work{k}", [P, PT, E]) for k in range(2)]
            chosen = sb("rt_chosen", [P, PT, E])
            diff = sb("rt_diff", n2)
            ex = sb("rt_ex", n2)
            ex1 = sb("rt_ex1", n2)
            pos = sb("rt_pos", [P, PT, E])
            slot_f = [sb(f"rt_slotf{k}", n2) for k in range(2)]
            slot = [sb(f"rt_slot{k}", n2, U32) for k in range(2)]
            prob = [sb(f"rt_prob{k}", n2) for k in range(2)]
            meta = sb("rt_meta", [P, 2, PT, 2], U32)
            psR = ps("rt_psR", [P, 3, PT * E])
            hback, hT_done, gate_done, chosen_done = sem("hback"), sem("hT"), sem("gate"), sem("chosen")
            exp_in, exp_out, rank_done, slots_done = sem("exp_in"), sem("exp_out"), sem("rank"), sem("slots")
            dchain, stored, scattered, slots_used = sem("dchain"), sem("stored"), sem("scattered"), sem("slots_used")
        acc = [[ps(f"{tag}_acc{b}{d}", [P, PANEL]) for d in range(KD)] for b in range(2)]
        psT = ps(f"{tag}_psT", [P, PT, 512])

        chunk_loaded = [sem(f"chunk{c}") for c in range(CHUNKS)]
        s_done, sh_done, sl_done = sem("s"), sem("sh"), sem("sl")
        hi_done, lo_done, mm_done = sem("hi"), sem("lo"), sem("mm")
        evicted, tr_done, add_done, act_done, x_done = (sem(n) for n in ("evicted", "tr", "add", "act", "x"))
        dscale_done, st_done, aggr_done, hn_done = sem("dscale"), sem("stats"), sem("aggr"), sem("hn")
        eps_done, rstd_done, mr_done, shift_done = sem("eps"), sem("rstd"), sem("mr"), sem("shift")
        passed = sem("passed")
        LINKS = 12 + (1 + PT) + 3 + 5

        block = ctx.enter_context(nc.Block())

        def run(eng, panel, finish):
            for p in range(2):
                panel(p, p)
            with eng.Fori(0, (PANELS - 2) // 2) as i:
                for m in (2, 3):
                    panel(i * 2 + m, m)
            panel(PANELS, PANELS)
            finish(PANELS + 1, PANELS + 1)
            if route:
                finish(PANELS + 2, PANELS + 2)

        def width(m):
            return PANEL if m < PANELS else LPANEL

        def split_slot(m, j):
            return (m * NT + j) % SPLITS

        def rows(p, m):
            n = PT if m <= PANELS else LT
            first = (p - 1) * PT
            return n, (slice(first, first + n) if isinstance(p, int) else bass.ds(first, n))

        def routed(m):
            return 0 if m < 2 else PT if m <= PANELS + 1 else LT

        @block.sync
        def _(sp):
            def store(p, m):
                n = routed(m)
                if not route or not n:
                    return
                first = (p - 2) * PT
                tiles = slice(first, first + n) if isinstance(p, int) else bass.ds(first, n)
                rows_of = slice(first * P, (first + n) * P) if isinstance(p, int) else bass.ds(first * P, n * P)
                sp.wait_ge(hn_done, p - 1)
                for to, source in ((route.xn_rows, hn[:, m % 2, 0:n, :]), (route.x_rows, g.x[:, tiles, :])):
                    sp.dma_start(to[rows_of, :].rearrange("(t p) d -> p t d", p=P), source).then_inc(stored, 16)

            def finish(p, m):
                store(p, m)
                if route and m == PANELS + 2:
                    sp.wait_ge(stored, 32 * (PANELS + 2))

            def panel(p, m):
                for c in range(CHUNKS):
                    if c == 4:
                        store(p, m)
                    if m >= 1:
                        sp.wait_ge(lo_done, p * NT + ((c + 1) * CT - NT))
                    if m < PANELS:
                        row = (p * CHUNKS + c) * P
                        src = adjt[row:row + P, :] if isinstance(p, int) else adjt[bass.ds(row, P), :]
                    else:
                        src = adjl[c * P:(c + 1) * P, :]
                    sp.dma_start(raw[:, c, 0:CT * width(m)], src).then_inc(chunk_loaded[c], 16)

            run(sp, panel, finish)

        @block.scalar
        def _(act):
            if route:
                for counted, by in ((hback, 1), (gate_done, 1), (slots_done, 1), (slots_used, 1), (stored, 32)):
                    act.sem_inc(counted, by)

            def round_s(c):
                act.wait_ge(s_done, c + 1)
                act.activation(sh[:, c * CT:(c + 1) * CT, :], s_row[:, c * CT:(c + 1) * CT, :],
                               ACT.Copy).then_inc(sh_done, 1)

            def evict(p, m):
                act.wait_ge(mm_done, p * NT)
                if m >= 2:
                    act.wait_ge(tr_done, p - 1)
                w = width(m - 1)
                for d in range(KD):
                    last = act.activation(out_t[:, d, 0:w], acc[(m - 1) % 2][d][:, 0:w], ACT.Copy)
                last.then_inc(evicted, 1)

            def scale(p, m):
                n, _ = rows(p, m)
                act.wait_ge(add_done, p)
                act.wait_ge(dscale_done, p)
                if m >= 2:
                    act.wait_ge(x_done, p - 1)
                for t in range(n):
                    last = act.activation(delta[:, t, :], plus_s[:, t, :], ACT.Relu if relu else ACT.Copy,
                                          scale=dscale[:, t:t + 1])
                last.then_inc(act_done, 1)

            def normalise(p, m):
                n, _ = rows(p, m)
                first = (p - 1) * PT
                act.wait_ge(shift_done, p)
                if route and m >= 2:
                    act.wait_ge(stored, (p - 1) * 32)
                    act.wait_ge(hback, p - 1)
                for t in range(n):
                    tile = slice(first + t, first + t + 1) if isinstance(p, int) else bass.ds(first + t, 1)
                    to = hn[:, (m - 1) % 2, t:t + 1, :] if route else hn[:, tile, :]
                    last = act.activation(to, g.x[:, tile, :], ACT.Identity, scale=rstd[:, t:t + 1],
                                          bias=shift[:, t:t + 1])
                last.then_inc(hn_done, 1)

            def copy_turned(p, m):
                n = routed(m)
                act.wait_ge(hback, p)
                act.wait_ge(gate_done, p - 1)
                act.activation(hT[:, 0:n, :], psT[:, 0:n, D:2 * D], ACT.Copy).then_inc(hT_done, 1)

            def exponent(p, m):
                n = routed(m)
                act.wait_ge(exp_in, p - 1)
                act.activation(ex[:, 0:n], diff[:, 0:n], ACT.Exp).then_inc(exp_out, 1)

            def panel(p, m):
                if m == 0:
                    round_s(0)
                for c in range(CHUNKS):
                    w = width(m)
                    act.wait_ge(chunk_loaded[c], p * 16 + 16)
                    for q in range(CT):
                        j = c * CT + q
                        if m * NT + j >= SPLITS:
                            act.wait_ge(mm_done, p * NT + (j + 1 - SPLITS))
                        act.activation(hi[:, split_slot(m, j), 0:w], raw[:, c, q * w:(q + 1) * w],
                                       ACT.Copy).then_inc(hi_done, 1)
                    if m == 0 and c + 1 < CHUNKS:
                        round_s(c + 1)
                    if m >= 1 and c == 1:
                        evict(p, m)
                    if m >= 1 and c == 6:
                        scale(p, m)
                    if route and m >= 2 and c == 2:
                        copy_turned(p, m)
                    if route and m >= 2 and c == 9:
                        exponent(p, m)
                    if m >= 1 and c == CHUNKS - 1:
                        normalise(p, m)

            def finish(p, m):
                if m == PANELS + 1:
                    evict(p, m)
                if route:
                    copy_turned(p, m)
                if m == PANELS + 1:
                    scale(p, m)
                    normalise(p, m)
                if route:
                    exponent(p, m)

            run(act, panel, finish)

        @block.vector
        def _(dve):
            def scale_s(c):
                for t in range(c * CT, (c + 1) * CT):
                    if column_scale is None:
                        last = dve.tensor_scalar(s_row[:, t, :], s_row[:, t, :], dinv[:, t:t + 1], None, ALU.mult)
                    else:
                        last = dve.scalar_tensor_tensor(out=s_row[:, t, :], in0=s_row[:, t, :], scalar=dinv[:, t:t + 1],
                                                        in1=column_scale[:], op0=ALU.mult, op1=ALU.mult)
                last.then_inc(s_done, 1)

            def rest_of_s(c):
                tiles = slice(c * CT, (c + 1) * CT)
                dve.wait_ge(sh_done, c + 1)
                dve.tensor_tensor(sl[:, tiles, :], s_row[:, tiles, :], sh[:, tiles, :].bitcast(F32),
                                  ALU.subtract).then_inc(sl_done, 1)

            def add_s(p, m):
                n, tiles = rows(p, m)
                if m >= 2:
                    dve.wait_ge(act_done, p - 1)
                dve.tensor_copy(dscale[:, 0:n], dinv[:, tiles]).then_inc(dscale_done, 1)
                dve.wait_ge(tr_done, p)
                if m == 1:
                    dve.wait_ge(s_done, CHUNKS)
                dve.tensor_tensor(plus_s[:, 0:n, :], psT[:, 0:n, 0:D], s_row[:, tiles, :], ALU.add).then_inc(add_done, 1)

            def add_to_x(p, m):
                n, tiles = rows(p, m)
                dve.wait_ge(act_done, p)
                dve.tensor_tensor(g.x[:, tiles, :], g.x[:, tiles, :], delta[:, 0:n, :], ALU.add).then_inc(x_done, 1)

            def statistics(p, m):
                n, tiles = rows(p, m)
                first = (p - 1) * PT
                if m >= 2:
                    dve.wait_ge(aggr_done, p - 1)
                wait_apart(dve, x_done, p, passed)
                for t in range(n):
                    x = g.x[:, first + t, :] if isinstance(p, int) else g.x[:, bass.ds(first + t, 1), :]
                    last = dve.bn_stats(stats[:, t, :], x)
                last.then_inc(st_done, 1)

            def aggregate(p, m):
                n, _ = rows(p, m)
                if m >= 2:
                    dve.wait_ge(shift_done, p - 1)
                wait_apart(dve, st_done, p, passed)
                for t in range(n):
                    last = dve.bn_aggr(mv[:, t, :], stats[:, t, :])
                last.then_inc(aggr_done, 1)

            def chain_from(p, k):
                c = Chain(dve, dchain, passed)
                c.n = (p - 2) * LINKS + k
                return c

            def best_scores(p, m, k):
                n = routed(m)
                bc = [P, n, E]
                chain = chain_from(p, k * 6)
                s = (sc, sc2)[k]
                if k == 0:
                    wait_apart(dve, gate_done, p, passed)
                    chain(dve.tensor_tensor(sc[:, 0:n, :], psR[:, 0, 0:n * E].rearrange("p (t e) -> p t e", e=E),
                                            route.bg_sb[:].unsqueeze(1).broadcast_to(bc), ALU.add))
                else:
                    chain(dve.scalar_tensor_tensor(out=sc2[:, 0:n, :], in0=hot[0][:, 0:n, :], scalar=-3.0e38,
                                                   in1=sc[:, 0:n, :], op0=ALU.mult, op1=ALU.add))
                chain(dve.tensor_reduce(best[k][:, 0:n], s[:, 0:n, :], AX.X, ALU.max))
                chain(dve.tensor_tensor(work[0][:, 0:n, :], s[:, 0:n, :],
                                        best[k][:, 0:n].unsqueeze(2).broadcast_to(bc), ALU.is_equal))

            def best_expert(p, m, k):
                n = routed(m)
                bc = [P, n, E]
                chain = chain_from(p, k * 6 + 3)
                revb = route.rev[:].unsqueeze(1).broadcast_to(bc)
                chain(dve.tensor_tensor(work[1][:, 0:n, :], work[0][:, 0:n, :], revb, ALU.mult))
                chain(dve.tensor_reduce(first_one[k][:, 0:n], work[1][:, 0:n, :], AX.X, ALU.max))
                chain(dve.tensor_tensor(hot[k][:, 0:n, :], revb,
                                        first_one[k][:, 0:n].unsqueeze(2).broadcast_to(bc), ALU.is_equal))

            def choose(p, m):
                n = routed(m)
                dve.tensor_tensor(diff[:, 0:n], best[1][:, 0:n], best[0][:, 0:n], ALU.subtract).then_inc(exp_in, 1)
                last = dve.tensor_tensor(chosen[:, 0:n, :], hot[0][:, 0:n, :], hot[1][:, 0:n, :], ALU.add)
                if m == PANELS + 2:
                    chain_from(p, 12)(last)
                    last = dve.tensor_scalar(chosen[:, n - 1, :], chosen[:, n - 1, :], g.valid[:, 0:1], None, ALU.mult)
                last.then_inc(chosen_done, 1)

            def count(p, m):
                n = routed(m)
                chain = chain_from(p, 12 + (m == PANELS + 2))
                free = route.free
                wait_apart(dve, rank_done, p - 1, passed)
                chain(dve.tensor_copy(free[:, 0, :], free[:, PT, :]))
                for t in range(n):
                    chain(dve.tensor_tensor(free[:, t + 1, :], free[:, t, :], psR[:, 2, t * E:(t + 1) * E], ALU.add))

            def weigh(p, m):
                n = routed(m)
                first = (p - 2) * PT
                tiles = slice(first, first + n) if isinstance(p, int) else bass.ds(first, n)
                chain = chain_from(p, 13 + n + (m == PANELS + 2))
                wait_apart(dve, exp_out, p - 1, passed)
                chain(dve.tensor_scalar(ex1[:, 0:n], ex[:, 0:n], 1.0, None, ALU.add))
                chain(dve.reciprocal(prob[0][:, 0:n], ex1[:, 0:n]))
                chain(dve.tensor_tensor(prob[1][:, 0:n], ex[:, 0:n], prob[0][:, 0:n], ALU.mult))
                wait_apart(dve, slots_used, p - 1, passed)
                for k in range(2):
                    dve.tensor_copy(meta[:, k, 0:n, 0], route.token[:, tiles])
                    dve.tensor_copy(meta[:, k, 0:n, 1].bitcast(F32), prob[k][:, 0:n])

            def give_slots(p, m):
                n = routed(m)
                chain = chain_from(p, 16 + n + (m == PANELS + 2))
                chain(dve.tensor_tensor(pos[:, 0:n, :], route.free[:, 0:n, :],
                                        psR[:, 1, 0:n * E].rearrange("p (t e) -> p t e", e=E), ALU.add))
                for k in range(2):
                    last = dve.tensor_tensor(work[k][:, 0:n, :], hot[k][:, 0:n, :], pos[:, 0:n, :], ALU.mult)
                    last.then_inc(dchain, 1)
                chain.n = chain.n + 2
                wait_apart(dve, dchain, chain.n, passed)
                for k in range(2):
                    last = dve.tensor_reduce(slot_f[k][:, 0:n], work[k][:, 0:n, :], AX.X, ALU.add)
                    last.then_inc(dchain, 1)
                chain.n = chain.n + 2
                wait_apart(dve, dchain, chain.n, passed)
                for k in range(2):
                    last = dve.tensor_copy(slot[k][:, 0:n], slot_f[k][:, 0:n])
                last.then_inc(slots_done, 1)

            def schedule():
                chain = chain_from(PANELS + 2, LINKS + 1 + LT - PT)
                count = sb("rt_count", [P, E])
                cmp = sb("rt_cmp", [P, E, KMAX])
                ntl = sb("rt_ntl", [P, E])
                cum = sb("rt_cum", [P, E])
                tb = [P, TILES + 1, E]
                le = sb("rt_le", tb)
                le2 = sb("rt_le2", tb)
                eidx = sb("rt_eidx", [P, TILES + 1])
                first_t = sb("rt_first_t", [P, TILES + 1])
                rowf = [sb(f"rt_rowf{k}", [P, TILES + 1]) for k in range(4)]
                chain(dve.tensor_tensor(count[:], route.free[:, LT, :], route.reg[:], ALU.subtract))
                bc = [P, E, KMAX]
                chain(dve.tensor_tensor(cmp[:], count[:].unsqueeze(2).broadcast_to(bc),
                                        route.kf[:].unsqueeze(1).broadcast_to(bc), ALU.is_gt))
                chain(dve.tensor_reduce(ntl[:], cmp[:], AX.X, ALU.add))
                chain(dve.tensor_tensor_scan(cum[:], g.ones[:, 0:E], ntl[:], 0.0, ALU.mult, ALU.add))
                chain(dve.tensor_tensor(le[:], cum[:].unsqueeze(1).broadcast_to(tb),
                                        route.tf[:].unsqueeze(2).broadcast_to(tb), ALU.is_le))
                dve.tensor_reduce(eidx[:], le[:], AX.X, ALU.add)
                chain(dve.tensor_tensor(le2[:], le[:], ntl[:].unsqueeze(1).broadcast_to(tb), ALU.mult))
                chain(dve.tensor_reduce(first_t[:], le2[:], AX.X, ALU.add))
                chain(dve.tensor_tensor(rowf[0][:], route.tf[:], first_t[:], ALU.subtract))
                chain(dve.tensor_scalar(rowf[1][:], rowf[0][:], float(TW), None, ALU.mult))
                dve.tensor_scalar(rowf[3][:], eidx[:], float(E - 1), None, ALU.min)
                chain(dve.scalar_tensor_tensor(out=rowf[2][:], in0=eidx[:], scalar=float(REG), in1=rowf[1][:],
                                               op0=ALU.mult, op1=ALU.add))
                dve.tensor_copy(route.sched[:, 0, :], rowf[2][0:1, :])
                dve.tensor_copy(route.sched[:, 1, :], rowf[3][0:1, :])

            def panel(p, m):
                if m == 0:
                    scale_s(0)
                    scale_s(1)
                    rest_of_s(0)
                for c in range(CHUNKS):
                    w = width(m)
                    for q in range(CT):
                        j = c * CT + q
                        b = split_slot(m, j)
                        dve.wait_ge(hi_done, p * NT + (j + 1))
                        dve.tensor_tensor(lo[:, b, 0:w], raw[:, c, q * w:(q + 1) * w], hi[:, b, 0:w].bitcast(F32),
                                          ALU.subtract).then_inc(lo_done, 1)
                    if m == 0 and c + 2 < CHUNKS:
                        scale_s(c + 2)
                    if m == 0 and c + 1 < CHUNKS:
                        rest_of_s(c + 1)
                    if m >= 1:
                        stage = {5: add_s, 8: add_to_x, 9: statistics, 10: aggregate}.get(c)
                        if stage:
                            stage(p, m)
                    if route and m >= 2:
                        if c in (5, 7):
                            best_scores(p, m, (c - 5) // 2)
                        if c in (6, 8):
                            best_expert(p, m, (c - 6) // 2)
                        stage = {8: choose, 10: count, 11: weigh, 12: give_slots}.get(c)
                        if stage:
                            stage(p, m)

            def finish(p, m):
                if m == PANELS + 1:
                    add_s(p, m)
                    add_to_x(p, m)
                    statistics(p, m)
                    aggregate(p, m)
                if route:
                    for k in range(2):
                        best_scores(p, m, k)
                        best_expert(p, m, k)
                    choose(p, m)
                    count(p, m)
                    weigh(p, m)
                    give_slots(p, m)
                if m == PANELS + 2:
                    schedule()

            run(dve, panel, finish)

        @block.gpsimd
        def _(pool):
            def scale_and_shift(p, m):
                n, _ = rows(p, m)
                wait_apart(pool, aggr_done, p, passed)
                pool.tensor_scalar(veps[:, 0:n], mv[:, 0:n, 1], 1.0, LN_EPS, ALU.mult, ALU.add).then_inc(eps_done, 1)
                if m >= 2:
                    pool.wait_ge(hn_done, p - 1)
                pool.wait_ge(eps_done, p)
                pool.tensor_tensor(rstd[:, 0:n], veps[:, 0:n], g.mhalf[:, 0:n], ALU.pow).then_inc(rstd_done, 1)
                pool.wait_ge(rstd_done, p)
                pool.tensor_tensor(mr[:, 0:n], mv[:, 0:n, 0], rstd[:, 0:n], ALU.mult).then_inc(mr_done, 1)
                wait_apart(pool, mr_done, p, passed)
                pool.tensor_scalar(shift[:, 0:n], mr[:, 0:n], -1.0, 0.0, ALU.mult, ALU.add).then_inc(shift_done, 1)

            def scatter(p, m):
                n = routed(m)
                wait_apart(pool, slots_done, p, passed)
                for t in range(n):
                    nodes = LAST if m == PANELS + 2 and t == n - 1 else P
                    for k in range(2):
                        pool.indirect_dma_start(route.table,
                                                bass.IndirectOffsetOnAxis(ap=slot[k][0:nodes, t:t + 1], axis=0),
                                                meta[0:nodes, k, t, :], None).then_inc(scattered, 16)
                if m < PANELS + 2:
                    pool.wait_ge(scattered, (p - 1) * (2 * PT * 16))
                    pool.sem_inc(slots_used, 1)

            def panel(p, m):
                if 1 <= m <= PANELS + 1:
                    scale_and_shift(p, m)
                if route and m >= 2:
                    scatter(p, m)
                if route and m == PANELS + 2:
                    pool.wait_ge(scattered, 2 * NT * 16)

            run(pool, panel, panel)

        @block.tensor
        def _(pe):
            def turn_back(p, m):
                n, _ = rows(p, m)
                pe.wait_ge(evicted, p)
                if m >= 2:
                    pe.wait_ge(add_done, p - 1)
                    if route:
                        pe.wait_ge(hT_done, p - 1)
                for t in range(n):
                    for d in range(KD):
                        last = pe.transpose(psT[:, t, d * P:(d + 1) * P], out_t[:, d, t * P:(t + 1) * P], g.ident[:])
                last.then_inc(tr_done, 1)

            def turn_normed(p, m):
                pe.wait_ge(hn_done, p - 1)
                pe.wait_ge(add_done, p - 1)
                for t in range(routed(m)):
                    for k in range(KD):
                        last = pe.transpose(psT[:, t, D + k * P:D + (k + 1) * P], hn[:, m % 2, t, k * P:(k + 1) * P],
                                            g.ident[:])
                last.then_inc(hback, 1)

            def gate(p, m):
                pe.wait_ge(hT_done, p - 1)
                pe.wait_ge(slots_done, p - 1)
                for t in range(routed(m)):
                    to = psR[:, 0, t * E:(t + 1) * E]
                    for k in range(KD):
                        last = pe.matmul(to, hT[:, t, k * P:(k + 1) * P], route.wg_sb[:, k, :], start=(k == 0),
                                         stop=(k == KD - 1))
                last.then_inc(gate_done, 1)

            def rank(p, m):
                n = routed(m)
                flat = chosen[:, 0:n, :].rearrange("p t e -> p (t e)")
                pe.wait_ge(chosen_done, p - 1)
                pe.matmul(psR[:, 1, 0:n * E], g.before[:], flat, start=True, stop=True)
                pe.matmul(psR[:, 2, 0:n * E], g.ones[:], flat, start=True, stop=True).then_inc(rank_done, 1)

            def finish(p, m):
                if m == PANELS + 1:
                    if route:
                        turn_normed(p, m)
                    turn_back(p, m)
                elif route:
                    turn_normed(p, m)
                if route:
                    gate(p, m)
                    rank(p, m)

            def panel(p, m):
                w = width(m)
                for c in range(CHUNKS):
                    if m >= 2 and c == 0:
                        pe.wait_ge(evicted, p - 1)
                    if m == 0:
                        pe.wait_ge(sl_done, c + 1)
                    for j in range(c * CT, (c + 1) * CT):
                        pe.wait_ge(lo_done, p * NT + (j + 1))
                        b = split_slot(m, j)
                        for d in range(KD):
                            fs = slice(d * P, (d + 1) * P)
                            for k, (s, a) in enumerate(((sh, hi), (sh, lo), (sl, hi))):
                                last = pe.matmul(acc[m % 2][d][:, 0:w], s[:, j, fs], a[:, b, 0:w],
                                                 start=(j == 0 and k == 0), stop=(j == NT - 1 and k == 2))
                        last.then_inc(mm_done, 1)
                    if route and m >= 2 and c == 0:
                        turn_normed(p, m)
                    if m >= 1 and c == 3:
                        turn_back(p, m)
                    if route and m >= 2 and c == 3:
                        gate(p, m)
                    if route and m >= 2 and c == 8:
                        rank(p, m)

            run(pe, panel, finish)


def experts_block(nc, g, wall, b1, b2, xn_rows, x_rows, table, sched):
    with ExitStack() as ctx:
        sb, ps = tensors(nc, ctx)
        sem = semaphores(nc, ctx, "moe")
        HALF = TW // P
        W1 = KD * H
        WA = 2 * W1
        CHW = 512
        NCH = WA // CHW
        FIRST = W1 // CHW
        POOL_CH = (FIRST - 1, NCH - 1)
        wraw = sb("moe_wraw", [P, 2, WA])
        wh = sb("moe_wh", [P, 2, WA], F32R)
        wl = sb("moe_wl", [P, 2, WA], F32R)
        b1s = sb("moe_b1", [P, 2, HB])
        b2s = sb("moe_b2", [P, 2, D])
        meta = sb("moe_meta", [P, 2, HALF, 2], U32)
        meta2 = sb("moe_meta2", [P, 2, HALF, 2], U32)
        xg = sb("moe_xg", [P, 2, HALF, D])
        xh = sb("moe_xh", [P, KD, TW], F32R)
        xl = sb("moe_xl", [P, KD, TW], F32R)
        hr = sb("moe_hr", [P, HB, TW])
        hh = sb("moe_hh", [P, HB, TW], F32R)
        hl = sb("moe_hl", [P, HB, TW], F32R)
        zero = sb("moe_zero", [(ROWS - NPAD) // 4, D])
        yb = sb("moe_yb", [P, 2, HALF, D])
        y = sb("moe_y", [P, 2, HALF, D])
        psX = ps("moe_psX", [P, KD, TW])
        psH = [ps(f"moe_psH{k}", [P, 2, TW]) for k in range(HB // 2)]
        psY = [ps(f"moe_psY{k}", [P, HALF, D]) for k in range(2)]

        w_loaded = [[sem(f"w{k}_loaded{b}") for b in range(2)] for k in range(2)]
        small_loaded = [sem(f"small_loaded{k}") for k in range(2)]
        meta_loaded = [sem(f"meta_loaded{k}") for k in range(2)]
        gathered = [sem(f"gathered{k}") for k in range(2)]
        wh_done = sem("wh_done")
        wl_done = sem("wl_done")
        wlp_done = sem("wlp_done")
        turned = sem("turned")
        xh_done, xl_done = sem("xh_done"), sem("xl_done")
        l1_done = sem("l1_done")
        relu_done = sem("relu_done")
        hh_done = sem("hh_done")
        hl_done = sem("hl_done")
        l2_done = sem("l2_done")
        yb_done = sem("yb_done")
        y_done = sem("y_done")
        copied = sem("copied")
        added = [sem(f"added{k}") for k in range(2)]
        zeroed = sem("zeroed")
        issued = sem("issued")
        passed = sem("passed")
        pairs = HB // 2
        DCH = NCH - len(POOL_CH)

        block = ctx.enter_context(nc.Block())

        def load_weights(sp, t, b, which=range(2)):
            e = sp.value_load(sched[0:1, 1, bass.ds(t, 1)] if not isinstance(t, int) else sched[0:1, 1, t:t + 1],
                              min_val=0, max_val=E - 1)
            for k in which:
                sp.dma_start(wraw[:, b, k * W1:(k + 1) * W1],
                             wall[bass.ds(e * P, P), k * W1:(k + 1) * W1]).then_inc(w_loaded[k][b], 16)

        def load_small(sp, t, b):
            e = sp.value_load(sched[0:1, 1, bass.ds(t, 1)] if not isinstance(t, int) else sched[0:1, 1, t:t + 1],
                              min_val=0, max_val=E - 1)
            sp.dma_start(b1s[:, b, :], b1[bass.ds(e * P, P), :]).then_inc(small_loaded[b], 16)
            sp.dma_start(b2s[:, b, :], b2[bass.ds(e, 1), :].broadcast_to([P, D])).then_inc(small_loaded[b], 16)

        def load_meta(sp, t, b):
            r = sp.value_load(sched[0:1, 0, bass.ds(t, 1)] if not isinstance(t, int) else sched[0:1, 0, t:t + 1],
                              min_val=0, max_val=SLOTS - TW)
            sp.dma_start(meta[:, b, :, :], table[bass.ds(r, TW), :].rearrange("(p h) c -> p h c", h=HALF)
                         ).then_inc(meta_loaded[b], 16)

        @block.sync
        def _(sp):
            for t in range(2):
                load_meta(sp, t, t)
            for t in range(2):
                load_weights(sp, t, t)
                load_small(sp, t, t)

            def ahead(t, b, weights=True, small=True, metas=True):
                o = 1 - b
                if metas:
                    sp.wait_ge(issued, t + 2)
                    wait_apart(sp, copied, t + 2, passed)
                    load_meta(sp, t + 3, o)
                if weights:
                    wait_apart(sp, wl_done, t * DCH + DCH + FIRST - 1, passed)
                    wait_apart(sp, wlp_done, t * len(POOL_CH) + len(POOL_CH) + 1, passed)
                    load_weights(sp, t + 3, o, [0])
                if small:
                    sp.wait_ge(relu_done, t * HB + 2 * HB)
                    wait_apart(sp, yb_done, t + 3, passed)
                    load_small(sp, t + 2, b)
                if weights:
                    wait_apart(sp, wl_done, t * DCH + 2 * DCH, passed)
                    wait_apart(sp, wlp_done, t * len(POOL_CH) + 2 * len(POOL_CH), passed)
                    load_weights(sp, t + 3, o, [1])

            ahead(-1, 1, small=False)
            with sp.Fori(0, (TILES - 3) // 2) as i:
                for b in range(2):
                    ahead(i * 2 + b, b)
            t = TILES - 3
            ahead(t, t % 2, weights=False)

        @block.gpsimd
        def _(pool):
            quarter = (ROWS - NPAD) // 4
            pool.memset(zero[:], 0.0).then_inc(zeroed, 1)

            def gather(t, b, use):
                wait_apart(pool, meta_loaded[b], use * 16 + 16, passed)
                for h in range(HALF):
                    pool.indirect_dma_start(xg[:, b, h, :], None, xn_rows,
                                            bass.IndirectOffsetOnAxis(ap=meta[:, b, h, 0:1], axis=0)
                                            ).then_inc(gathered[b], 16)

            def split_low(c, b):
                cols = slice(c * CHW, (c + 1) * CHW)
                return pool.tensor_tensor(wl[:, b, cols], wraw[:, b, cols], wh[:, b, cols].bitcast(F32), ALU.subtract)

            gather(0, 0, 0)
            gather(1, 1, 0)
            pool.wait_ge(zeroed, 1)
            for k in range(4):
                pool.dma_start(x_rows[NPAD + k * quarter:NPAD + (k + 1) * quarter, :], zero[:]).then_inc(added[k % 2], 16)
            pool.wait_ge(gathered[0], 32)
            pool.sem_inc(issued, 1)
            pool.wait_ge(wh_done, FIRST)
            split_low(POOL_CH[0], 0).then_inc(wlp_done, 1)

            def step(t, i, b, ahead=True):
                o = 1 - b
                pool.wait_ge(wh_done, t * NCH + NCH)
                split_low(POOL_CH[1], b).then_inc(wlp_done, 1)
                if ahead:
                    pool.wait_ge(turned, t + 1)
                    gather(t + 2, b, i + 1)
                    pool.wait_ge(gathered[o], i * 32 + (32 if b == 0 else 64))
                    pool.sem_inc(issued, 1)
                if ahead:
                    pool.wait_ge(wh_done, t * NCH + NCH + FIRST)
                    split_low(POOL_CH[0], o).then_inc(wlp_done, 1)
                wait_apart(pool, yb_done, t + 3, passed)
                wait_apart(pool, added[b], i * 32 + 32, passed)
                for h in range(HALF):
                    last = pool.tensor_scalar(y[:, b, h, :], yb[:, b, h, :], meta2[:, b, h, 1:2].bitcast(F32), 0.0,
                                              ALU.mult, ALU.add)
                last.then_inc(y_done, 1)
                pool.wait_ge(y_done, t + 3)
                wait_apart(pool, added[o], i * 32 + (32 if b == 0 else 64), passed)
                for h in range(HALF):
                    pool.indirect_dma_start(x_rows, bass.IndirectOffsetOnAxis(ap=meta2[:, b, h, 0:1], axis=0),
                                            y[:, b, h, :], None, compute_op=ALU.add).then_inc(added[b], 16)

            with pool.Fori(0, TILES // 2) as i:
                for b in range(2):
                    step(i * 2 + b, i, b)
            step(TILES - 1, TILES // 2, 0, ahead=False)
            pool.wait_ge(added[0], 32 * (TILES // 2 + 1) + 32)
            pool.wait_ge(added[1], 32 * (TILES // 2) + 32)
            pool.wait_ge(gathered[1], 32 * (TILES // 2 + 1))

        def split_high(act, c, b):
            cols = slice(c * CHW, (c + 1) * CHW)
            act.activation(wh[:, b, cols], wraw[:, b, cols], ACT.Copy).then_inc(wh_done, 1)

        @block.scalar
        def _(act):
            for c in range(NCH):
                if c % FIRST == 0:
                    act.wait_ge(w_loaded[c // FIRST][0], 16)
                split_high(act, c, 0)
                if c == FIRST - 1:
                    act.wait_ge(turned, 1)
                    act.activation(xh[:], psX[:], ACT.Copy).then_inc(xh_done, 1)

            def step(t, i, b, ahead=True):
                o = 1 - b
                for hb in range(HB):
                    if hb == 0:
                        act.wait_ge(small_loaded[b], i * 32 + 32)
                    act.wait_ge(l1_done, t * HB + hb // 2 * 2 + 2)
                    act.wait_ge(hl_done, t * pairs + hb // 2 + 1)
                    act.activation(hr[:, hb, :], psH[hb // 2][:, hb % 2, :], ACT.Relu,
                                   bias=b1s[:, b, hb:hb + 1]).then_inc(relu_done, 1)
                    if ahead and hb % 2 == 1:
                        if hb == 1:
                            act.wait_ge(w_loaded[0][o], i * 16 + (16 if b == 0 else 32))
                            act.wait_ge(l2_done, t + 1)
                        split_high(act, hb // 2, o)
                if ahead:
                    act.wait_ge(turned, t + 2)
                    act.wait_ge(l1_done, t * HB + HB)
                    act.activation(xh[:], psX[:], ACT.Copy).then_inc(xh_done, 1)
                    act.wait_ge(w_loaded[1][o], i * 16 + (16 if b == 0 else 32))
                    for c in range(FIRST, NCH):
                        split_high(act, c, o)

            with act.Fori(0, TILES // 2) as i:
                for b in range(2):
                    step(i * 2 + b, i, b)
            step(TILES - 1, TILES // 2, 0, ahead=False)

        @block.vector
        def _(dve):
            dve.sem_inc(hl_done, pairs)
            dve.sem_inc(yb_done, 2)
            dve.sem_inc(relu_done, HB)
            dve.sem_inc(y_done, 2)

            def split_low(c, b):
                cols = slice(c * CHW, (c + 1) * CHW)
                dve.tensor_tensor(wl[:, b, cols], wraw[:, b, cols], wh[:, b, cols].bitcast(F32),
                                  ALU.subtract).then_inc(wl_done, 1)

            for c in range(FIRST):
                if c not in POOL_CH:
                    dve.wait_ge(wh_done, c + 1)
                    split_low(c, 0)
            dve.wait_ge(xh_done, 1)
            dve.tensor_tensor(xl[:], psX[:], xh[:].bitcast(F32), ALU.subtract).then_inc(xl_done, 1)
            dve.wait_ge(meta_loaded[0], 16)
            dve.tensor_copy(meta2[:, 0], meta[:, 0]).then_inc(copied, 1)

            def step(t, i, b, ahead=True):
                o = 1 - b
                for c in range(FIRST, NCH):
                    if c not in POOL_CH:
                        dve.wait_ge(wh_done, t * NCH + c + 1)
                        split_low(c, b)
                for k in range(pairs):
                    blocks = slice(2 * k, 2 * k + 2)
                    dve.wait_ge(relu_done, t * HB + 2 * k + 2 + HB)
                    if k == 0:
                        dve.wait_ge(l2_done, t + 1)
                    dve.tensor_copy(hh[:, blocks, :], hr[:, blocks, :]).then_inc(hh_done, 1)
                    dve.wait_ge(hh_done, t * pairs + k + 1)
                    dve.tensor_tensor(hl[:, blocks, :], hr[:, blocks, :], hh[:, blocks, :].bitcast(F32),
                                      ALU.subtract).then_inc(hl_done, 1)
                    if ahead and k not in POOL_CH:
                        dve.wait_ge(wh_done, t * NCH + NCH + k + 1)
                        split_low(k, o)
                if ahead:
                    dve.wait_ge(xh_done, t + 2)
                    dve.tensor_tensor(xl[:], psX[:], xh[:].bitcast(F32), ALU.subtract).then_inc(xl_done, 1)
                    dve.wait_ge(meta_loaded[o], i * 16 + (16 if b == 0 else 32))
                    dve.wait_ge(added[o], i * 32 + (32 if b == 0 else 64))
                    dve.tensor_copy(meta2[:, o], meta[:, o]).then_inc(copied, 1)
                dve.wait_ge(l2_done, t + 2)
                dve.wait_ge(small_loaded[b], i * 32 + 32)
                dve.wait_ge(y_done, t + 1)
                dve.tensor_tensor(yb[:, b], psY[b][:], b2s[:, b, :].unsqueeze(1).broadcast_to([P, HALF, D]),
                                  ALU.add).then_inc(yb_done, 1)

            with dve.Fori(0, TILES // 2) as i:
                for b in range(2):
                    step(i * 2 + b, i, b)
            step(TILES - 1, TILES // 2, 0, ahead=False)

        @block.tensor
        def _(pe):
            pe.sem_inc(l2_done, 1)

            def turn(b):
                for h in range(HALF):
                    for k in range(KD):
                        last = pe.transpose(psX[:, k, h * P:(h + 1) * P], xg[:, b, h, k * P:(k + 1) * P], g.ident[:])
                last.then_inc(turned, 1)

            pe.wait_ge(gathered[0], 32)
            turn(0)

            def step(t, i, b, ahead=True):
                o = 1 - b
                pe.wait_ge(xl_done, t + 1)
                pe.wait_ge(wl_done, t * DCH + FIRST - 1)
                pe.wait_ge(wlp_done, t * len(POOL_CH) + 1)
                for hb in range(HB):
                    if hb % 2 == 0:
                        pe.wait_ge(relu_done, t * HB + hb + 2)
                    n = 0
                    for k in range(KD):
                        cols = slice(k * H + hb * P, k * H + (hb + 1) * P)
                        for w, x in ((wh, xh), (wh, xl), (wl, xh)):
                            last = pe.matmul(psH[hb // 2][:, hb % 2, :], w[:, b, cols], x[:, k, :],
                                             start=(n == 0), stop=(n == 3 * KD - 1))
                            n += 1
                    last.then_inc(l1_done, 1)
                if ahead:
                    pe.wait_ge(gathered[o], i * 32 + (32 if b == 0 else 64))
                    turn(o)
                pe.wait_ge(yb_done, t + 1)
                pe.wait_ge(wl_done, t * DCH + DCH)
                pe.wait_ge(wlp_done, t * len(POOL_CH) + 2)
                for hb in range(HB):
                    if hb % 2 == 0:
                        pe.wait_ge(hl_done, t * pairs + hb // 2 + 1 + pairs)
                    for h in range(HALF):
                        rows = slice(h * P, (h + 1) * P)
                        w2 = slice(W1 + hb * D, W1 + (hb + 1) * D)
                        for m, (hx, w) in enumerate(((hh, wh), (hh, wl), (hl, wh))):
                            last = pe.matmul(psY[b][:, h, :], hx[:, hb, rows], w[:, b, w2],
                                             start=(hb == 0 and h == 0 and m == 0), stop=(hb == HB - 1 and m == 2),
                                             skip_group_check=True)
                last.then_inc(l2_done, 1)

            with pe.Fori(0, TILES // 2) as i:
                for b in range(2):
                    step(i * 2 + b, i, b)
            step(TILES - 1, TILES // 2, 0, ahead=False)


def standardise_block(nc, g, x_rows, w1, b1, z, scale):
    with ExitStack() as ctx:
        sb, ps = tensors(nc, ctx)
        sem = semaphores(nc, ctx, "std")
        Q = 2
        G = NT // Q
        LOADS = ((0, 6), (6, 14), (14, 20), (20, NT))
        B = 3
        w = sb("std_w", [P, KD, D])
        b = sb("std_b", [P, D])
        stats = sb("std_stats", [P, NT, 6])
        mv = sb("std_mv", [P, NT, 2])
        veps = sb("std_veps", [P, NT])
        rstd = sb("std_rstd", [P, NT])
        shift = sb("std_shift", [P, NT])
        negshift = sb("std_negshift", [P, NT])
        xn = sb("std_xn", [P, B, Q, D])
        xnT = sb("std_xnT", [P, B, Q, KD, P])
        total = sb("std_total", [P, Q, D])
        sq = sb("std_sq", [P, B, Q, D])
        mean = sb("std_mean", [P, D])
        squares = sb("std_squares", [1, D])
        var = sb("std_var", [P, KD])
        half = sb("std_half", [P, KD])
        std = sb("std_std", [P, KD])
        stde = sb("std_stde", [P, KD])
        rinv = sb("std_rinv", [P, KD])
        diag = sb("std_diag", [P, KD, P])
        psT = [ps(f"std_psT{k}", [P, Q, KD, P]) for k in range(B)]
        psZ = [ps(f"std_psZ{k}", [P, Q, D]) for k in range(B)]
        psM = ps("std_psM", [P, D])
        psV = ps("std_psV", [P, KD])

        x_loaded = [sem(f"x_loaded{k}") for k in range(len(LOADS))]
        w_loaded = sem("w_loaded")
        st_done, aggr_done, eps_done = sem("stats"), sem("aggr"), sem("eps")
        rstd_done, shift_done, norm_done = sem("rstd"), sem("shift"), sem("norm")
        xn_done, tr_done, xnT_done, mm_done, z_done, total_done = (
            sem(n) for n in ("xn", "tr", "xnT", "mm", "z", "total"))
        zc_done, sq_done, var_mm, squares_done = sem("zc"), sem("sq"), sem("varmm"), sem("squares")
        sum_done, mean_done, var_done, root_done, dchain, diag_done, bc_done = (
            sem(n) for n in ("sum", "mean", "var", "root", "dchain", "diag", "bc"))
        block = ctx.enter_context(nc.Block())

        def load_of(k):
            return next(i for i, (first, end) in enumerate(LOADS) if first <= k * Q < end)

        def group(k):
            return slice(k * Q, (k + 1) * Q)

        @block.sync
        def _(sp):
            rows = x_rows[0:NPAD, :].rearrange("(t p) d -> p t d", p=P)
            for k, (first, end) in enumerate(LOADS):
                sp.dma_start(g.x[:, first:end, :], rows[:, first:end, :]).then_inc(x_loaded[k], 16)
                if k == 0:
                    sp.dma_start(w[:], w1.rearrange("(k p) n -> p k n", p=P)).then_inc(w_loaded, 16)
                    sp.dma_start(b[:], b1.broadcast_to([P, D])).then_inc(w_loaded, 16)

        @block.vector
        def _(dve):
            def statistics(k):
                first, end = LOADS[k]
                dve.wait_ge(x_loaded[k], 16)
                for t in range(first, end):
                    last = dve.bn_stats(stats[:, t, :], g.x[:, t, :])
                last.then_inc(st_done, 1)
                dve.wait_ge(st_done, k + 1)
                for t in range(first, end):
                    last = dve.bn_aggr(mv[:, t, :], stats[:, t, :])
                last.then_inc(aggr_done, 1)
                dve.wait_ge(aggr_done, k + 1)
                dve.tensor_scalar(veps[:, first:end], mv[:, first:end, 1], LN_EPS, None, ALU.add).then_inc(eps_done, 1)

            statistics(0)
            statistics(1)
            dve.wait_ge(w_loaded, 32)
            for k in range(G):
                dve.wait_ge(mm_done, k + 1)
                dve.tensor_tensor(z[:, group(k), :], psZ[k % B][:], b[:].unsqueeze(1).broadcast_to([P, Q, D]),
                                  ALU.add).then_inc(z_done, 1)
                if k in (0, 2):
                    statistics(2 + k // 2)
            dve.memset(half[:], 0.5)
            dve.wait_ge(sum_done, 1)
            dve.tensor_scalar(mean[:], psM[:], 1.0 / N, None, ALU.mult).then_inc(mean_done, 1)
            dve.wait_ge(mean_done, 1)
            for k in range(G):
                dve.tensor_tensor(z[:, group(k), :], z[:, group(k), :], mean[:].unsqueeze(1).broadcast_to([P, Q, D]),
                                  ALU.subtract).then_inc(zc_done, 1)
            dve.wait_ge(var_mm, G)
            dve.tensor_copy(squares[:], psM[0:1, :]).then_inc(squares_done, 1)
            dve.wait_ge(var_mm, G + 1)
            dve.tensor_scalar(var[:], psV[:], 1.0 / (N - 1), None, ALU.mult).then_inc(var_done, 1)
            chain = Chain(dve, dchain)
            dve.wait_ge(root_done, 1)
            chain(dve.tensor_scalar(stde[:], std[:], 1e-6, None, ALU.add))
            chain(dve.reciprocal(rinv[:], stde[:]))
            for k in range(KD):
                last = dve.tensor_scalar(diag[:, k, :], g.ident[:], rinv[:, k:k + 1], None, ALU.mult)
            last.then_inc(diag_done, 1)
            dve.wait_ge(bc_done, 1)
            dve.tensor_copy(scale[:], psM[:])

        @block.gpsimd
        def _(pool):
            def scale_and_shift(k):
                first, end = LOADS[k]
                part = slice(first, end)
                pool.wait_ge(eps_done, k + 1)
                pool.tensor_tensor(rstd[:, part], veps[:, part], g.mhalf[:, part], ALU.pow).then_inc(rstd_done, 1)
                pool.wait_ge(rstd_done, k + 1)
                pool.tensor_tensor(shift[:, part], mv[:, part, 0], rstd[:, part], ALU.mult).then_inc(shift_done, 1)
                pool.wait_ge(shift_done, k + 1)
                pool.tensor_scalar(negshift[:, part], shift[:, part], -1.0, 0.0, ALU.mult, ALU.add).then_inc(norm_done, 1)

            for k in range(len(LOADS)):
                scale_and_shift(k)
            for k in range(1, G - 1):
                pool.wait_ge(z_done, k + 1)
                if k >= 2:
                    pool.wait_ge(total_done, k - 1)
                pool.tensor_tensor(total[:], z[:, group(0), :] if k == 1 else total[:], z[:, group(k), :],
                                   ALU.add).then_inc(total_done, 1)
            pool.wait_ge(var_done, 1)
            pool.tensor_tensor(std[:], var[:], half[:], ALU.pow).then_inc(root_done, 1)

        @block.scalar
        def _(act):
            for k in range(G + 1):
                if k < G:
                    if k == 0 or load_of(k) != load_of(k - 1):
                        act.wait_ge(norm_done, load_of(k) + 1)
                    if k >= B:
                        act.wait_ge(tr_done, k - B + 1)
                    for q in range(Q):
                        t = k * Q + q
                        last = act.activation(xn[:, k % B, q, :], g.x[:, t, :], ACT.Identity, bias=negshift[:, t:t + 1],
                                              scale=rstd[:, t:t + 1])
                    last.then_inc(xn_done, 1)
                if k >= 1:
                    act.wait_ge(tr_done, k)
                    if k > B:
                        act.wait_ge(mm_done, k - B)
                    act.activation(xnT[:, (k - 1) % B], psT[(k - 1) % B][:], ACT.Copy).then_inc(xnT_done, 1)
            for k in range(G):
                act.wait_ge(zc_done, k + 1)
                if k >= B:
                    act.wait_ge(var_mm, k - B + 1)
                act.activation(sq[:, k % B], z[:, group(k), :], ACT.Square).then_inc(sq_done, 1)

        @block.tensor
        def _(pe):
            pe.wait_ge(w_loaded, 32)
            AHEAD = 2
            for n in range(G + AHEAD):
                if n < G:
                    pe.wait_ge(xn_done, n + 1)
                    if n >= B:
                        pe.wait_ge(xnT_done, n - B + 1)
                    for q in range(Q):
                        for d in range(KD):
                            last = pe.transpose(psT[n % B][:, q, d, :], xn[:, n % B, q, d * P:(d + 1) * P], g.ident[:])
                    last.then_inc(tr_done, 1)
                k = n - AHEAD
                if k >= 0:
                    pe.wait_ge(xnT_done, k + 1)
                    if k >= B:
                        pe.wait_ge(z_done, k - B + 1)
                    for q in range(Q):
                        for d in range(KD):
                            last = pe.matmul(psZ[k % B][:, q, :], xnT[:, k % B, q, d, :], w[:, d, :], start=(d == 0),
                                             stop=(d == KD - 1))
                    last.then_inc(mm_done, 1)
            pe.wait_ge(z_done, G)
            for q in range(Q):
                pe.matmul(psM[:], (g.ones if q < Q - 1 else g.valid)[:], z[:, (G - 1) * Q + q, :], start=(q == 0),
                          stop=False)
            pe.wait_ge(total_done, G - 2)
            for q in range(Q):
                last = pe.matmul(psM[:], g.ones[:], total[:, q, :], start=False, stop=(q == Q - 1))
            last.then_inc(sum_done, 1)
            for k in range(G):
                pe.wait_ge(sq_done, k + 1)
                for q in range(Q):
                    t = k * Q + q
                    last = pe.matmul(psM[:], (g.valid if t == NT - 1 else g.ones)[:], sq[:, k % B, q, :],
                                     start=(t == 0), stop=(t == NT - 1))
                last.then_inc(var_mm, 1)
            pe.wait_ge(squares_done, 1)
            for d in range(KD):
                last = pe.matmul(psV[:, d:d + 1], squares[0:1, d * P:(d + 1) * P], g.ones[0:1, 0:1], start=True, stop=True)
            last.then_inc(var_mm, 1)
            pe.wait_ge(diag_done, 1)
            for k in range(KD):
                last = pe.matmul(psM[:, k * P:(k + 1) * P], g.ones[:], diag[:, k, :], start=True, stop=True)
            last.then_inc(bc_done, 1)


def steps_block(nc, g, wt_in, lw_in, lb_in, b_in, h0, out):
    with ExitStack() as ctx:
        sb, ps = tensors(nc, ctx)
        sem = semaphores(nc, ctx, "ffn")
        Q = 2
        G = NT // Q
        W = Q * D
        BODY = 4
        R = 4
        FOUR_PASS = (1, 4, 7, 10)
        BY_ACT = (1, 2, 4, 5, 7, 8, 10, 11)
        wt = sb("ffn_wt", [P, KD, D])
        lw = sb("ffn_lw", [P, KD])
        lb = sb("ffn_lb", [P, KD])
        bias = sb("ffn_bias", [1, D])
        wlw = sb("ffn_wlw", [P, KD, D])
        lbm = sb("ffn_lbm", [P, KD, P])
        w2 = sb("ffn_w2", [P, KD, D])
        w2h = sb("ffn_w2h", [P, KD, D], F32R)
        w2l = sb("ffn_w2l", [P, KD, D], F32R)
        vT = sb("ffn_vT", [P, R, Q * KD, P])
        vTh = sb("ffn_vTh", [P, R, Q * KD, P], F32R)
        vTl = sb("ffn_vTl", [P, R, Q * KD, P], F32R)
        th = sb("ffn_th", [P, R, W])
        u = sb("ffn_u", [P, R, W])
        stats = sb("ffn_stats", [P, NT, 6])
        mv = sb("ffn_mv", [P, NT, 2])
        veps = sb("ffn_veps", [P, NT])
        rstd = sb("ffn_rstd", [P, NT])
        mr = sb("ffn_mr", [P, NT])
        shift = sb("ffn_shift", [P, NT])
        vn = sb("ffn_vn", [P, NT, D])
        warm = sb("ffn_warm", [P, 1])
        psT = [ps(f"ffn_psT{k}", [P, Q * KD, P]) for k in range(R)]
        psH = [ps(f"ffn_psH{k}", [P, W]) for k in range(R)]
        psW = psT[0][:, 0:Q, :]

        loaded, wprep, delta_done, w_ready = sem("loaded"), sem("wprep"), sem("delta"), sem("w_ready")
        wlw_done = sem("wlw")
        turned, copied, lo_done = sem("turned"), sem("copied"), sem("lo")
        mm_done, th_done, u_done, v_done = sem("mm"), sem("th"), sem("u"), sem("v")
        st_done, aggr_done, eps_done, rstd_done = sem("stats"), sem("aggr"), sem("eps"), sem("rstd")
        mr_done, shift_done, vn_done = sem("mr"), sem("shift"), sem("vn")
        vn2_done = sem("vn2")
        summed, stored = sem("summed"), sem("stored")
        passed = sem("passed")
        ALL = STEPS * G
        END = (STEPS + 1) * G
        LOW, MM, TANH, U, SILU, STATS, SHIFT, NORM = 1, 3, 4, 4, 5, 6, 7, 9

        block = ctx.enter_context(nc.Block())

        def run(eng, slot):
            for n in range(2 * G):
                slot(n, n, 0)
            with eng.Fori(0, (STEPS - 2) // BODY) as i:
                for k in range(BODY * G):
                    slot(i * (BODY * G) + (2 * G + k), 2 * G + k, i)
            for n in range(STEPS * G, END + NORM):
                slot(n, n, 0)

        def tiles(m):
            return slice(m % G * Q, m % G * Q + Q)

        def chained(m, lag):
            return 0 <= m - lag < ALL

        def split(m):
            return m % G not in FOUR_PASS

        def lows(rounds, m):
            return rounds * (BODY * (G - len(FOUR_PASS))) + len([k for k in range(G, m + 1) if split(k)])

        def by_act(rounds, m):
            return rounds * (BODY * len(BY_ACT)) + len([k for k in range(m + 1) if k % G in BY_ACT])

        @block.sync
        def _(sp):
            sp.dma_start(wt[:], wt_in.rearrange("(k p) n -> p k n", p=P)).then_inc(loaded, 16)
            sp.dma_start(lw[:], lw_in).then_inc(loaded, 16)
            sp.dma_start(lb[:], lb_in).then_inc(loaded, 16)
            sp.dma_start(bias[:], b_in).then_inc(loaded, 16)
            for k in range(G):
                sp.wait_ge(summed, k + 1)
                rows = out[k * Q * P:(k + 1) * Q * P, :] if k < G - 1 else out[k * Q * P:k * Q * P + P, :]
                n = Q if k < G - 1 else 1
                sp.dma_start(rows.rearrange("(q p) d -> p q d", p=P), vn[:, k * Q:k * Q + n, :]).then_inc(stored, 16)
            sp.dma_start(out[(NT - 1) * P:N, :], vn[0:LAST, NT - 1, :]).then_inc(stored, 16)
            sp.wait_ge(stored, (G + 1) * 16)

        @block.tensor
        def _(pe):
            delta = psW.rearrange("p q n -> p (q n)")
            pe.wait_ge(wprep, 2)
            for k in range(KD):
                pe.matmul(delta, lbm[:, k, :], wt[:, k, :], start=(k == 0), stop=False)
            for k in range(KD):
                pe.matmul(delta, g.negones[:], wlw[:, k, :], start=False, stop=False)
            pe.matmul(delta, g.ones[0:1, :], bias[0:1, :], start=False, stop=True).then_inc(delta_done, 1)
            pe.wait_ge(w_ready, 3 * KD)

            def slot(n, m, rounds):
                if m < G:
                    if m >= R:
                        pe.wait_ge(u_done, n - R + 1)
                    for q in range(Q):
                        last = pe.matmul(psH[m % R][:, q * D:(q + 1) * D], g.ident[:], h0[:, m * Q + q, :],
                                         start=True, stop=True)
                    last.then_inc(mm_done, 1)
                    return
                if m < END:
                    gr = m % G
                    pe.wait_ge(vn_done, n - G + 1)
                    if gr in BY_ACT:
                        pe.wait_ge(vn2_done, by_act(rounds, m - G))
                    if m - R >= G:
                        pe.wait_ge(copied, n - R - G + 1)
                        if split(m - R):
                            pe.wait_ge(lo_done, lows(rounds, m - R))
                    for q in range(Q):
                        for k in range(KD):
                            last = pe.transpose(psT[m % R][:, q * KD + k, :], vn[:, gr * Q + q, k * P:(k + 1) * P],
                                                g.ident[:])
                    last.then_inc(turned, 1)
                if G <= m - MM < END:
                    w = m - MM
                    if w - R < ALL:
                        pe.wait_ge(u_done, n - MM - R + 1)
                    else:
                        pe.wait_ge(summed, n - MM - R - ALL + 1)
                    if split(w):
                        pe.wait_ge(lo_done, lows(rounds, w))
                        pairs = ((vTh, w2h), (vTh, w2l), (vTl, w2h))
                    else:
                        pe.wait_ge(copied, n - MM - G + 1)
                        pairs = ((vT, w2),)
                    for q in range(Q):
                        for k in range(KD):
                            for j, (a, b) in enumerate(pairs):
                                last = pe.matmul(psH[w % R][:, q * D:(q + 1) * D], a[:, w % R, q * KD + k, :], b[:, k, :],
                                                 start=(k == 0 and j == 0), stop=(k == KD - 1 and j == len(pairs) - 1))
                    last.then_inc(mm_done, 1)

            run(pe, slot)

        @block.scalar
        def _(act):
            act.wait_ge(w_ready, KD)
            for k in range(KD):
                act.activation(w2h[:, k, :], w2[:, k, :], ACT.Copy).then_inc(w_ready, 1)
            act.activation(warm[:], w2[:, 0, 0:1], ACT.Silu)

            def slot(n, m, rounds):
                if G <= m < END:
                    act.wait_ge(turned, n - G + 1)
                    if m - R >= 0:
                        act.wait_ge(mm_done, n - R + 1)
                    to = vTh if split(m) else vT
                    act.activation(to[:, m % R], psT[m % R][:], ACT.Copy).then_inc(copied, 1)
                if chained(m, TANH):
                    a = (m - TANH) % R
                    act.wait_ge(mm_done, n - TANH + 1)
                    if m - TANH >= R:
                        act.wait_ge(u_done, n - TANH - R + 1)
                    act.activation(th[:, a], psH[a][:], ACT.Tanh).then_inc(th_done, 1)
                if chained(m, SILU):
                    act.wait_ge(u_done, n - SILU + 1)
                    act.activation(vn[:, tiles(m - SILU)].rearrange("p q d -> p (q d)"), u[:, (m - SILU) % R],
                                   ACT.Silu).then_inc(v_done, 1)
                if chained(m, NORM) and (m - NORM) % G in BY_ACT:
                    t = (m - NORM) % G * Q + 1
                    act.wait_ge(shift_done, n - NORM + 1)
                    act.activation(vn[:, t, :], vn[:, t, :], ACT.Identity, scale=rstd[:, t:t + 1],
                                   bias=shift[:, t:t + 1]).then_inc(vn2_done, 1)

            run(act, slot)

        @block.vector
        def _(dve):
            dve.wait_ge(loaded, 64)
            for k in range(KD):
                dve.tensor_scalar(wlw[:, k, :], wt[:, k, :], lw[:, k:k + 1], None, ALU.mult).then_inc(wlw_done, 1)
                last = dve.tensor_scalar(lbm[:, k, :], g.ones[:], lb[:, k:k + 1], None, ALU.mult)
            last.then_inc(wprep, 2)
            dve.wait_ge(wlw_done, KD)
            dve.wait_ge(delta_done, 1)
            for k in range(KD):
                dve.scalar_tensor_tensor(out=w2[:, k, :], in0=psW.rearrange("p q n -> p (q n)"), scalar=1.0 / D,
                                         in1=wlw[:, k, :], op0=ALU.mult, op1=ALU.add).then_inc(w_ready, 1)
            dve.wait_ge(w_ready, 2 * KD)
            for k in range(KD):
                dve.tensor_tensor(w2l[:, k, :], w2[:, k, :], w2h[:, k, :].bitcast(F32), ALU.subtract).then_inc(w_ready, 1)

            def slot(n, m, rounds):
                if chained(m, STATS):
                    dve.wait_ge(v_done, n - STATS + 1)
                    for q in range(Q):
                        t = (m - STATS) % G * Q + q
                        last = dve.bn_stats(stats[:, t, :], vn[:, t, :])
                    last.then_inc(st_done, 1)
                if G <= m - LOW < END and split(m - LOW):
                    w = m - LOW
                    dve.wait_ge(copied, n - LOW - G + 1)
                    dve.tensor_tensor(vTl[:, w % R], psT[w % R][:], vTh[:, w % R].bitcast(F32),
                                      ALU.subtract).then_inc(lo_done, 1)
                if chained(m, U):
                    a = (m - U) % R
                    dve.wait_ge(th_done, n - U + 1)
                    if m - U >= R:
                        dve.wait_ge(v_done, n - U - R + 1)
                    dve.scalar_tensor_tensor(out=u[:, a], in0=th[:, a], scalar=0.01, in1=psH[a][:],
                                             op0=ALU.mult, op1=ALU.add).then_inc(u_done, 1)
                if chained(m, STATS):
                    wait_apart(dve, st_done, n - STATS + 1, passed)
                    for q in range(Q):
                        t = (m - STATS) % G * Q + q
                        last = dve.bn_aggr(mv[:, t, :], stats[:, t, :])
                    last.then_inc(aggr_done, 1)
                if ALL <= m - U < END:
                    dve.wait_ge(mm_done, n - U + 1)
                    dve.tensor_tensor(vn[:, tiles(m - U), :], g.x[:, tiles(m - U), :],
                                      psH[(m - U) % R][:].rearrange("p (q d) -> p q d", q=Q),
                                      ALU.add).then_inc(summed, 1)

            run(dve, slot)

        @block.gpsimd
        def _(pool):
            def slot(n, m, rounds):
                if chained(m, STATS):
                    q = tiles(m - STATS)
                    wait_apart(pool, aggr_done, n - STATS + 1, passed)
                    pool.tensor_scalar(veps[:, q], mv[:, q, 1], 1.0, LN_EPS, ALU.mult, ALU.add).then_inc(eps_done, 1)
                if chained(m, SHIFT):
                    q = tiles(m - SHIFT)
                    pool.wait_ge(rstd_done, n - SHIFT + 1)
                    pool.tensor_tensor(mr[:, q], mv[:, q, 0], rstd[:, q], ALU.mult).then_inc(mr_done, 1)
                if chained(m, NORM):
                    wait_apart(pool, shift_done, n - NORM + 1, passed)
                    for q in range(1 if (m - NORM) % G in BY_ACT else Q):
                        t = (m - NORM) % G * Q + q
                        last = pool.tensor_scalar(vn[:, t, :], vn[:, t, :], rstd[:, t:t + 1], shift[:, t:t + 1],
                                                  ALU.mult, ALU.add)
                    last.then_inc(vn_done, 1)
                if chained(m, STATS):
                    q = tiles(m - STATS)
                    pool.wait_ge(eps_done, n - STATS + 1)
                    pool.tensor_tensor(rstd[:, q], veps[:, q], g.mhalf[:, 0:Q], ALU.pow).then_inc(rstd_done, 1)
                if chained(m, SHIFT):
                    q = tiles(m - SHIFT)
                    wait_apart(pool, mr_done, n - SHIFT + 1, passed)
                    pool.tensor_scalar(shift[:, q], mr[:, q], -1.0, 1.0, ALU.mult, ALU.add).then_inc(shift_done, 1)

            run(pool, slot)


def two_layer_graph_network(nc, x, adjt, adjl, w0, wg, bg, wall, eb1, eb2, w1, b1, ffw, lw, lb, fb, out):
    xn_rows = nc.dram_tensor("xn_rows", (ROWS, D), F32, kind="Internal").ap()
    x_rows = nc.dram_tensor("x_rows", (ROWS, D), F32, kind="Internal").ap()
    table = nc.dram_tensor("slot_table", (SLOTS, 2), U32, kind="Internal").ap()
    with ExitStack() as ctx:
        sb, _ = tensors(nc, ctx)
        g = Shared(sb)
        sched = sb("sched", [1, 2, TILES + 1], I32)
        constants_block(nc, g)
        with ExitStack() as layer0:
            sb0, _ = tensors(nc, layer0)
            s_row = sb0("l0_s", [P, NT, D])
            route = Routing(sb0, wg, bg, xn_rows, x_rows, table, sched)
            support_block(nc, g, x, w0, adjt, adjl, s_row, route)
            graph_block(nc, g, "g0", adjt, adjl, s_row, g.dinv0, None, True, None, route)
        experts_block(nc, g, wall, eb1, eb2, xn_rows, x_rows, table, sched)
        with ExitStack() as layer1:
            sb1, _ = tensors(nc, layer1)
            s_row = sb1("l1_s", [P, NT, D])
            h0 = sb1("l1_h0", [P, NT, D])
            column_scale = sb1("l1_column_scale", [P, D])
            standardise_block(nc, g, x_rows, w1, b1, s_row, column_scale)
            graph_block(nc, g, "g1", adjt, adjl, s_row, g.dinv1, column_scale, False, h0)
            steps_block(nc, g, ffw, lw, lb, fb, h0, out)


def kernel(x, adj, L0_gnn_W, L0_ffn_Wg, L0_ffn_bg, L0_ffn_W1, L0_ffn_b1, L0_ffn_W2, L0_ffn_b2, L1_gnn_W, L1_gnn_b,
           L1_ffn_ln_w, L1_ffn_ln_b, L1_ffn_W, L1_ffn_b):
    import numpy as np
    from concourse import bacc
    from concourse.bass_utils import run_bass_kernel_spmd

    f = lambda a: np.asarray(a)
    c = np.ascontiguousarray
    xp = np.zeros((NPAD, D), np.float32)
    xp[:N] = f(x)
    at = np.zeros((NPAD, NPAD), np.float32)
    at[:N, :N] = f(adj).T
    whole = PANELS * PANEL
    al = at[:, whole:].reshape(CHUNKS, CT, P, LPANEL).transpose(0, 2, 1, 3).reshape(CHUNKS * P, LCW)
    at = at[:, :whole].reshape(CHUNKS, CT, P, PANELS, PANEL).transpose(3, 0, 2, 1, 4).reshape(PANELS * CHUNKS * P, CW)
    w1 = f(L0_ffn_W1).transpose(0, 2, 1).reshape(E, KD, P, H).transpose(0, 2, 1, 3).reshape(E * P, KD * H)
    w2 = f(L0_ffn_W2).transpose(0, 2, 1).reshape(E, HB, P, D).transpose(0, 2, 1, 3).reshape(E * P, HB * D)
    arrays = {
        "x": xp, "adjt": c(at), "adjl": c(al), "w0": c(f(L0_gnn_W).T), "wg": c(f(L0_ffn_Wg).T), "bg": c(f(L0_ffn_bg).reshape(1, E)),
        "wall": c(np.concatenate([w1, w2], 1)),
        "eb1": c(f(L0_ffn_b1).reshape(E, HB, P).transpose(0, 2, 1).reshape(E * P, HB)), "eb2": c(f(L0_ffn_b2)),
        "w1": c(f(L1_gnn_W).T), "b1": c(f(L1_gnn_b).reshape(1, D)), "ffw": c(f(L1_ffn_W).T),
        "lw": c(f(L1_ffn_ln_w).reshape(KD, P).T), "lb": c(f(L1_ffn_ln_b).reshape(KD, P).T),
        "fb": c(f(L1_ffn_b).reshape(1, D)),
    }
    nc = bacc.Bacc("TRN2", target_bir_lowering=False, num_devices=1)
    aps = {k: nc.dram_tensor(f"in_{k}", a.shape, mybir.dt.from_np(a.dtype), kind="ExternalInput").ap()
           for k, a in arrays.items()}
    out = nc.dram_tensor("out", (N, D), F32, kind="ExternalOutput").ap()
    two_layer_graph_network(nc, **aps, out=out)
    r = run_bass_kernel_spmd(nc, [{f"in_{k}": a for k, a in arrays.items()}], core_ids=[0])
    return r.results[0]["out"]
```
